# Optimizing a Trainium2 kernel written in Bass

```python
import numpy as np
import jax
import jax.numpy as jnp

def _softmax(x, axis=-1):
    return jax.nn.softmax(x, axis=axis)

def _gelu(x):
    return jax.nn.gelu(x, approximate=True)

def _silu(x):
    return jax.nn.silu(x)

def _sigmoid(x):
    return jax.nn.sigmoid(x)

def _layernorm(x, axis=-1, eps=1e-05):
    m = jnp.mean(x, axis=axis, keepdims=True)
    v = jnp.var(x, axis=axis, keepdims=True)
    return (x - m) / jnp.sqrt(v + eps)

def _scatter_add(tgt, idx, src, axis=0):
    return tgt.at[idx].add(src)

def _segment_sum(src, seg, n):
    return jax.ops.segment_sum(src, seg, n)
kernel_name = 'mk_adaln_d1_jaxref_r8_ce74eb'

def setup_inputs(seed: int=0):
    np.random.seed(seed)
    _w = jnp.asarray

    def _L0_attn_setup():
        import jax, jax.numpy as jnp
        import numpy as np
        D_MODEL = 256
        H = 16
        HKV = 4
        DS = 32
        DG = 32
        DV = 64
        B, T = (2, 512)
        MB = 64
        LW = 128
        ROPE_BASE = 10000.0
        NEG_INF = -1000000000.0

        def _rope(x, pos, base):
            d = x.shape[-1]
            inv_freq = 1.0 / base ** (jnp.arange(0, d, 2, dtype=jnp.float32) / d)
            ang = pos.astype(jnp.float32)[:, None] * inv_freq
            cos, sin = (jnp.cos(ang), jnp.sin(ang))
            x1, x2 = jnp.split(x, 2, axis=-1)
            return jnp.concatenate([x1 * cos - x2 * sin, x2 * cos + x1 * sin], axis=-1)
        key = jax.random.key(seed)
        ks = jax.random.split(key, 8)
        w = lambda k, sh: jax.random.normal(k, sh, jnp.float32) * 0.02
        return {'x': jax.random.normal(ks[0], (B, T, D_MODEL), jnp.float32), 'Wq_sem': w(ks[1], (D_MODEL, H * DS)), 'Wk_sem': w(ks[2], (D_MODEL, HKV * DS)), 'Wq_geo': w(ks[3], (D_MODEL, H * DG)), 'Wk_geo': w(ks[4], (D_MODEL, HKV * DG)), 'Wv': w(ks[5], (D_MODEL, HKV * DV)), 'Wo': w(ks[6], (H * DV, D_MODEL)), 'logit_scale': jnp.zeros((H,), jnp.float32)}
    _L0_attn_in = _L0_attn_setup()

    def _L0_ffn_setup():
        import jax, jax.numpy as jnp
        import numpy as np
        H = 256
        I = 128
        K = 8
        E = 128
        TOPK = 4
        EPS = 1e-08
        key = jax.random.key(seed)
        ks = jax.random.split(key, 10)
        s = 0.02
        return {'x': jax.random.normal(ks[0], (4, 256, H), jnp.float32), 'w_router': jax.random.normal(ks[1], (H, E), jnp.float32) * s, 'w_gate': jax.random.normal(ks[2], (H, K * I), jnp.float32) * s, 'w_up': jax.random.normal(ks[3], (H, K * I), jnp.float32) * s, 'w_down': jax.random.normal(ks[4], (I, H), jnp.float32) * s, 'amplitudes': jax.random.normal(ks[5], (E, K, 2), jnp.float32) * 0.1, 'expert_scale': jnp.ones((E,), jnp.float32), 'shared_w_gate': jax.random.normal(ks[6], (H, 2 * I), jnp.float32) * s, 'shared_w_up': jax.random.normal(ks[7], (H, 2 * I), jnp.float32) * s, 'shared_w_down': jax.random.normal(ks[8], (2 * I, H), jnp.float32) * s}
    _L0_ffn_in = _L0_ffn_setup()
    _L0_c = _w((lambda *s: np.random.randn(*s).astype(np.float32) * 0.05)(16, 256))
    _L0_wmod = _w((lambda *s: np.random.randn(*s).astype(np.float32) * 0.05)(256, 6 * 256) * 256 ** (-0.5))
    _d = {'L0_attn_x': _L0_attn_in['x'], 'L0_attn_Wq_sem': _L0_attn_in['Wq_sem'], 'L0_attn_Wk_sem': _L0_attn_in['Wk_sem'], 'L0_attn_Wq_geo': _L0_attn_in['Wq_geo'], 'L0_attn_Wk_geo': _L0_attn_in['Wk_geo'], 'L0_attn_Wv': _L0_attn_in['Wv'], 'L0_attn_Wo': _L0_attn_in['Wo'], 'L0_attn_logit_scale': _L0_attn_in['logit_scale'], 'L0_ffn_w_router': _L0_ffn_in['w_router'], 'L0_ffn_w_gate': _L0_ffn_in['w_gate'], 'L0_ffn_w_up': _L0_ffn_in['w_up'], 'L0_ffn_w_down': _L0_ffn_in['w_down'], 'L0_ffn_amplitudes': _L0_ffn_in['amplitudes'], 'L0_ffn_expert_scale': _L0_ffn_in['expert_scale'], 'L0_ffn_shared_w_gate': _L0_ffn_in['shared_w_gate'], 'L0_ffn_shared_w_up': _L0_ffn_in['shared_w_up'], 'L0_ffn_shared_w_down': _L0_ffn_in['shared_w_down'], 'L0_c': _L0_c, 'L0_wmod': _L0_wmod}
    _x0 = _d['L0_attn_x']
    _d['L0_attn_x'] = jax.random.normal(jax.random.fold_in(jax.random.key(seed), 1), (16, 256, 256), dtype=_x0.dtype)
    del _x0
    return _d

def reference(L0_attn_x, L0_attn_Wq_sem, L0_attn_Wk_sem, L0_attn_Wq_geo, L0_attn_Wk_geo, L0_attn_Wv, L0_attn_Wo, L0_attn_logit_scale, L0_ffn_w_router, L0_ffn_w_gate, L0_ffn_w_up, L0_ffn_w_down, L0_ffn_amplitudes, L0_ffn_expert_scale, L0_ffn_shared_w_gate, L0_ffn_shared_w_up, L0_ffn_shared_w_down, L0_c, L0_wmod):

    def _L0_attn_ref(x, Wq_sem, Wk_sem, Wq_geo, Wk_geo, Wv, Wo, logit_scale):
        import jax, jax.numpy as jnp
        import numpy as np
        D_MODEL = 256
        H = 16
        HKV = 4
        DS = 32
        DG = 32
        DV = 64
        B, T = (2, 512)
        MB = 64
        LW = 128
        ROPE_BASE = 10000.0
        NEG_INF = -1000000000.0

        def _rope(x, pos, base):
            d = x.shape[-1]
            inv_freq = 1.0 / base ** (jnp.arange(0, d, 2, dtype=jnp.float32) / d)
            ang = pos.astype(jnp.float32)[:, None] * inv_freq
            cos, sin = (jnp.cos(ang), jnp.sin(ang))
            x1, x2 = jnp.split(x, 2, axis=-1)
            return jnp.concatenate([x1 * cos - x2 * sin, x2 * cos + x1 * sin], axis=-1)
        Bq, Tq = (x.shape[0], x.shape[1])
        split = lambda y, h, d: y.reshape(Bq, Tq, h, d).transpose(0, 2, 1, 3)
        q_sem = split(x @ Wq_sem, H, DS)
        k_sem = split(x @ Wk_sem, HKV, DS)
        q_geo = split(x @ Wq_geo, H, DG)
        k_geo = split(x @ Wk_geo, HKV, DG)
        v = split(x @ Wv, HKV, DV)
        pos = jnp.arange(Tq)
        q_geo = _rope(q_geo, pos, ROPE_BASE)
        k_geo = _rope(k_geo, pos, ROPE_BASE)
        remote = Tq - LW
        nblk = remote // MB
        pool = lambda a: jnp.concatenate([a[:, :, :remote].reshape(Bq, HKV, nblk, MB, a.shape[-1]).mean(axis=3), a[:, :, remote:]], axis=2)
        k_sem2, k_geo2, v2 = (pool(k_sem), pool(k_geo), pool(v))
        k_pos = jnp.concatenate([jnp.arange(nblk) * MB + (MB - 1), jnp.arange(remote, Tq)])
        rep = lambda a: jnp.repeat(a, H // HKV, axis=1)
        k_sem2, k_geo2, v2 = (rep(k_sem2), rep(k_geo2), rep(v2))
        scores = jnp.einsum('bhqd,bhkd->bhqk', q_sem, k_sem2) * (1.0 / jnp.sqrt(float(DS))) + jnp.einsum('bhqd,bhkd->bhqk', q_geo, k_geo2) * (1.0 / jnp.sqrt(float(DG)))
        scores = scores * jnp.exp(logit_scale)[None, :, None, None]
        mask = k_pos[None, :] <= pos[:, None]
        scores = jnp.where(mask[None, None], scores, NEG_INF)
        probs = jax.nn.softmax(scores, axis=-1)
        out = jnp.einsum('bhqk,bhkd->bhqd', probs, v2)
        out = out.transpose(0, 2, 1, 3).reshape(Bq, Tq, H * DV)
        return out @ Wo

    def _L0_ffn_ref(x, w_router, w_gate, w_up, w_down, amplitudes, expert_scale, shared_w_gate, shared_w_up, shared_w_down):
        import jax, jax.numpy as jnp
        import numpy as np
        H = 256
        I = 128
        K = 8
        E = 128
        TOPK = 4
        EPS = 1e-08
        B, S, _ = x.shape
        T = B * S
        xt = x.reshape(T, H)
        probs = jax.nn.softmax(xt @ w_router, axis=-1)
        topk_p, topk_idx = jax.lax.top_k(probs, TOPK)
        topk_w = topk_p / (jnp.sum(topk_p, axis=-1, keepdims=True) + EPS)
        gate = (xt @ w_gate).reshape(T, K, I)
        up = (xt @ w_up).reshape(T, K, I)
        basis = jax.nn.silu(gate) * up
        p = amplitudes[..., 0] ** 2 + amplitudes[..., 1] ** 2
        mix = p / (jnp.sum(p, axis=-1, keepdims=True) + EPS)
        mix_sel = mix[topk_idx]
        mixed = jnp.einsum('tek,tki->tei', mix_sel, basis)
        down = jnp.einsum('tei,ih->teh', mixed, w_down)
        coeff = topk_w * expert_scale[topk_idx]
        out = jnp.einsum('teh,te->th', down, coeff)
        shared = jax.nn.silu(xt @ shared_w_gate) * (xt @ shared_w_up) @ shared_w_down
        out = out + shared
        return out.reshape(B, S, H)
    x = L0_attn_x
    mod = (_silu(L0_c) @ L0_wmod).reshape(L0_c.shape[0], 6, 1, -1)
    sa, ca, ga, sb, cb, gb = (mod[:, 0], mod[:, 1], mod[:, 2], mod[:, 3], mod[:, 4], mod[:, 5])
    ga = (2 * (ga >= 0) - 1) * jnp.maximum(jnp.abs(ga), 0.25)
    gb = (2 * (gb >= 0) - 1) * jnp.maximum(jnp.abs(gb), 0.25)
    h = _layernorm(x, axis=-1) * (1 + ca) + sa
    x = x + ga * _L0_attn_ref(h, L0_attn_Wq_sem, L0_attn_Wk_sem, L0_attn_Wq_geo, L0_attn_Wk_geo, L0_attn_Wv, L0_attn_Wo, L0_attn_logit_scale)
    h = _layernorm(x, axis=-1) * (1 + cb) + sb
    x = x + gb * _L0_ffn_ref(h, L0_ffn_w_router, L0_ffn_w_gate, L0_ffn_w_up, L0_ffn_w_down, L0_ffn_amplitudes, L0_ffn_expert_scale, L0_ffn_shared_w_gate, L0_ffn_shared_w_up, L0_ffn_shared_w_down)
    return x

_drawn_inputs = setup_inputs


def setup_inputs(seed=0):
    import zlib

    import numpy as np

    out = dict(_drawn_inputs(seed))
    spreads = {'L0_attn_logit_scale': (0.0, 0.8), 'L0_ffn_expert_scale': (1.0, 0.6)}
    factors = {'L0_attn_Wq_sem': 8.0,
     'L0_attn_Wk_sem': 8.0,
     'L0_attn_Wq_geo': 8.0,
     'L0_attn_Wk_geo': 8.0,
     'L0_attn_Wv': 8.0,
     'L0_attn_Wo': 8.0,
     'L0_ffn_w_router': 8.0,
     'L0_ffn_w_gate': 8.0,
     'L0_ffn_w_up': 8.0,
     'L0_ffn_w_down': 8.0,
     'L0_ffn_amplitudes': 8.0,
     'L0_ffn_shared_w_gate': 8.0,
     'L0_ffn_shared_w_up': 8.0,
     'L0_ffn_shared_w_down': 8.0,
     'L0_c': 6.816,
     'L0_wmod': 6.944}
    for name, (base, spread) in spreads.items():
        noise = np.random.default_rng([zlib.crc32(name.encode()), seed]).standard_normal(out[name].shape)
        drawn = base * np.exp(spread * noise) if base else spread * noise
        out[name] = jnp.asarray(drawn.astype(out[name].dtype))
    for name, factor in factors.items():
        out[name] = (out[name] * factor).astype(out[name].dtype)
    return out
```

```python
from contextlib import ExitStack

import concourse.bass as bass
from concourse import mybir

ALU = mybir.AluOpType
ACT = mybir.ActivationFunctionType
F32 = mybir.dt.float32
F32R = mybir.dt.float32r
BF16 = mybir.dt.bfloat16
X = mybir.AxisListType.X

P = 128
B, T, D = 16, 256, 256
NT = B * T // P
H, HKV, DH = 16, 4, 64
NP = 2
NK = P + NP
QC, KC, VC = H * DH, HKV * DH, HKV * DH
QKV = QC + KC + VC
NE, NB = 128, 8
NCH = 5
LN_EPS, EPS = 1e-5, 1e-8
HIDE = -float(2 ** 30)
TAKEN = -3.0e38

C_ID = 0
C_COS1 = C_ID + P
C_SIN1 = C_COS1 + 32
C_COS0 = C_SIN1 + 32
C_SIN0 = C_COS0 + 32
C_COSL = C_SIN0 + 32
C_SINL = C_COSL + 32
C_POOL0 = C_SINL + 32
C_POOL1 = C_POOL0 + 4
C_SEL = C_POOL1 + 4
NTAB = C_SEL + P

A0, A1, A2, A3, AO, FM, FR = 0, 1, 2, 3, 4, 5, 6


def build(nc, x_in, wq_sem, wk_sem, wq_geo, wk_geo, wv, wo, logit_scale, w_router, w_gate, w_up,
          w_down, amplitudes, expert_scale, sw_gate, sw_up, sw_down, c_in, wmod, table, mask_in, out):
    gates_dram = nc.dram_tensor("gates", [B, 2, D], F32, kind="Internal").ap()
    rows_dram = nc.dram_tensor("rows", [3, B, D], F32, kind="Internal").ap()
    vw_dram = nc.dram_tensor("vw", [B, NP, H, D], F32, kind="Internal").ap()

    with ExitStack() as ctx:
        def sb(name, shape, dt=F32):
            return ctx.enter_context(nc.sbuf_tensor(name, shape, dt))

        def sem(name):
            return ctx.enter_context(nc.semaphore(name))

        ps = ctx.enter_context(nc.psum_tensor("ps", [P, 8, 512], F32))

        tab = sb("tab", [P, NTAB])
        ident = tab[:, C_ID:C_ID + P]
        pool0, pool1 = tab[:, C_POOL0:C_POOL0 + 4], tab[:, C_POOL1:C_POOL1 + 4]
        x = sb("x", [P, NT, D])
        st = sb("st", [P, NT, 2])
        rs1 = sb("rs1", [P, NT])
        modT = sb("modT", [P, B, 8])
        wqkv_h = sb("wqkv_h", [P, 2, QKV], F32R)
        wqkv_l = sb("wqkv_l", [P, 2, QKV], F32R)
        wo_h = sb("wo_h", [P, 8, D], F32R)
        wo_l = sb("wo_l", [P, 8, D], F32R)
        wgu_h = sb("wgu_h", [P, 2, NCH, 512], F32R)
        wgu_l = sb("wgu_l", [P, 2, NCH, 512], F32R)
        wr_h = sb("wr_h", [P, 2, NE], F32R)
        wr_l = sb("wr_l", [P, 2, NE], F32R)
        wd_h = sb("wd_h", [P, 3, D], F32R)
        wd_l = sb("wd_l", [P, 3, D], F32R)
        mix = sb("mix", [P, NB])
        kpool = sb("kpool", [P, B, 2, NP])
        id16 = sb("id16", [P, P], BF16)
        mask16 = sb("mask16", [P, 3, NK], BF16)
        mhalf = sb("mhalf", [P, NT])

        early = sb("early", [P, 2560])
        probs = early[:, 0:H * NK].rearrange("p (h k) -> p h k", k=NK)
        qk = early[:, 0:QC + KC].rearrange("p (h e) -> p h e", e=DH)
        rot1 = early[:, 1280:1920].rearrange("p (h e) -> p h e", e=32)
        rot2 = early[:, 1920:2560].rearrange("p (h e) -> p h e", e=32)
        gate_a = sb("gate_a", [P, D])
        gate_f = sb("gate_f", [P, D])
        vwb = sb("vwb", [NP * H, D])
        rowb = sb("rowb", [3, D])
        mod_a = sb("mod_a", [P, 4])
        mod_f = sb("mod_f", [P, 4])
        xh = sb("xh", [P, D])
        hf = sb("hf", [P, 2, P])
        hh = sb("hh", [P, 2, P], F32R)
        hl = sb("hl", [P, 2, P], F32R)
        qT_h = sb("qT_h", [P, 8, P], F32R)
        qT_l = sb("qT_l", [P, 8, P], F32R)
        kT_h = sb("kT_h", [P, 2, 2, NK], F32R)
        kT_l = sb("kT_l", [P, 2, 2, NK], F32R)
        v_h = sb("v_h", [P, 2, 2, P], F32R)
        v_l = sb("v_l", [P, 2, 2, P], F32R)
        nmax = sb("nmax", [P, 2, 8])
        psums = sb("psums", [P, 2, 8])
        rinv = sb("rinv", [P, 2, 8])
        pT_h = sb("pT_h", [P, 2, 512], F32R)
        pT_l = sb("pT_l", [P, 2, 512], F32R)
        pp = sb("pp", [P, NP, H])
        ppT = sb("ppT", [NP * H, P])
        oT_h = sb("oT_h", [P, 8, P], F32R)
        oT_l = sb("oT_l", [P, 8, P], F32R)
        upd = sb("upd", [P, 2, D])

        stage = [sb(f"stage{i}", [P, 1024]) for i in range(2)]
        th = [stage[0][:, 256 * i:256 * i + 256] for i in range(2)]
        act_g = [stage[0][:, 512 + 256 * i:768 + 256 * i] for i in range(2)]
        acc = stage[1][:, 0:256]
        mixed = [stage[1][:, 256 + 128 * i:384 + 128 * i] for i in range(2)]
        xh2 = stage[1][:, 512:768]
        hf2 = stage[1][:, 768:1024].rearrange("p (h n) -> p h n", h=2)
        prod = sb("prod", [P, 4, 256])
        shared = [sb(f"shared{u}", [P, 256]) for u in range(2)]
        bst = sb("bst", [P, 6])
        beat = sb("beat", [P, 2])
        leps = sb("leps", [P, 1])
        mv = sb("mv", [P, 2])
        veps = sb("veps", [P, 1])
        rs2 = sb("rs2", [P, 1])
        fh = [sb(f"fh{u}", [P, 2, P], F32R) for u in range(2)]
        fl = [sb(f"fl{u}", [P, 2, P], F32R) for u in range(2)]
        lg = sb("lg", [P, NE])
        top8 = sb("top8", [P, 8])
        take = sb("take", [P, 8])
        nm = sb("nm", [P, 1])
        rest = sb("rest", [P, NE])
        ex = sb("ex", [P, NE])
        zsum = sb("zsum", [P, 1])
        s4 = sb("s4", [P, 1])
        den = sb("den", [P, 2])
        rn = sb("rn", [P, 1])
        coef = sb("coef", [P, NE])
        coefT = sb("coefT", [P, P])
        w8 = [sb(f"w8_{u}", [P, NB]) for u in range(2)]
        mT_h = sb("mT_h", [P, 3, P], F32R)
        mT_l = sb("mT_l", [P, 3, P], F32R)
        updf = sb("updf", [P, D])

        c_row = early[0:B, 0:768].rearrange("p (a d) -> p a d", a=3)
        modrow = early[0:B, 768:768 + 6 * D]
        cT = sb("cT", [P, 2, B])
        bst4 = sb("bst4", [P, 4, 6])
        mv4 = sb("mv4", [P, 4, 2])
        lsc = sb("lsc", [P, 2, H])
        amp = sb("amp", [P, NB, 2])
        ampp = sb("ampp", [P, NB])
        amps = sb("amps", [P, 4])
        mask_f = upd[:].rearrange("p a d -> p (a d)")[:, 0:3 * NK]
        mod_p = [sb(f"mod_p{i}", [P, 4]) for i in range(2)]
        xh0 = [early[:, 1024 * i:1024 * i + 256] for i in range(2)]
        xh1 = [early[:, 1024 * i + 256:1024 * i + 512] for i in range(2)]
        kr0 = [early[:, 1024 * i + 512:1024 * i + 768] for i in range(2)]
        rk1 = [early[:, 1024 * i + 768:1024 * i + 896].rearrange("p (h e) -> p h e", e=32) for i in range(2)]
        rk2 = [early[:, 1024 * i + 896:1024 * i + 1024].rearrange("p (h e) -> p h e", e=32) for i in range(2)]
        hf0 = [hf, sb("hf0b", [P, 2, P])]
        h0h, h0l = [hh, fh[0]], [hl, fl[0]]
        hpool = sb("hpool", [P, 2, 4, B])
        hp_h = sb("hp_h", [P, 2, 4, B], F32R)
        hp_l = sb("hp_l", [P, 2, 4, B], F32R)
        vTf = sb("vTf", [P, 2, NP * B])
        q127 = early[0:B, 0:1024].rearrange("p (h e) -> p h e", e=DH)
        tmpq = early[0:B, 1024:2048].rearrange("p (h e) -> p h e", e=DH)
        kprow = early[0:B, 2048:2560].rearrange("p (k n) -> p k n", k=NP)
        dots = stage[0][0:B, 0:1024].rearrange("p (h e) -> p h e", e=DH)
        vrow = stage[1][0:B, 0:768].rearrange("p (r n) -> p r n", r=3)
        s127 = stage[1][0:B, 768:768 + NP * H].rearrange("p (k h) -> p k h", k=NP)
        sm127 = stage[1][0:B, 832:832 + 6 * H].rearrange("p (k h) -> p k h", k=6)
        rT = prod[:].rearrange("p a n -> p (a n)")[:, 0:8 * 48].rearrange("p (j r b) -> p j r b", j=8, r=3)
        vws = early[0:NP * B, 0:2048].rearrange("p (h n) -> p h n", n=D)
        rows_sb = updf[0:48, :]

        names = """tab_ld mask_ld c_ld mod_ld small_ld stage_ld0 stage_ld1 x_ld0 x_ld1 x_ld2 x_ld3
        silu_t silu_a silu_row cT_ps cT_copied mod_ps modrow_done gate_fix modT_ps modT_done gates_st
        lsc_exp lsc_done amp_d mix_done mask_done const_done q_scaled piece_hi piece_lo
        bn1 aggr1 stats_done rs_var rs_done
        a_xh a_ps a_hf a_hi a_lo a_kps a_ksem a_km a_krot a_kp_ps a_kp a_hp
        hp_hi hp_lo z_v_ps z_v_copied z_q_ps z_kp_ps z_chain z_exp z_row_ps z_rT z_rT_hi
        z_rT_lo z_vT_ps z_vT z_vT_hi z_vT_lo z_rows_ps z_rows z_rows_st z_vw_ps z_vw z_vw_st z_zero
        gate_a_ld gate_f_ld vw_ld row_ld
        mod_a_ready xh_ready hT_ps hf_ready h_hi h_lo kv_ps q_ps v_hi q_sem v_lo k_m q_m k_rot q_rot
        kT_ps qT_ps kp_hi kT_hi kT_lo qT_hi qT_lo s_ps nmax_ready exp_done rinv_ready p_ready
        pT_ps pT_hi pT_lo o_ps oT_hi_r oT_lo_r pp_ps ppT_ready row_ps y_ps upd_ready x_mid
        f_bn f_var f_veps f_rs f_xh f_mod f_hT_ps f_hf f_hi f_lo l_ps lg_ready top_ready nm_ready take_ready
        rest_ready ex_ready coef_ready den_ready rcp_ready rn_ready cT2_ps cT2_ready w_ps w8_ready
        gu_ps th_ready ag_ready chunk_done mix_sum mixed_ready m_ps mT_hi_r mT_lo_r d_ps updf_ready x_done
        out_st""".split()
        S = {n: sem(n) for n in names}

        block = ctx.enter_context(nc.Block())

        def d_rows(ap):
            return ap.rearrange("(h p) n -> p h n", p=P)

        def halves(stg):
            return stg[:].rearrange("p (h n) -> p h n", h=2)

        wo_rows = wo.rearrange("(t s j e) n -> s t e j n", t=2, s=2, j=JH_)

        PIECES = ["m0", "m1", "m2", "kv", "qs", "qg", "o0", "o1", "rd", "g0", "u0", "g1", "u1", "sh"]
        SPLIT = PIECES[3:]
        LOADS = {"kv": 3, "o0": 2, "o1": 2, "rd": 3, "sh": 2}

        def loads_to(i):
            return 16 * sum(LOADS.get(p, 1) for p in PIECES[i % 2:i + 1:2])

        def split_views(name, stg):
            s3 = halves(stg)
            if name == "kv":
                r = []
                for lo, e0 in ((0, 0), (128, 32)):
                    src = s3[:, :, lo:lo + 128].rearrange("p h (g e) -> p h g e", e=32)
                    dst = [w[:, :, QC:QC + KC].rearrange("p h (g e) -> p h g e", e=DH)[:, :, :, e0:e0 + 32]
                           for w in (wqkv_h, wqkv_l)]
                    r.append((src, dst[0], dst[1]))
                r.append((s3[:, :, 256:512], wqkv_h[:, :, QC + KC:QKV], wqkv_l[:, :, QC + KC:QKV]))
                return r
            if name in ("qs", "qg"):
                e0 = 0 if name == "qs" else 32
                r = []
                for h in range(2):
                    for t in range(2):
                        src = s3[:, h, 256 * t:256 * t + 256].rearrange("p (s j e) -> p j s e", s=2, j=4)
                        dst = [w[:, h, 512 * t:512 * t + 512].rearrange("p (j s e) -> p j s e", j=4, s=2)
                               [:, :, :, e0:e0 + 32] for w in (wqkv_h, wqkv_l)]
                        r.append((src, dst[0], dst[1]))
                return r
            if name in ("o0", "o1"):
                t = int(name[1])
                return [(stg[:].rearrange("p (j n) -> p j n", j=4), wo_h[:, 4 * t:4 * t + 4, :],
                         wo_l[:, 4 * t:4 * t + 4, :])]
            if name == "rd":
                return [(stg[:, 0:256].rearrange("p (h n) -> p h n", h=2), wr_h[:], wr_l[:]),
                        (stg[:, 256:1024].rearrange("p (k n) -> p k n", k=3), wd_h[:], wd_l[:])]
            if name == "sh":
                s4_ = stg[:].rearrange("p (a h n) -> p a h n", a=2, h=2)
                return [(s4_[:, a], wgu_h[:, :, 0, 256 * a:256 * a + 256], wgu_l[:, :, 0, 256 * a:256 * a + 256])
                        for a in range(2)]
            a, c0 = (0 if name[0] == "g" else 256), 1 + 2 * int(name[1])
            return [(s3.rearrange("p h (c n) -> p h c n", c=2), wgu_h[:, :, c0:c0 + 2, a:a + 256],
                     wgu_l[:, :, c0:c0 + 2, a:a + 256])]

        def real(n):
            return not isinstance(n, int) or 0 <= n < NT

        @block.sync
        def _(sp):
            sp.dma_start(c_row[:, 0, :], c_in).then_inc(S["c_ld"], 16)
            sp.dma_start(tab[:], table).then_inc(S["tab_ld"], 16)
            sp.dma_start(mask_f, mask_in).then_inc(S["mask_ld"], 16)
            sp.dma_start(lsc[:, 0, :], logit_scale.rearrange("(a h) -> a h", a=1).to_broadcast([P, H])
                         ).then_inc(S["small_ld"], 16)
            sp.dma_start(amp[:], amplitudes).then_inc(S["small_ld"], 16)
            sp.dma_start(amps[:, 2:3], expert_scale.rearrange("(e a) -> e a", a=1)).then_inc(S["small_ld"], 16)

            def load_piece(i):
                name, stg, s = PIECES[i], stage[i % 2], S[f"stage_ld{i % 2}"]
                s3 = halves(stg)
                if 2 <= i < 5:
                    sp.wait_ge(S["mod_ps"], i - 1)
                if i >= 5:
                    sp.wait_ge(S["piece_lo"], i - 4)
                if name[0] == "m":
                    n = int(name[1])
                    sp.dma_start(s3, d_rows(wmod)[:, :, 512 * n:512 * n + 512]).then_inc(s, 16)
                elif name == "kv":
                    sp.dma_start(s3[:, :, 0:128], d_rows(wk_sem)).then_inc(s, 16)
                    sp.dma_start(s3[:, :, 128:256], d_rows(wk_geo)).then_inc(s, 16)
                    sp.dma_start(s3[:, :, 256:512], d_rows(wv)).then_inc(s, 16)
                elif name in ("qs", "qg"):
                    sp.dma_start(s3, d_rows(wq_sem if name == "qs" else wq_geo)).then_inc(s, 16)
                elif name in ("o0", "o1"):
                    o4 = stg[:].rearrange("p (j n) -> p j n", j=4)
                    for k in range(2):
                        sp.dma_start(o4[64 * k:64 * k + 64], wo_rows[k, int(name[1])]).then_inc(s, 16)
                elif name == "rd":
                    sp.dma_start(stg[:, 0:256].rearrange("p (h n) -> p h n", h=2), d_rows(w_router)).then_inc(s, 16)
                    sp.dma_start(stg[:, 256:512], w_down).then_inc(s, 16)
                    sp.dma_start(stg[:, 512:1024].rearrange("p (h n) -> p h n", h=2), d_rows(sw_down)).then_inc(s, 16)
                elif name == "sh":
                    s4_ = stg[:].rearrange("p (a h n) -> p a h n", a=2, h=2)
                    sp.dma_start(s4_[:, 0], d_rows(sw_gate)).then_inc(s, 16)
                    sp.dma_start(s4_[:, 1], d_rows(sw_up)).then_inc(s, 16)
                else:
                    w, n = (w_gate if name[0] == "g" else w_up), int(name[1])
                    sp.dma_start(s3, d_rows(w)[:, :, 512 * n:512 * n + 512]).then_inc(s, 16)

            load_piece(0)
            load_piece(1)
            x_tiles = x_in.rearrange("b (u p) d -> p (b u) d", p=P)
            for q in range(2):
                sp.dma_start(x[:, 8 * q:8 * q + 8, :], x_tiles[:, 8 * q:8 * q + 8, :]).then_inc(S[f"x_ld{q}"], 16)
            load_piece(2)
            load_piece(3)
            for q in range(2, 4):
                sp.dma_start(x[:, 8 * q:8 * q + 8, :], x_tiles[:, 8 * q:8 * q + 8, :]).then_inc(S[f"x_ld{q}"], 16)
            sp.wait_ge(S["gate_fix"], 5)
            for a, col in ((0, 2 * D), (1, 5 * D)):
                sp.dma_start(gates_dram[:, a, :], modrow[:, col:col + D]).then_inc(S["gates_st"], 16)
            for i in range(4, len(PIECES)):
                load_piece(i)
            sp.wait_ge(S["z_rows"], 1)
            sp.dma_start(rows_dram.rearrange("r b n -> (r b) n"), rows_sb).then_inc(S["z_rows_st"], 16)
            for t in range(2):
                sp.wait_ge(S["z_vw"], 4 * t + 4)
                for k in range(NP):
                    sp.dma_start(vw_dram[:, k, 8 * t:8 * t + 8, :], vws[B * k:B * k + B]).then_inc(S["z_vw_st"], 16)
            sp.wait_ge(S["gates_st"], 32)
            sp.wait_ge(S["z_rows_st"], 16)
            sp.wait_ge(S["z_vw_st"], 64)

            def load_entry(b):
                sp.dma_start(gate_a[:], gates_dram[b, 0:1, :].to_broadcast([P, D])).then_inc(S["gate_a_ld"], 16)
                sp.dma_start(vwb[:], vw_dram[b].rearrange("k h n -> (k h) n")).then_inc(S["vw_ld"], 16)
                sp.dma_start(rowb[:], rows_dram[:, b, :]).then_inc(S["row_ld"], 16)

            def load_gate_f(f):
                sp.dma_start(gate_f[:], gates_dram[f, 1:2, :].to_broadcast([P, D])).then_inc(S["gate_f_ld"], 16)

            def store(f):
                for u in range(2):
                    sp.wait_ge(S["x_done"], 2 * f + u + 2)
                    sp.dma_start(out[f, P * u:P * u + P, :], x[:, 2 * f + u, :]).then_inc(S["out_st"], 16)

            load_entry(0)
            sp.wait_ge(S["x_mid"], 1)
            load_entry(1)
            load_gate_f(0)
            with sp.Fori(2, B) as b:
                sp.wait_ge(S["x_mid"], b)
                load_entry(b)
                store(b - 2)
                load_gate_f(b - 1)
            store(B - 2)
            load_gate_f(B - 1)
            store(B - 1)
            sp.wait_ge(S["out_st"], 16 * NT)

        @block.gpsimd
        def _(gp):
            gp.memset(leps[:], LN_EPS)
            gp.memset(mhalf[:], -0.5).then_inc(S["const_done"], 1)
            for i, name in enumerate(SPLIT):
                gp.wait_ge(S["piece_hi"], i + 1)
                views = split_views(name, stage[(i + 3) % 2])
                for k, (src, hi, lo) in enumerate(views):
                    ins = gp.tensor_tensor(lo, src, hi.bitcast(F32), ALU.subtract)
                    if k == len(views) - 1:
                        ins.then_inc(S["piece_lo"], 1)
                if name == "kv":
                    gp.wait_ge(S["stats_done"], NT // 4)
                    gp.wait_ge(S["const_done"], 1)
                    gp.tensor_scalar(rs1[:], st[:, :, 1], LN_EPS, None, ALU.add).then_inc(S["rs_var"], 1)
                    gp.wait_ge(S["rs_var"], 1)
                    gp.tensor_tensor(rs1[:], rs1[:], mhalf[:], ALU.pow).then_inc(S["rs_done"], 1)

            def keys_and_queries(b):
                gp.wait_ge(S["k_m"], b + 1)
                gp.tensor_tensor(qk[:, H:, 32:64], rot1[:, H:], rot2[:, H:], ALU.add).then_inc(S["k_rot"], 1)
                gp.wait_ge(S["q_m"], b + 1)
                gp.tensor_tensor(qk[:, 0:H, 32:64], rot1[:, 0:H], rot2[:, 0:H], ALU.add).then_inc(S["q_rot"], 1)

            def normalise(b, t):
                gp.wait_ge(S["rinv_ready"], 2 * b + t + 1)
                scale = rinv[:, t, :].unsqueeze(2)
                gp.tensor_tensor(pp[:, :, 8 * t:8 * t + 8].rearrange("p k h -> p h k"),
                                 probs[:, 8 * t:8 * t + 8, P:NK], scale.to_broadcast([P, 8, NP]), ALU.mult)
                gp.tensor_tensor(probs[:, 8 * t:8 * t + 8, 0:P], probs[:, 8 * t:8 * t + 8, 0:P],
                                 scale.to_broadcast([P, 8, P]), ALU.mult).then_inc(S["p_ready"], 1)

            def ln2(n):
                gp.wait_ge(S["f_var"], n + 1)
                gp.tensor_tensor(veps[:], mv[:, 1:2], leps[:], ALU.add).then_inc(S["f_veps"], 1)
                gp.wait_ge(S["f_veps"], n + 1)
                gp.tensor_tensor(rs2[:], veps[:], mhalf[:, 0:1], ALU.pow).then_inc(S["f_rs"], 1)

            def mix_sum(n, u, k):
                gp.wait_ge(S["chunk_done"], NCH * n + k + 1 + 2)
                if k == 2:
                    if not (isinstance(n, int) and n == 0):
                        gp.wait_ge(S["mixed_ready"], n)
                    gp.tensor_tensor(acc, prod[:, 0, :], prod[:, 1, :], ALU.add).then_inc(S["mix_sum"], 1)
                else:
                    gp.wait_ge(S["mix_sum"], 3 * n + k - 2)
                    gp.tensor_tensor(acc, acc, prod[:, k - 1, :], ALU.add).then_inc(S["mix_sum"], 1)
                if k == 4:
                    gp.wait_ge(S["mix_sum"], 3 * n + 3)
                    gp.tensor_tensor(mixed[u], acc[:, 0:128], acc[:, 128:256], ALU.add
                                     ).then_inc(S["mixed_ready"], 1)

            def body(b, attn):
                m0, m1, m2 = 2 * b - 3, 2 * b - 2, 2 * b - 1
                if real(m1):
                    ln2(m1)
                if attn:
                    keys_and_queries(b)
                if real(m0):
                    for k in range(2, 5):
                        mix_sum(m0, 1, k)
                if attn:
                    normalise(b, 0)
                if real(m2):
                    ln2(m2)
                if real(m1):
                    mix_sum(m1, 0, 2)
                if attn:
                    normalise(b, 1)
                if real(m1):
                    mix_sum(m1, 0, 3)
                    mix_sum(m1, 0, 4)

            body(0, True)
            body(1, True)
            with gp.Fori(2, B) as b:
                body(b, True)
            body(B, False)
            body(B + 1, False)

        @block.tensor
        def _(pe):
            def mm3(out_, lh, ll, rh, rl, start, stop, **kw):
                pe.matmul(out_, lh, rh, start=start, stop=False, **kw)
                pe.matmul(out_, lh, rl, start=False, stop=False, **kw)
                return pe.matmul(out_, ll, rh, start=False, stop=stop, **kw)

            pe.wait_ge(S["tab_ld"], 16)
            pe.wait_ge(S["silu_row"], 1)
            for h in range(2):
                ins = pe.transpose(ps[:, AO, 16 * h:16 * h + 16], c_row[:, 2, P * h:P * h + P], ident[0:B, 0:B])
            ins.then_inc(S["cT_ps"], 1)
            pe.wait_ge(S["cT_copied"], 1)
            for n in range(3):
                pe.wait_ge(S[f"stage_ld{n % 2}"], loads_to(n))
                for h in range(2):
                    ins = pe.matmul(ps[0:B, n, :], cT[:, h, :], halves(stage[n % 2])[:, h, :],
                                    start=(h == 0), stop=(h == 1))
                ins.then_inc(S["mod_ps"], 1)
            pe.wait_ge(S["modrow_done"], 4)
            for k, col in enumerate((D, 0, 4 * D, 3 * D)):
                for h in range(2):
                    ins = pe.transpose(ps[:, AO, 32 + 16 * (2 * k + h):48 + 16 * (2 * k + h)],
                                       modrow[:, col + P * h:col + P * h + P], ident[0:B, 0:B])
            ins.then_inc(S["modT_ps"], 1)

            pe.wait_ge(S["piece_lo"], 1)
            with pe.Fori(0, B // 2) as i:
                for p in range(2):
                    pe.wait_ge(S["a_xh"], 2 * i + p + 1)
                    for h in range(2):
                        pe.transpose(ps[:, p, P * h:P * h + P], xh0[p][:, P * h:P * h + P], ident)
                    for h in range(2):
                        pe.matmul(ps[:, p, 256 + 4 * h:260 + 4 * h], xh0[p][:, P * h:P * h + P], pool0,
                                  start=True, stop=False)
                        ins = pe.matmul(ps[:, p, 256 + 4 * h:260 + 4 * h], xh1[p][:, P * h:P * h + P], pool1,
                                        start=False, stop=True)
                    ins.then_inc(S["a_ps"], 1)
                for p in range(2):
                    pe.wait_ge(S["a_lo"], 2 * i + p + 1)
                    for h in range(2):
                        ins = mm3(ps[:, 2 + p, 0:KC], h0h[p][:, h, :], h0l[p][:, h, :],
                                  wqkv_h[:, h, QC:QC + KC], wqkv_l[:, h, QC:QC + KC], h == 0, h == 1)
                    ins.then_inc(S["a_kps"], 1)
                for p in range(2):
                    pe.wait_ge(S["a_krot"], 2 * i + p + 1)
                    for t in range(2):
                        ins = pe.matmul(ps[:, 4 + p, 2 * t:2 * t + 2], kr0[p][:, P * t:P * t + P],
                                        pool0[:, 0:2], start=True, stop=True)
                    ins.then_inc(S["a_kp_ps"], 1)

            pe.wait_ge(S["hp_lo"], 1)
            pe.wait_ge(S["piece_lo"], 5)
            for k, r in enumerate((3, 0, 1)):
                for h in range(2):
                    ins = mm3(ps[0:B, k // 2, 256 * (k % 2):256 * (k % 2) + 256], hp_h[:, h, r, :], hp_l[:, h, r, :],
                              wqkv_h[:, h, QC + KC:QKV], wqkv_l[:, h, QC + KC:QKV], h == 0, h == 1)
            ins.then_inc(S["z_v_ps"], 1)
            for t in range(2):
                for h in range(2):
                    ins = mm3(ps[0:B, 2 + t, :], hp_h[:, h, 2, :], hp_l[:, h, 2, :],
                              wqkv_h[:, h, 512 * t:512 * t + 512], wqkv_l[:, h, 512 * t:512 * t + 512],
                              h == 0, h == 1)
            ins.then_inc(S["z_q_ps"], 1)
            pe.wait_ge(S["a_kp"], B)
            for k in range(NP):
                for t in range(2):
                    ins = pe.transpose(ps[0:B, 4, 256 * k + P * t:256 * k + P * t + P], kpool[:, :, t, k], ident)
            ins.then_inc(S["z_kp_ps"], 1)
            for t in range(2):
                for h in range(2):
                    ins = mm3(ps[:, 5, 32 * t:32 * t + 32], wqkv_h[:, h, QC + KC + P * t:QC + KC + P * t + P],
                              wqkv_l[:, h, QC + KC + P * t:QC + KC + P * t + P],
                              hp_h[:, h, 0:2, :], hp_l[:, h, 0:2, :], h == 0, h == 1)
            ins.then_inc(S["z_vT_ps"], 1)
            pe.wait_ge(S["z_v_copied"], 1)
            for r in range(2):
                for t in range(2):
                    ins = pe.transpose(ps[:, 6, 16 * (2 * r + t):16 * (2 * r + t) + 16],
                                       vrow[:, r, P * t:P * t + P], ident[0:B, 0:B])
            pe.wait_ge(S["z_chain"], Z_ROW_C)
            for j in range(8):
                ins = pe.transpose(ps[:, 6, 64 + 16 * j:80 + 16 * j],
                                   tmpq[:, 2 * j:2 * j + 2, :], ident[0:B, 0:B])
            ins.then_inc(S["z_row_ps"], 1)
            pe.wait_ge(S["z_rT_lo"], 1)
            for j in range(8):
                ins = mm3(ps[0:48, 7, 0:D], qT_h[:, j, 0:48], qT_l[:, j, 0:48], wo_h[:, j, :], wo_l[:, j, :],
                          j == 0, j == 7)
            ins.then_inc(S["z_rows_ps"], 1)
            pe.wait_ge(S["z_vT_lo"], 1)
            for j in range(8):
                if j >= 2:
                    pe.wait_ge(S["z_vw"], j - 1)
                for s in range(2):
                    r = slice(64 * s, 64 * s + 64)
                    ins = mm3(ps[0:NP * B, 2 * (j % 2) + s, 0:D], pT_h[r, j // 4, 0:32], pT_l[r, j // 4, 0:32],
                              wo_h[r, j, :], wo_l[r, j, :], True, True)
                ins.then_inc(S["z_vw_ps"], 1)

            def to_features(b):
                pe.wait_ge(S["xh_ready"], b + 1)
                for h in range(2):
                    ins = pe.transpose(ps[:, A3, P * h:P * h + P], xh[:, P * h:P * h + P], ident)
                ins.then_inc(S["hT_ps"], 1)

            def project(b):
                pe.wait_ge(S["h_lo"], b + 1)
                for bank, lo, n in ((A2, QC, KC + VC), (A0, 0, 512), (A1, 512, 512)):
                    for h in range(2):
                        ins = mm3(ps[:, bank, 0:n], hh[:, h, :], hl[:, h, :], wqkv_h[:, h, lo:lo + n],
                                  wqkv_l[:, h, lo:lo + n], h == 0, h == 1)
                    if bank == A2:
                        ins.then_inc(S["kv_ps"], 1)
                ins.then_inc(S["q_ps"], 1)

            def keys_T(b):
                pe.wait_ge(S["v_lo"], b + 1)
                pe.wait_ge(S["k_rot"], b + 1)
                for t in range(2):
                    ins = pe.transpose(ps[:, A2, P * t:P * t + P], qk[:, H + 2 * t:H + 2 * t + 2, :], ident)
                ins.then_inc(S["kT_ps"], 1)

            def queries_T(b):
                pe.wait_ge(S["q_rot"], b + 1)
                for t in range(2):
                    for j in range(4):
                        p = 8 * t + 2 * j
                        ins = pe.transpose(ps[:, A0 + t, P * j:P * j + P], qk[:, p:p + 2, :], ident)
                    ins.then_inc(S["qT_ps"], 1)

            def scores(b, t):
                if t == 0:
                    pe.wait_ge(S["kT_lo"], b + 1)
                    pe.wait_ge(S["kp_hi"], 2 * b + 2)
                    pe.wait_ge(S["qT_lo"], 2 * b + 2)
                else:
                    pe.wait_ge(S["exp_done"], 2 * b + 1)
                for k in range(3):
                    m = min(3, 8 - 3 * k)
                    pe.matmul(ps[:, A0 + k, 0:m * NK], id16[:], mask16[:, 0:m, :], start=True, stop=False,
                              skip_group_check=True)
                for i in range(8):
                    j, s = 4 * t + i // 2, i % 2
                    o = ps[:, A0 + i // 3, NK * (i % 3):NK * (i % 3) + NK]
                    for a, (q_, k_) in enumerate(((qT_h, kT_h), (qT_h, kT_l), (qT_l, kT_h))):
                        ins = pe.matmul(o, q_[:, j, :], k_[:, t, s, :], start=False, stop=(a == 2),
                                        skip_group_check=True)
                ins.then_inc(S["s_ps"], 1)

            def probs_T(b, t, s):
                n = 4 * b + 2 * t + s
                if s == 0:
                    pe.wait_ge(S["p_ready"], 2 * b + t + 1)
                if t or s:
                    pe.wait_ge(S["pT_lo"], n)
                for j in range(4):
                    ins = pe.transpose(ps[:, A3, P * j:P * j + P], probs[:, 8 * t + 2 * j + s, 0:P], ident)
                ins.then_inc(S["pT_ps"], 1)

            def values(b, t):
                if t:
                    pe.wait_ge(S["oT_lo_r"], 2 * b + 1)
                for s in range(2):
                    pe.wait_ge(S["pT_lo"], 4 * b + 2 * t + s + 1)
                    ins = mm3(ps[:, AO, :], v_h[:, t, s, :], v_l[:, t, s, :], pT_h[:, s, :], pT_l[:, s, :],
                              s == 0, s == 1)
                ins.then_inc(S["o_ps"], 1)

            def pooled_T(b):
                pe.wait_ge(S["p_ready"], 2 * b + 2)
                pe.transpose(ps[0:NP * H, A2, 0:P], pp[:].rearrange("p k h -> p (k h)"), ident
                             ).then_inc(S["pp_ps"], 1)

            def first_tile(b):
                pe.wait_ge(S["row_ld"], 16 * b + 16)
                pe.wait_ge(S["pT_lo"], 4 * b + 4)
                pe.matmul(ps[:, A3, 0:D], tab[0:3, C_SEL:C_SEL + P], rowb[:], start=True, stop=True
                          ).then_inc(S["row_ps"], 1)

            def project_out(b):
                pe.wait_ge(S["oT_lo_r"], 2 * b + 2)
                pe.wait_ge(S["ppT_ready"], b + 1)
                pe.wait_ge(S["vw_ld"], 16 * b + 16)
                pe.matmul(ps[:, AO, 0:D], ppT[:], vwb[:], start=True, stop=False)
                for j in range(8):
                    ins = mm3(ps[:, AO, 0:D], oT_h[:, j, :], oT_l[:, j, :], wo_h[:, j, :], wo_l[:, j, :],
                              False, j == 7)
                ins.then_inc(S["y_ps"], 1)

            def f_features(n, u):
                pe.wait_ge(S["f_xh"], n + 1)
                if not (isinstance(n, int) and n == 0):
                    pe.wait_ge(S["w8_ready"], n)
                for h in range(2):
                    ins = pe.transpose(ps[:, FM, P * h:P * h + P], xh2[:, P * h:P * h + P], ident)
                ins.then_inc(S["f_hT_ps"], 1)

            def f_inner_T(n, u):
                pe.wait_ge(S["mixed_ready"], n + 1)
                if real(n + 2):
                    pe.wait_ge(S["f_hf"], n + 3)
                elif n == NT - 2:
                    pe.wait_ge(S["w8_ready"], NT)
                else:
                    pe.wait_ge(S["x_done"], NT)
                pe.transpose(ps[:, FM, 0:P], mixed[u], ident)
                for h in range(2):
                    ins = pe.transpose(ps[:, FM, P * (h + 1):P * (h + 2)], shared[u][:, P * h:P * h + P], ident)
                ins.then_inc(S["m_ps"], 1)

            def f_logits(n, u):
                pe.wait_ge(S["f_lo"], n + 1)
                if real(n - 2):
                    pe.wait_ge(S["mT_lo_r"], n - 1)
                for h in range(2):
                    ins = mm3(ps[:, FM, 256:384], fh[u][:, h, :], fl[u][:, h, :], wr_h[:, h, :], wr_l[:, h, :],
                              h == 0, h == 1)
                ins.then_inc(S["l_ps"], 1)

            def f_down(n):
                pe.wait_ge(S["mT_lo_r"], n + 1)
                if real(n + 2):
                    pe.wait_ge(S["top_ready"], n + 3)
                for k in range(3):
                    ins = mm3(ps[:, FM, 0:D], mT_h[:, k, :], mT_l[:, k, :], wd_h[:, k, :], wd_l[:, k, :],
                              k == 0, k == 2)
                ins.then_inc(S["d_ps"], 1)

            def f_coefT(n):
                pe.wait_ge(S["coef_ready"], n + 1)
                if real(n - 2):
                    pe.wait_ge(S["x_done"], n)
                pe.transpose(ps[:, FM, 384:512], coef[:], ident).then_inc(S["cT2_ps"], 1)

            def f_weights(n):
                pe.wait_ge(S["cT2_ready"], n + 1)
                pe.matmul(ps[:, FM, 0:NB], coefT[:], mix[:], start=True, stop=True).then_inc(S["w_ps"], 1)

            def f_chunk(n, u, k):
                bank = FR + (k + u) % 2
                pe.wait_ge(S["chunk_done"], NCH * n + k + 1)
                if k == 0:
                    pe.wait_ge(S["f_lo"], n + 1)
                for h in range(2):
                    ins = mm3(ps[:, bank, :], fh[u][:, h, :], fl[u][:, h, :], wgu_h[:, h, k, :],
                              wgu_l[:, h, k, :], h == 0, h == 1)
                ins.then_inc(S["gu_ps"], 1)

            def body(b, attn):
                m0, m1, m2 = 2 * b - 3, 2 * b - 2, 2 * b - 1
                if real(m0):
                    f_chunk(m0, 1, 0)
                if attn:
                    to_features(b)
                if real(m0):
                    f_chunk(m0, 1, 1)
                if real(m1):
                    f_features(m1, 0)
                if attn:
                    project(b)
                if real(m1 - 2):
                    f_inner_T(m1 - 2, 0)
                if real(m1):
                    f_logits(m1, 0)
                if attn:
                    keys_T(b)
                if real(m0):
                    f_chunk(m0, 1, 2)
                if attn:
                    queries_T(b)
                if real(m1 - 2):
                    f_down(m1 - 2)
                if real(m0):
                    f_chunk(m0, 1, 3)
                if attn:
                    scores(b, 0)
                if real(m1):
                    f_coefT(m1)
                if real(m0):
                    f_chunk(m0, 1, 4)
                if real(m1):
                    f_weights(m1)
                    f_chunk(m1, 0, 0)
                if attn:
                    scores(b, 1)
                    probs_T(b, 0, 0)
                if real(m1):
                    f_chunk(m1, 0, 1)
                if attn:
                    probs_T(b, 0, 1)
                if real(m2):
                    f_features(m2, 1)
                if real(m1):
                    f_chunk(m1, 0, 2)
                if attn:
                    values(b, 0)
                    probs_T(b, 1, 0)
                if real(m0):
                    f_inner_T(m0, 1)
                if real(m2):
                    f_logits(m2, 1)
                if real(m1):
                    f_chunk(m1, 0, 3)
                if attn:
                    probs_T(b, 1, 1)
                    pooled_T(b)
                if real(m0):
                    f_down(m0)
                if attn:
                    values(b, 1)
                if real(m2):
                    f_coefT(m2)
                if real(m1):
                    f_chunk(m1, 0, 4)
                if real(m2):
                    f_weights(m2)
                if attn:
                    first_tile(b)
                    project_out(b)

            pe.wait_ge(S["piece_lo"], len(SPLIT))
            pe.wait_ge(S["mask_done"], 1)
            pe.wait_ge(S["mix_done"], 1)
            pe.wait_ge(S["z_zero"], 2)
            body(0, True)
            body(1, True)
            with pe.Fori(2, B) as b:
                body(b, True)
            body(B, False)
            body(B + 1, False)

        @block.scalar
        def _(act):
            act.wait_ge(S["small_ld"], 48)
            act.activation(lsc[:, 1, :], lsc[:, 0, :], ACT.Exp).then_inc(S["lsc_exp"], 1)
            act.wait_ge(S["c_ld"], 16)
            act.activation(c_row[:, 1, :], c_row[:, 0, :], ACT.Tanh, scale=0.5).then_inc(S["silu_t"], 1)
            for n in range(3):
                act.wait_ge(S["mod_ps"], n + 1)
                act.copy(modrow[:, 512 * n:512 * n + 512], ps[0:B, n, :]).then_inc(S["mod_ld"], 1)

            def split(i):
                name = SPLIT[i]
                if name in ("qs", "qg"):
                    act.wait_ge(S["q_scaled"], 1 + ("qs", "qg").index(name))
                else:
                    act.wait_ge(S[f"stage_ld{(i + 3) % 2}"], loads_to(i + 3))
                views = split_views(name, stage[(i + 3) % 2])
                for k, (src, hi, lo) in enumerate(views):
                    ins = act.copy(hi, src)
                    if k == len(views) - 1:
                        ins.then_inc(S["piece_hi"], 1)

            for i in range(5):
                split(i)

            def first_half_keys(i):
                for p in range(2):
                    act.wait_ge(S["a_ps"], 2 * i + p + 1)
                    for h in range(2):
                        ins = act.activation(hf0[p][:, h, :], ps[:, p, P * h:P * h + P], ACT.Identity,
                                             bias=mod_p[p][:, 2 + h:3 + h], scale=mod_p[p][:, h:h + 1])
                    ins.then_inc(S["a_hf"], 1)
                for p in range(2):
                    act.wait_ge(S["a_kps"], 2 * i + p + 1)
                    act.copy(kr0[p].rearrange("p (g e) -> p g e", e=DH)[:, :, 0:32],
                             ps[:, 2 + p, 0:KC].rearrange("p (g e) -> p g e", e=DH)[:, :, 0:32]
                             ).then_inc(S["a_ksem"], 1)

            with act.Fori(0, B // 2) as i:
                first_half_keys(i)
            for i in range(5, len(SPLIT)):
                split(i)

            act.wait_ge(S["z_chain"], Z_MAX)
            act.activation(sm127[:, 2:4, :], sm127[:, 0:2, :], ACT.Exp).then_inc(S["z_exp"], 1)

            def hidden(b):
                act.wait_ge(S["hT_ps"], b + 1)
                for h in range(2):
                    ins = act.activation(hf[:, h, :], ps[:, A3, P * h:P * h + P], ACT.Identity,
                                         bias=mod_a[:, 2 + h:3 + h], scale=mod_a[:, h:h + 1])
                ins.then_inc(S["hf_ready"], 1)

            def semantic_k(b):
                act.wait_ge(S["kv_ps"], b + 1)
                act.copy(qk[:, H:, 0:32], ps[:, A2, 0:KC].rearrange("p (g e) -> p g e", e=DH)[:, :, 0:32])
                v4 = ps[:, A2, KC:KC + VC].rearrange("p (t s e) -> p t s e", t=2, s=2)
                act.copy(v_h[:, :, 0, 0:64], v4[:, :, 0, :])
                act.copy(v_h[:, :, 1, 64:128], v4[:, :, 1, :]).then_inc(S["v_hi"], 1)

            def semantic_q(b):
                act.wait_ge(S["q_ps"], b + 1)
                act.copy(qk[:, 0:H, 0:32], ps[:, A0:A0 + 2, :].rearrange("p a (h e) -> p (a h) e", e=DH)[:, :, 0:32]
                         ).then_inc(S["q_sem"], 1)

            def split_k(b):
                act.wait_ge(S["kT_ps"], b + 1)
                for s in range(2):
                    r = slice(64 * s, 64 * s + 64)
                    ins = act.copy(kT_h[r, :, s, 0:P], ps[r, A2, 0:256].rearrange("p (t k) -> p t k", t=2))
                ins.then_inc(S["kT_hi"], 1)

            def split_q(b):
                for t in range(2):
                    act.wait_ge(S["qT_ps"], 2 * b + t + 1)
                    act.copy(qT_h[:, 4 * t:4 * t + 4, :], ps[:, A0 + t, :].rearrange("p (j k) -> p j k", j=4)
                             ).then_inc(S["qT_hi"], 1)

            def exps(b, t):
                act.wait_ge(S["nmax_ready"], 2 * b + t + 1)
                for i in range(8):
                    ins = act.activation(probs[:, 8 * t + i, :], ps[:, A0 + i // 3, NK * (i % 3):NK * (i % 3) + NK],
                                         ACT.Exp, bias=nmax[:, t, i:i + 1], accum_out=psums[:, t, i:i + 1])
                ins.then_inc(S["exp_done"], 1)

            def split_probs(b, t, s):
                act.wait_ge(S["pT_ps"], 4 * b + 2 * t + s + 1)
                act.copy(pT_h[:, s, :], ps[:, A3, :]).then_inc(S["pT_hi"], 1)

            def split_out(b, t):
                act.wait_ge(S["o_ps"], 2 * b + t + 1)
                act.copy(oT_h[:, 4 * t:4 * t + 4, :], ps[:, AO, :].rearrange("p (j k) -> p j k", j=4)
                         ).then_inc(S["oT_hi_r"], 1)

            def pooled(b):
                act.wait_ge(S["pp_ps"], b + 1)
                act.copy(ppT[:], ps[0:NP * H, A2, 0:P]).then_inc(S["ppT_ready"], 1)

            def f_hidden(n):
                act.wait_ge(S["f_hT_ps"], n + 1)
                for h in range(2):
                    ins = act.activation(hf2[:, h, :], ps[:, FM, P * h:P * h + P], ACT.Identity,
                                         bias=mod_f[:, 2 + h:3 + h], scale=mod_f[:, h:h + 1])
                ins.then_inc(S["f_hf"], 1)

            def f_route(n):
                act.wait_ge(S["nm_ready"], n + 1)
                act.activation(ex[:], lg[:], ACT.Exp, bias=nm[:, 0:1], accum_out=zsum[:]).then_inc(S["ex_ready"], 1)

            def f_coefT(n):
                act.wait_ge(S["cT2_ps"], n + 1)
                act.copy(coefT[:], ps[:, FM, 384:512]).then_inc(S["cT2_ready"], 1)

            def f_tanh(n, u, k):
                act.wait_ge(S["gu_ps"], NCH * n + k + 1)
                act.activation(th[(k + u) % 2], ps[:, FR + (k + u) % 2, 0:256], ACT.Tanh, scale=0.5
                               ).then_inc(S["th_ready"], 1)

            def f_inner(n):
                act.wait_ge(S["m_ps"], n + 1)
                act.copy(mT_h[:], ps[:, FM, 0:384].rearrange("p (k n) -> p k n", k=3)).then_inc(S["mT_hi_r"], 1)

            def body(b, attn):
                m0, m1, m2 = 2 * b - 3, 2 * b - 2, 2 * b - 1
                if real(m0):
                    f_tanh(m0, 1, 0)
                if attn:
                    hidden(b)
                if real(m0):
                    f_tanh(m0, 1, 1)
                if real(m1):
                    f_hidden(m1)
                if attn:
                    semantic_k(b)
                    semantic_q(b)
                if real(m1 - 2):
                    f_inner(m1 - 2)
                if real(m1):
                    f_route(m1)
                if attn:
                    split_k(b)
                if real(m0):
                    f_tanh(m0, 1, 2)
                if attn:
                    split_q(b)
                if real(m0):
                    f_tanh(m0, 1, 3)
                if real(m1):
                    f_coefT(m1)
                if attn:
                    exps(b, 0)
                if real(m0):
                    f_tanh(m0, 1, 4)
                if real(m1):
                    f_tanh(m1, 0, 0)
                if attn:
                    split_probs(b, 0, 0)
                if real(m1):
                    f_tanh(m1, 0, 1)
                if attn:
                    exps(b, 1)
                    split_probs(b, 0, 1)
                if real(m2):
                    f_hidden(m2)
                if real(m1):
                    f_tanh(m1, 0, 2)
                if attn:
                    split_out(b, 0)
                    split_probs(b, 1, 0)
                if real(m0):
                    f_inner(m0)
                if real(m2):
                    f_route(m2)
                if real(m1):
                    f_tanh(m1, 0, 3)
                if attn:
                    split_probs(b, 1, 1)
                    pooled(b)
                    split_out(b, 1)
                if real(m2):
                    f_coefT(m2)
                if real(m1):
                    f_tanh(m1, 0, 4)

            body(0, True)
            body(1, True)
            with act.Fori(2, B) as b:
                body(b, True)
            body(B, False)
            body(B + 1, False)

        @block.vector
        def _(ve):
            cs1, sn1 = tab[:, C_COS1:C_COS1 + 32], tab[:, C_SIN1:C_SIN1 + 32]
            cs0, sn0 = tab[:, C_COS0:C_COS0 + 32], tab[:, C_SIN0:C_SIN0 + 32]

            def carrier(s, value):
                ve.wait_ge(s, value)
                ve.tensor_copy(beat[:, 1:2], beat[:, 0:1])

            def over_heads(ap, n):
                return ap.unsqueeze(1).to_broadcast([ap.shape[0], n, ap.shape[1]])

            def rotate_products(m1, m2, src, cs, sn, n):
                ve.tensor_tensor(m1, src[:, :, 32:64], over_heads(cs, n), ALU.mult)
                ve.tensor_tensor(m2[:, :, 0:16], src[:, :, 48:64], over_heads(sn[:, 0:16], n), ALU.mult)
                return ve.tensor_tensor(m2[:, :, 16:32], src[:, :, 32:48], over_heads(sn[:, 16:32], n), ALU.mult)

            ve.wait_ge(S["silu_t"], 1)
            ve.scalar_tensor_tensor(c_row[:, 1, :], c_row[:, 1, :], 1.0, c_row[:, 0, :], ALU.add, ALU.mult
                                    ).then_inc(S["silu_a"], 1)
            ve.wait_ge(S["silu_a"], 1)
            ve.tensor_scalar(c_row[:, 2, :], c_row[:, 1, :], 0.5, None, ALU.mult).then_inc(S["silu_row"], 1)
            ve.wait_ge(S["cT_ps"], 1)
            ve.tensor_copy(cT[:], ps[:, AO, 0:32].rearrange("p (h b) -> p h b", h=2)).then_inc(S["cT_copied"], 1)
            ve.wait_ge(S["mask_ld"], 16)
            ve.tensor_copy(mask16[:], mask_f.rearrange("p (a k) -> p a k", a=3))
            ve.wait_ge(S["tab_ld"], 16)
            ve.tensor_copy(id16[:], ident).then_inc(S["mask_done"], 1)
            ve.memset(take[:], TAKEN)
            ve.memset(beat[:], 0.0)
            ve.memset(den[:], 0.0).then_inc(S["chunk_done"], 2)
            ve.memset(rn[:], 0.0).then_inc(S["x_done"], 1)
            ve.wait_ge(S["lsc_exp"], 1)
            ve.tensor_scalar(lsc[:, 0, :], lsc[:, 1, :], 32.0 ** -0.5, None, ALU.mult).then_inc(S["lsc_done"], 1)
            ve.wait_ge(S["small_ld"], 48)
            ve.tensor_tensor(amp[:], amp[:], amp[:], ALU.mult).then_inc(S["amp_d"], 1)
            ve.wait_ge(S["amp_d"], 1)
            ve.tensor_tensor(ampp[:], amp[:, :, 0], amp[:, :, 1], ALU.add).then_inc(S["amp_d"], 1)
            ve.wait_ge(S["amp_d"], 2)
            ve.tensor_reduce(amps[:, 0:1], ampp[:], X, ALU.add).then_inc(S["amp_d"], 1)
            ve.wait_ge(S["amp_d"], 3)
            ve.tensor_scalar(amps[:, 1:2], amps[:, 0:1], EPS, None, ALU.add).then_inc(S["amp_d"], 1)
            ve.wait_ge(S["amp_d"], 4)
            ve.reciprocal(amps[:, 3:4], amps[:, 1:2]).then_inc(S["amp_d"], 1)
            ve.wait_ge(S["amp_d"], 5)
            ve.tensor_scalar(mix[:], ampp[:], amps[:, 3:4], amps[:, 2:3], ALU.mult, ALU.mult
                             ).then_inc(S["mix_done"], 1)
            ve.wait_ge(S["mod_ld"], 3)
            gates = modrow.rearrange("p (a k d) -> p a k d", a=2, k=3)[:, :, 2, :]
            ups = modrow.rearrange("p (a k d) -> p a k d", a=2, k=3)[:, :, 1, :]
            g_sign, g_neg = upd[0:B], prod[0:B, 0:2, :]
            ve.tensor_scalar(ups, ups, 1.0, None, ALU.add).then_inc(S["modrow_done"], 4)
            ve.wait_ge(S["mask_done"], 1)
            ve.tensor_scalar(g_sign, gates, 0.0, 2.0, ALU.is_ge, ALU.mult).then_inc(S["gate_fix"], 1)
            ve.wait_ge(S["gate_fix"], 1)
            ve.tensor_scalar(g_neg, gates, -1.0, None, ALU.mult).then_inc(S["gate_fix"], 1)
            ve.wait_ge(S["gate_fix"], 2)
            ve.tensor_tensor(gates, gates, g_neg, ALU.max).then_inc(S["gate_fix"], 1)
            ve.wait_ge(S["gate_fix"], 3)
            ve.tensor_scalar(gates, gates, 0.25, None, ALU.max).then_inc(S["gate_fix"], 1)
            ve.wait_ge(S["gate_fix"], 4)
            ve.scalar_tensor_tensor(gates, g_sign, -1.0, gates, ALU.add, ALU.mult).then_inc(S["gate_fix"], 1)
            ve.wait_ge(S["modT_ps"], 1)
            ve.tensor_copy(modT[:], ps[:, AO, 32:160].rearrange("p (k b) -> p b k", k=8)).then_inc(S["modT_done"], 1)
            for q in range(2):
                ve.wait_ge(S[f"x_ld{q}"], 16)
            for q in range(2, 4):
                ve.wait_ge(S[f"x_ld{q}"], 16)
            with ve.Fori(0, NT // 4) as i:
                for u in range(4):
                    ins = ve.bn_stats(bst4[:, u, :], x[:, 4 * i + u, :])
                ins.then_inc(S["bn1"], 1)
                carrier(S["bn1"], i + 1)
                for u in range(4):
                    ins = ve.bn_aggr(mv4[:, u, :], bst4[:, u, :])
                ins.then_inc(S["aggr1"], 1)
                ve.wait_ge(S["aggr1"], i + 1)
                ve.tensor_scalar(st[:, bass.ds(4 * i, 4), :], mv4[:], 1.0, None, ALU.mult).then_inc(S["stats_done"], 1)
            ve.wait_ge(S["lsc_done"], 1)
            for n, name in enumerate(("qs", "qg")):
                i = PIECES.index(name)
                ve.wait_ge(S[f"stage_ld{i % 2}"], loads_to(i))
                for h in range(2):
                    w = halves(stage[i % 2])[:, h, :].rearrange("p (h e) -> p h e", e=32)
                    ins = ve.tensor_tensor(w, w, lsc[:, 0, :].unsqueeze(2).to_broadcast([P, H, 32]), ALU.mult)
                ins.then_inc(S["q_scaled"], 1)
            zero = early[:, 2300:2560]
            ve.memset(zero, 0.0).then_inc(S["z_zero"], 1)
            ve.wait_ge(S["z_zero"], 1)
            for k in (kT_h, kT_l):
                for s in range(2):
                    r = slice(64 - 64 * s, 128 - 64 * s)
                    ve.tensor_copy(k[r, :, s, :], zero[r].rearrange("p (t k) -> p t k", t=2))
            for v in (v_h, v_l):
                for s in range(2):
                    c = slice(64 - 64 * s, 128 - 64 * s)
                    ins = ve.tensor_copy(v[:, :, s, c], zero[:, 0:P].rearrange("p (t e) -> p t e", t=2))
            ins.then_inc(S["z_zero"], 1)

            ve.wait_ge(S["rs_done"], 1)
            ve.wait_ge(S["modT_done"], 1)
            ve.wait_ge(S["gates_st"], 32)
            with ve.Fori(0, B // 2) as i:
                for p in range(2):
                    b = 2 * i + p
                    ve.tensor_copy(mod_p[p][:], modT[:, b, 0:4])
                    for u, dst in ((0, xh0[p]), (1, xh1[p])):
                        ins = ve.tensor_scalar(dst, x[:, 2 * b + u, :], st[:, 2 * b + u, 0:1], rs1[:, bass.ds(2 * b + u, 1)],
                                               ALU.subtract, ALU.mult)
                    ins.then_inc(S["a_xh"], 1)
                for p in range(2):
                    b = 2 * i + p
                    ve.wait_ge(S["a_hf"], b + 1)
                    ve.tensor_copy(h0h[p][:], hf0[p][:]).then_inc(S["a_hi"], 1)
                    for h in range(2):
                        ins = ve.tensor_scalar(hpool[:, h, :, b], ps[:, p, 256 + 4 * h:260 + 4 * h],
                                               mod_p[p][:, h:h + 1], mod_p[p][:, 2 + h:3 + h], ALU.mult, ALU.add)
                    ins.then_inc(S["a_hp"], 1)
                    ve.wait_ge(S["a_hi"], b + 1)
                    ve.tensor_tensor(h0l[p][:], hf0[p][:], h0h[p][:].bitcast(F32), ALU.subtract
                                     ).then_inc(S["a_lo"], 1)
                for p in range(2):
                    b = 2 * i + p
                    ve.wait_ge(S["a_ksem"], b + 1)
                    src = ps[:, 2 + p, 0:KC].rearrange("p (g e) -> p g e", e=DH)
                    rotate_products(rk1[p], rk2[p], src, cs0, sn0, HKV).then_inc(S["a_km"], 1)
                for p in range(2):
                    b = 2 * i + p
                    ve.wait_ge(S["a_km"], b + 1)
                    ve.tensor_tensor(kr0[p].rearrange("p (g e) -> p g e", e=DH)[:, :, 32:64], rk1[p], rk2[p],
                                     ALU.add).then_inc(S["a_krot"], 1)
                for p in range(2):
                    b = 2 * i + p
                    ve.wait_ge(S["a_kp_ps"], b + 1)
                    ve.tensor_scalar(kpool[:, b], ps[:, 4 + p, 0:4].rearrange("p (t k) -> p t k", t=2), 1.0, None,
                                     ALU.mult).then_inc(S["a_kp"], 1)

            ve.wait_ge(S["a_hp"], B)
            ve.tensor_copy(hp_h[:], hpool[:]).then_inc(S["hp_hi"], 1)
            ve.wait_ge(S["hp_hi"], 1)
            ve.tensor_tensor(hp_l[:], hpool[:], hp_h[:].bitcast(F32), ALU.subtract).then_inc(S["hp_lo"], 1)
            ve.wait_ge(S["z_v_ps"], 1)
            ve.wait_ge(S["piece_lo"], len(SPLIT))
            ve.tensor_copy(vrow, ps[0:B, 0:2, :].rearrange("p a n -> p (a n)")[:, 0:768]
                           .rearrange("p (r n) -> p r n", r=3)).then_inc(S["z_v_copied"], 1)
            csl = tab[0:B, C_COSL:C_COSL + 32]
            snl = tab[0:B, C_SINL:C_SINL + 32]
            z = [0]

            def link(ins):
                z[0] += 1
                ins.then_inc(S["z_chain"], 1)
                ve.wait_ge(S["z_chain"], z[0])

            ve.wait_ge(S["z_q_ps"], 1)
            q_ps = ps[0:B, 2:4, :].rearrange("p a (h e) -> p (a h) e", e=DH)
            ve.tensor_copy(q127[:, :, 0:32], q_ps[:, :, 0:32])
            link(rotate_products(dots[:, :, 0:32], dots[:, :, 32:64], q_ps, csl, snl, H))
            ve.tensor_tensor(q127[:, :, 32:64], dots[:, :, 0:32], dots[:, :, 32:64], ALU.add)
            ve.wait_ge(S["z_kp_ps"], 1)
            ins = ve.tensor_copy(kprow, ps[0:B, 4, :].rearrange("p (k n) -> p k n", k=NP))
            link(ins)
            for k in range(NP):
                for t in range(2):
                    kk = kprow[:, k, P * t:P * t + P].unsqueeze(1).to_broadcast([B, 4, P])
                    q4 = q127[:, 8 * t:8 * t + 8, :].rearrange("p (j s) e -> p j (s e)", j=4)
                    d4 = dots[:, 8 * t:8 * t + 8, :].rearrange("p (j s) e -> p j (s e)", j=4)
                    ins = ve.tensor_tensor(d4, q4, kk, ALU.mult)
                link(ins)
                link(ve.tensor_reduce(s127[:, k, :], dots, X, ALU.add))
            link(ve.tensor_tensor(sm127[:, 4, :], s127[:, 0, :], s127[:, 1, :], ALU.max))
            for k in range(NP):
                ins = ve.tensor_tensor(sm127[:, k, :], s127[:, k, :], sm127[:, 4, :], ALU.subtract)
            link(ins)
            assert z[0] == Z_MAX
            ve.wait_ge(S["z_exp"], 1)
            link(ve.tensor_tensor(sm127[:, 4, :], sm127[:, 2, :], sm127[:, 3, :], ALU.add))
            link(ve.reciprocal(sm127[:, 5, :], sm127[:, 4, :]))
            for k in range(NP):
                ins = ve.tensor_tensor(s127[:, k, :], sm127[:, 2 + k, :], sm127[:, 5, :], ALU.mult)
            link(ins)
            for k in range(NP):
                for t in range(2):
                    dst = (dots, tmpq)[k][:, 8 * t:8 * t + 8, :]
                    vv = vrow[:, 1 + k, P * t:P * t + P].unsqueeze(1).to_broadcast([B, 4, P])
                    pp = s127[:, k, 8 * t:8 * t + 8].unsqueeze(2).to_broadcast([B, 8, DH])
                    link(ve.tensor_copy(dst.rearrange("p (j s) e -> p j (s e)", j=4), vv))
                    ins = ve.tensor_tensor(dst, dst, pp, ALU.mult)
            link(ins)
            link(ve.tensor_tensor(tmpq, tmpq, dots, ALU.add))
            assert z[0] == Z_ROW_C
            ve.wait_ge(S["z_vT_ps"], 1)
            ve.tensor_copy(vTf[:], ps[:, 5, 0:64].rearrange("p (t n) -> p t n", t=2)).then_inc(S["z_vT"], 1)
            ve.wait_ge(S["z_vT"], 1)
            ve.tensor_copy(pT_h[:, :, 0:32], vTf[:]).then_inc(S["z_vT_hi"], 1)
            ve.wait_ge(S["z_vT_hi"], 1)
            ve.tensor_tensor(pT_l[:, :, 0:32], vTf[:], pT_h[:, :, 0:32].bitcast(F32), ALU.subtract
                             ).then_inc(S["z_vT_lo"], 1)
            ve.wait_ge(S["z_row_ps"], 1)
            for r in range(2):
                for t in range(2):
                    ve.tensor_copy(rT[:, 4 * t:4 * t + 4, r, :], ps[:, 6, 16 * (2 * r + t):16 * (2 * r + t) + 16]
                                   .unsqueeze(1).to_broadcast([P, 4, B]))
            ve.tensor_copy(rT[:, :, 2, :], ps[:, 6, 64:192].rearrange("p (j b) -> p j b", j=8)
                           ).then_inc(S["z_rT"], 1)
            ve.wait_ge(S["z_rT"], 1)
            rT2 = rT.rearrange("p j r b -> p j (r b)")
            ve.tensor_copy(qT_h[:, :, 0:48], rT2).then_inc(S["z_rT_hi"], 1)
            ve.wait_ge(S["z_rT_hi"], 1)
            ve.tensor_tensor(qT_l[:, :, 0:48], rT2, qT_h[:, :, 0:48].bitcast(F32), ALU.subtract
                             ).then_inc(S["z_rT_lo"], 1)
            ve.wait_ge(S["z_rows_ps"], 1)
            ve.tensor_copy(rows_sb, ps[0:48, 7, 0:D]).then_inc(S["z_rows"], 1)
            for j in range(8):
                ve.wait_ge(S["z_vw_ps"], j + 1)
                if j == 4:
                    ve.wait_ge(S["z_vw_st"], 32)
                for s in range(2):
                    ins = ve.tensor_copy(vws[:, (2 * j + s) % 8, :], ps[0:NP * B, 2 * (j % 2) + s, 0:D])
                ins.then_inc(S["z_vw"], 1)
            ve.wait_ge(S["z_vw_st"], 64)
            ve.wait_ge(S["z_rows_st"], 16)

            def normed(b):
                ve.tensor_scalar(mod_a[:], modT[:, b, 0:4], 1.0, None, ALU.mult)
                ve.tensor_scalar(xh[:], x[:, 2 * b + 1, :], st[:, 2 * b + 1, 0:1], rs1[:, bass.ds(2 * b + 1, 1)],
                                 ALU.subtract, ALU.mult).then_inc(S["xh_ready"], 1)
                for s in range(2):
                    r = slice(64 * s, 64 * s + 64)
                    ins = ve.tensor_scalar(kT_h[r, :, s, P:NK], kpool[r, b], 1.0, None, ALU.mult)
                ins.then_inc(S["kp_hi"], 1)
                ve.wait_ge(S["kp_hi"], 2 * b + 1)
                for s in range(2):
                    r = slice(64 * s, 64 * s + 64)
                    ins = ve.tensor_tensor(kT_l[r, :, s, P:NK], kpool[r, b], kT_h[r, :, s, P:NK].bitcast(F32),
                                           ALU.subtract)
                ins.then_inc(S["kp_hi"], 1)

            def split_h(b):
                ve.wait_ge(S["hf_ready"], b + 1)
                ve.tensor_copy(hh[:], hf[:]).then_inc(S["h_hi"], 1)
                ve.wait_ge(S["h_hi"], b + 1)
                ve.tensor_tensor(hl[:], hf[:], hh[:].bitcast(F32), ALU.subtract).then_inc(S["h_lo"], 1)

            def rotate_k(b):
                ve.wait_ge(S["v_hi"], b + 1)
                rotate_products(rot1[:, H:], rot2[:, H:], ps[:, A2, 0:KC].rearrange("p (g e) -> p g e", e=DH),
                                cs1, sn1, HKV).then_inc(S["k_m"], 1)
                v4 = ps[:, A2, KC:KC + VC].rearrange("p (t s e) -> p t s e", t=2, s=2)
                ve.tensor_tensor(v_l[:, :, 0, 0:64], v4[:, :, 0, :], v_h[:, :, 0, 0:64].bitcast(F32), ALU.subtract)
                ve.tensor_tensor(v_l[:, :, 1, 64:128], v4[:, :, 1, :], v_h[:, :, 1, 64:128].bitcast(F32),
                                 ALU.subtract).then_inc(S["v_lo"], 1)

            def rotate_q(b):
                ve.wait_ge(S["q_sem"], b + 1)
                rotate_products(rot1[:, 0:H], rot2[:, 0:H],
                                ps[:, A0:A0 + 2, :].rearrange("p a (h e) -> p (a h) e", e=DH),
                                cs1, sn1, H).then_inc(S["q_m"], 1)

            def split_k(b):
                ve.wait_ge(S["kT_hi"], b + 1)
                for s in range(2):
                    r = slice(64 * s, 64 * s + 64)
                    ins = ve.tensor_tensor(kT_l[r, :, s, 0:P], ps[r, A2, 0:256].rearrange("p (t k) -> p t k", t=2),
                                           kT_h[r, :, s, 0:P].bitcast(F32), ALU.subtract)
                ins.then_inc(S["kT_lo"], 1)

            def split_q(b):
                for t in range(2):
                    ve.wait_ge(S["qT_hi"], 2 * b + t + 1)
                    ve.tensor_tensor(qT_l[:, 4 * t:4 * t + 4, :], ps[:, A0 + t, :].rearrange("p (j k) -> p j k", j=4),
                                     qT_h[:, 4 * t:4 * t + 4, :].bitcast(F32), ALU.subtract
                                     ).then_inc(S["qT_lo"], 1)

            def maxima(b, t):
                ve.wait_ge(S["s_ps"], 2 * b + t + 1)
                s6 = ps[:, A0:A0 + 2, 0:3 * NK].rearrange("p a (h k) -> p a h k", k=NK)
                ve.tensor_reduce(nmax[:, t, 0:6], s6, X, ALU.max, negate=True)
                s2 = ps[:, A2, 0:2 * NK].rearrange("p (h k) -> p h k", k=NK)
                ve.tensor_reduce(nmax[:, t, 6:8], s2, X, ALU.max, negate=True).then_inc(S["nmax_ready"], 1)

            def inverse_sums(b, t):
                ve.wait_ge(S["exp_done"], 2 * b + t + 1)
                ve.reciprocal(rinv[:, t, :], psums[:, t, :]).then_inc(S["rinv_ready"], 1)

            def split_probs(b, t, s):
                ve.wait_ge(S["pT_hi"], 4 * b + 2 * t + s + 1)
                ve.tensor_tensor(pT_l[:, s, :], ps[:, A3, :], pT_h[:, s, :].bitcast(F32), ALU.subtract
                                 ).then_inc(S["pT_lo"], 1)

            def split_out(b, t):
                ve.wait_ge(S["oT_hi_r"], 2 * b + t + 1)
                ve.tensor_tensor(oT_l[:, 4 * t:4 * t + 4, :], ps[:, AO, :].rearrange("p (j k) -> p j k", j=4),
                                 oT_h[:, 4 * t:4 * t + 4, :].bitcast(F32), ALU.subtract
                                 ).then_inc(S["oT_lo_r"], 1)

            def add_attention(b):
                ve.wait_ge(S["gate_a_ld"], 16 * b + 16)
                ve.wait_ge(S["row_ps"], b + 1)
                ve.tensor_tensor(upd[:, 0, :], ps[:, A3, 0:D], gate_a[:], ALU.mult).then_inc(S["upd_ready"], 1)
                ve.wait_ge(S["upd_ready"], 2 * b + 1)
                ve.tensor_tensor(x[:, 2 * b, :], x[:, 2 * b, :], upd[:, 0, :], ALU.add)
                ve.wait_ge(S["y_ps"], b + 1)
                ve.tensor_tensor(upd[:, 1, :], ps[:, AO, 0:D], gate_a[:], ALU.mult).then_inc(S["upd_ready"], 1)
                ve.wait_ge(S["upd_ready"], 2 * b + 2)
                ve.tensor_tensor(x[:, 2 * b + 1, :], x[:, 2 * b + 1, :], upd[:, 1, :], ALU.add
                                 ).then_inc(S["x_mid"], 1)

            def f_norm(n, f, u):
                if u == 0:
                    ve.wait_ge(S["x_mid"], f + 1)
                    ve.tensor_scalar(mod_f[:], modT[:, f, 4:8], 1.0, None, ALU.mult)
                ve.bn_stats(bst[:], x[:, n, :]).then_inc(S["f_bn"], 1)
                carrier(S["f_bn"], n + 1)
                ve.bn_aggr(mv[:], bst[:]).then_inc(S["f_var"], 1)
                ve.wait_ge(S["f_rs"], n + 1)
                ve.wait_ge(S["f_var"], n + 1)
                ve.tensor_scalar(xh2, x[:, n, :], mv[:, 0:1], rs2[:, 0:1], ALU.subtract, ALU.mult
                                 ).then_inc(S["f_xh"], 1)

            def f_split(n, u):
                ve.wait_ge(S["f_hf"], n + 1)
                ve.tensor_copy(fh[u][:], hf2).then_inc(S["f_hi"], 1)
                ve.wait_ge(S["f_hi"], n + 1)
                ve.tensor_tensor(fl[u][:], hf2, fh[u][:].bitcast(F32), ALU.subtract).then_inc(S["f_lo"], 1)

            def f_top4(n):
                ve.wait_ge(S["l_ps"], n + 1)
                ve.tensor_copy(lg[:], ps[:, FM, 256:384]).then_inc(S["lg_ready"], 1)
                ve.max(top8[:], ps[:, FM, 256:384]).then_inc(S["top_ready"], 1)
                ve.wait_ge(S["top_ready"], n + 1)
                ve.tensor_copy(take[:, 0:4], top8[:, 0:4]).then_inc(S["take_ready"], 1)
                ve.wait_ge(S["take_ready"], n + 1)
                ve.tensor_scalar(nm[:], top8[:, 0:1], -1.0, None, ALU.mult).then_inc(S["nm_ready"], 1)
                ve.match_replace(rest[:], take[:], lg[:], TAKEN).then_inc(S["rest_ready"], 1)
                ve.wait_ge(S["rest_ready"], n + 1)
                ve.wait_ge(S["ex_ready"], n + 1)
                ve.scalar_tensor_tensor(coef[:], rest[:], 0.999 * TAKEN, ex[:], ALU.is_le, ALU.mult,
                                        accum_out=s4[:]).then_inc(S["coef_ready"], 1)
                ve.wait_ge(S["coef_ready"], n + 1)
                ve.scalar_tensor_tensor(den[:, 0:1], zsum[:], EPS, s4[:], ALU.mult, ALU.add
                                        ).then_inc(S["den_ready"], 1)
                ve.wait_ge(S["den_ready"], n + 1)
                ve.reciprocal(den[:, 1:2], den[:, 0:1]).then_inc(S["rcp_ready"], 1)
                ve.wait_ge(S["rcp_ready"], n + 1)

            def f_weights(n, u):
                ve.wait_ge(S["w_ps"], n + 1)
                ve.tensor_scalar(w8[u][:], ps[:, FM, 0:NB], den[:, 1:2], 0.5, ALU.mult, ALU.mult
                                 ).then_inc(S["w8_ready"], 1)

            def f_chunk(n, u, k):
                r = (k + u) % 2
                ve.wait_ge(S["th_ready"], NCH * n + k + 1)
                bank = ps[:, FR + r, :]
                ve.scalar_tensor_tensor(act_g[r], th[r], 1.0, bank[:, 0:256], ALU.add, ALU.mult
                                        ).then_inc(S["ag_ready"], 1)
                ve.wait_ge(S["ag_ready"], NCH * n + k + 1)
                if k == 0:
                    ve.scalar_tensor_tensor(shared[u][:], act_g[r], 0.5, bank[:, 256:512], ALU.mult, ALU.mult
                                            ).then_inc(S["chunk_done"], 1)
                    return
                if k == 1:
                    ve.wait_ge(S["w8_ready"], n + 1)
                if not (isinstance(n, int) and n == 0):
                    ve.wait_ge(S["mix_sum"], 3 * n - 3 + max(1, k - 1))
                for i in range(2):
                    ins = ve.scalar_tensor_tensor(prod[:, k - 1, P * i:P * i + P], act_g[r][:, P * i:P * i + P],
                                                  w8[u][:, 2 * (k - 1) + i:2 * (k - 1) + i + 1],
                                                  bank[:, 256 + P * i:256 + P * i + P], ALU.mult, ALU.mult)
                ins.then_inc(S["chunk_done"], 1)

            def f_inner(n):
                ve.wait_ge(S["mT_hi_r"], n + 1)
                ve.tensor_tensor(mT_l[:], ps[:, FM, 0:384].rearrange("p (k n) -> p k n", k=3),
                                 mT_h[:].bitcast(F32), ALU.subtract).then_inc(S["mT_lo_r"], 1)

            def f_add(n, f, u):
                ve.wait_ge(S["d_ps"], n + 1)
                if u == 0:
                    ve.wait_ge(S["gate_f_ld"], 16 * f + 16)
                ve.tensor_tensor(updf[:], ps[:, FM, 0:D], gate_f[:], ALU.mult).then_inc(S["updf_ready"], 1)
                ve.wait_ge(S["updf_ready"], n + 1)
                ve.tensor_tensor(x[:, n, :], x[:, n, :], updf[:], ALU.add).then_inc(S["x_done"], 1)

            def body(b, attn):
                m0, m1, m2 = 2 * b - 3, 2 * b - 2, 2 * b - 1
                if attn:
                    normed(b)
                if real(m0):
                    f_chunk(m0, 1, 0)
                if attn:
                    split_h(b)
                if real(m1):
                    f_norm(m1, b - 1, 0)
                if real(m0):
                    f_chunk(m0, 1, 1)
                if real(m1):
                    f_split(m1, 0)
                if attn:
                    rotate_k(b)
                    rotate_q(b)
                if real(m1 - 2):
                    f_inner(m1 - 2)
                if real(m1):
                    f_top4(m1)
                if attn:
                    split_k(b)
                if real(m0):
                    f_chunk(m0, 1, 2)
                if attn:
                    split_q(b)
                if real(m1 - 2):
                    f_add(m1 - 2, b - 2, 0)
                if real(m0):
                    f_chunk(m0, 1, 3)
                if attn:
                    maxima(b, 0)
                if real(m0):
                    f_chunk(m0, 1, 4)
                if real(m1):
                    f_weights(m1, 0)
                if attn:
                    inverse_sums(b, 0)
                if real(m1):
                    f_chunk(m1, 0, 0)
                if attn:
                    maxima(b, 1)
                    split_probs(b, 0, 0)
                if real(m2):
                    f_norm(m2, b - 1, 1)
                if real(m1):
                    f_chunk(m1, 0, 1)
                if attn:
                    inverse_sums(b, 1)
                    split_probs(b, 0, 1)
                if real(m2):
                    f_split(m2, 1)
                if real(m1):
                    f_chunk(m1, 0, 2)
                if attn:
                    split_out(b, 0)
                    split_probs(b, 1, 0)
                if real(m0):
                    f_inner(m0)
                if real(m2):
                    f_top4(m2)
                if real(m1):
                    f_chunk(m1, 0, 3)
                if attn:
                    split_probs(b, 1, 1)
                if real(m0):
                    f_add(m0, b - 2, 1)
                if attn:
                    split_out(b, 1)
                if real(m1):
                    f_chunk(m1, 0, 4)
                if real(m2):
                    f_weights(m2, 1)
                if attn:
                    add_attention(b)

            body(0, True)
            body(1, True)
            with ve.Fori(2, B) as b:
                body(b, True)
            body(B, False)
            body(B + 1, False)


JH_ = H // HKV
Z_MAX = 8
Z_ROW_C = 17


_INS = ['L0_attn_x', 'L0_attn_Wq_sem', 'L0_attn_Wk_sem', 'L0_attn_Wq_geo', 'L0_attn_Wk_geo', 'L0_attn_Wv',
        'L0_attn_Wo', 'L0_attn_logit_scale', 'L0_ffn_w_router', 'L0_ffn_w_gate', 'L0_ffn_w_up', 'L0_ffn_w_down',
        'L0_ffn_amplitudes', 'L0_ffn_expert_scale', 'L0_ffn_shared_w_gate', 'L0_ffn_shared_w_up',
        'L0_ffn_shared_w_down', 'L0_c', 'L0_wmod']


def constants():
    import numpy as np

    tab = np.zeros((P, NTAB), np.float32)
    tab[:, C_ID:C_ID + P] = np.eye(P)
    freq = (1.0 / np.float32(10000.0) ** (np.arange(0, 32, 2, dtype=np.float32) / np.float32(32))).astype(np.float32)

    def rotary(pos, c, s):
        ang = (pos.astype(np.float32)[:, None] * freq).astype(np.float32)
        tab[:, c:c + 32] = np.concatenate([np.cos(ang), np.cos(ang)], 1)
        tab[:, s:s + 32] = np.concatenate([-np.sin(ang), np.sin(ang)], 1)

    rotary(np.arange(P, 2 * P), C_COS1, C_SIN1)
    rotary(np.arange(P), C_COS0, C_SIN0)
    rotary(np.full(P, P - 1), C_COSL, C_SINL)
    tab[0:64, C_POOL0] = 1.0 / 64
    tab[64:P, C_POOL0 + 1] = 1.0 / 64
    tab[P - 1, C_POOL0 + 2] = 1.0
    tab[:, C_POOL0 + 3] = 1.0 / (64 * NK)
    tab[:, C_POOL1 + 3] = 1.0 / NK
    tab[0, C_SEL:C_SEL + 63] = 1.0
    tab[1, C_SEL + 63:C_SEL + P - 1] = 1.0
    tab[2, C_SEL + P - 1] = 1.0
    mask = np.zeros((P, 3, NK), np.float32)
    mask[:, :, 0:P] = np.where(np.arange(P)[None, :] <= np.arange(P)[:, None], 0.0, HIDE)[:, None, :]
    return tab, mask.reshape(P, 3 * NK)


def kernel(**inputs):
    import numpy as np
    import concourse.bacc as bacc
    from concourse.bass_utils import run_bass_kernel_spmd

    nc = bacc.Bacc("TRN2", target_bir_lowering=False, num_devices=1)
    tab, mask = constants()
    arrays, args = {}, []
    named = [(n, np.ascontiguousarray(inputs[n])) for n in _INS] + [("table", tab), ("mask", mask)]
    for name, a in named:
        arrays[f"in_{name}_dram"] = a
        args.append(nc.dram_tensor(f"in_{name}_dram", a.shape, mybir.dt.from_np(a.dtype), kind="ExternalInput").ap())
    args.append(nc.dram_tensor("out_0_dram", (B, T, D), F32, kind="ExternalOutput").ap())
    build(nc, *args)
    r = run_bass_kernel_spmd(nc, [arrays], core_ids=[0])
    return r.results[0]["out_0_dram"]
```

```python
from contextlib import ExitStack

import concourse.bass as bass
from concourse import mybir

ALU = mybir.AluOpType
ACT = mybir.ActivationFunctionType
F32 = mybir.dt.float32
F32R = mybir.dt.float32r
BF16 = mybir.dt.bfloat16
X = mybir.AxisListType.X

P = 128
B, T, D = 16, 256, 256
NT = B * T // P
H, HKV, DH = 16, 4, 64
NP = 2
NK = P + NP
QC, KC, VC = H * DH, HKV * DH, HKV * DH
QKV = QC + KC + VC
NE, NB = 128, 8
NCH = 5
LN_EPS, EPS = 1e-5, 1e-8
HIDE = -float(2 ** 30)
TAKEN = -3.0e38

C_ID = 0
C_COS1 = C_ID + P
C_SIN1 = C_COS1 + 32
C_COS0 = C_SIN1 + 32
C_SIN0 = C_COS0 + 32
C_COSL = C_SIN0 + 32
C_SINL = C_COSL + 32
C_POOL0 = C_SINL + 32
C_POOL1 = C_POOL0 + 4
C_SEL = C_POOL1 + 4
NTAB = C_SEL + P

A0, A1, A2, A3, AO, FM, FR = 0, 1, 2, 3, 4, 5, 6


def build(nc, x_in, wq_sem, wk_sem, wq_geo, wk_geo, wv, wo, logit_scale, w_router, w_gate, w_up,
          w_down, amplitudes, expert_scale, sw_gate, sw_up, sw_down, c_in, wmod, table, mask_in, out):
    gates_dram = nc.dram_tensor("gates", [B, 2, D], F32, kind="Internal").ap()
    rows_dram = nc.dram_tensor("rows", [3, B, D], F32, kind="Internal").ap()
    vw_dram = nc.dram_tensor("vw", [B, NP, H, D], F32, kind="Internal").ap()

    with ExitStack() as ctx:
        def sb(name, shape, dt=F32):
            return ctx.enter_context(nc.sbuf_tensor(name, shape, dt))

        def sem(name):
            return ctx.enter_context(nc.semaphore(name))

        ps = ctx.enter_context(nc.psum_tensor("ps", [P, 8, 512], F32))

        tab = sb("tab", [P, NTAB])
        ident = tab[:, C_ID:C_ID + P]
        pool0, pool1 = tab[:, C_POOL0:C_POOL0 + 4], tab[:, C_POOL1:C_POOL1 + 4]
        x = sb("x", [P, NT, D])
        st = sb("st", [P, NT, 2])
        rs1 = sb("rs1", [P, NT])
        modT = sb("modT", [P, B, 8])
        wqkv_h = sb("wqkv_h", [P, 2, QKV], F32R)
        wqkv_l = sb("wqkv_l", [P, 2, QKV], F32R)
        wo_h = sb("wo_h", [P, 8, D], F32R)
        wo_l = sb("wo_l", [P, 8, D], F32R)
        wgu_h = sb("wgu_h", [P, 2, NCH, 512], F32R)
        wgu_l = sb("wgu_l", [P, 2, NCH, 512], F32R)
        wr_h = sb("wr_h", [P, 2, NE], F32R)
        wr_l = sb("wr_l", [P, 2, NE], F32R)
        wd_h = sb("wd_h", [P, 3, D], F32R)
        wd_l = sb("wd_l", [P, 3, D], F32R)
        mix = sb("mix", [P, NB])
        kpool = sb("kpool", [P, B, 2, NP])
        kpz_h = sb("kpz_h", [P, B, 2, 2, NP], F32R)
        kpz_l = sb("kpz_l", [P, B, 2, 2, NP], F32R)
        id16 = sb("id16", [P, P], BF16)
        mask16 = sb("mask16", [P, 2, NK], BF16)
        mhalf = sb("mhalf", [P, NT])

        probs = sb("probs", [P, H, NK])
        early = sb("early", [P, 1920])
        qk = early[:, 0:QC + KC].rearrange("p (h e) -> p h e", e=DH)
        rot1 = qk[:, :, 32:64]
        rot2 = early[:, 1280:1920].rearrange("p (h e) -> p h e", e=32)
        gate_a = sb("gate_a", [P, D])
        gate_f = sb("gate_f", [P, D])
        entry = sb("entry", [NP * H + 3, D])
        vwb = entry[0:NP * H]
        rowb = entry[NP * H:]
        mod_a = sb("mod_a", [P, 4])
        mod_f = sb("mod_f", [P, 4])
        xh = sb("xh", [P, D])
        hf = sb("hf", [P, 2, P])
        hh = sb("hh", [P, 2, P], F32R)
        hl = sb("hl", [P, 2, P], F32R)
        qT_h = sb("qT_h", [P, 8, P], F32R)
        qT_l = sb("qT_l", [P, 8, P], F32R)
        kT_h = sb("kT_h", [P, 2, 2, NK], F32R)
        kT_l = sb("kT_l", [P, 2, 2, NK], F32R)
        v_h = sb("v_h", [P, 2, 2, P], F32R)
        v_l = sb("v_l", [P, 2, 2, P], F32R)
        nmax = sb("nmax", [P, H])
        psums = sb("psums", [P, H])
        rinv = sb("rinv", [P, H])
        pT_h = sb("pT_h", [P, 2, 512], F32R)
        pT_l = sb("pT_l", [P, 2, 512], F32R)
        pp = sb("pp", [P, NP, H])
        ppT = sb("ppT", [NP * H, P])
        oT_h = sb("oT_h", [P, 8, P], F32R)
        oT_l = sb("oT_l", [P, 8, P], F32R)
        upd = sb("upd", [P, 2, D])

        stage = [sb(f"stage{i}", [P, 1024]) for i in range(2)]
        th = [stage[0][:, 256 * i:256 * i + 256] for i in range(2)]
        act_g = [stage[0][:, 512 + 256 * i:768 + 256 * i] for i in range(2)]
        acc = stage[1][:, 0:256]
        mixed = [stage[1][:, 256 + 128 * i:384 + 128 * i] for i in range(2)]
        xh2 = stage[1][:, 512:768]
        hf2 = stage[1][:, 768:1024].rearrange("p (h n) -> p h n", h=2)
        prod = sb("prod", [P, 4, 256])
        shared = [sb(f"shared{u}", [P, 256]) for u in range(2)]
        bst = sb("bst", [P, 6])
        beat = sb("beat", [P, 2])
        leps = sb("leps", [P, 1])
        mv = sb("mv", [P, 2])
        veps = sb("veps", [P, 1])
        rs2 = sb("rs2", [P, 1])
        fh = [sb(f"fh{u}", [P, 2, P], F32R) for u in range(2)]
        fl = [sb(f"fl{u}", [P, 2, P], F32R) for u in range(2)]
        lg = sb("lg", [P, NE])
        top8 = sb("top8", [P, 8])
        take = sb("take", [P, 8])
        nm = sb("nm", [P, 1])
        rest = sb("rest", [P, NE])
        ex = sb("ex", [P, NE])
        zsum = sb("zsum", [P, 1])
        s4 = sb("s4", [P, 1])
        den = sb("den", [P, 2])
        rn = sb("rn", [P, 1])
        coef = sb("coef", [P, NE])
        coefT = lg
        w8 = [sb(f"w8_{u}", [P, NB]) for u in range(2)]
        mT_h = sb("mT_h", [P, 3, P], F32R)
        mT_l = sb("mT_l", [P, 3, P], F32R)
        updf = sb("updf", [P, D])

        spare = probs[:].rearrange("p h k -> p (h k)")
        c_row = spare[0:B, 0:768].rearrange("p (a d) -> p a d", a=3)
        modrow = early[0:B, 0:6 * D]
        cT = sb("cT", [P, 2, B])
        bst4 = sb("bst4", [P, 4, 6])
        mv4 = sb("mv4", [P, 4, 2])
        lsc = sb("lsc", [P, 2, H])
        amp = sb("amp", [P, NB, 2])
        ampp = sb("ampp", [P, NB])
        amps = sb("amps", [P, 4])
        mask_f = upd[:].rearrange("p a d -> p (a d)")[:, 0:2 * NK]
        mod_p = [sb(f"mod_p{i}", [P, 4]) for i in range(2)]
        first = (early[:, 0:1024], spare[:, 1024:2048])
        xh0 = [f[:, 0:256] for f in first]
        xh1 = [f[:, 256:512] for f in first]
        kr0 = [f[:, 512:768] for f in first]
        rk1 = [f[:, 768:896].rearrange("p (h e) -> p h e", e=32) for f in first]
        rk2 = [f[:, 896:1024].rearrange("p (h e) -> p h e", e=32) for f in first]
        hf0 = [hf[:], spare[:, 0:256].rearrange("p (h n) -> p h n", h=2)]
        h0h, h0l = [hh, fh[0]], [hl, fl[0]]
        hpool = spare[:, 256:384].rearrange("p (h r b) -> p h r b", h=2, r=4)
        hp_h, hp_l = [o[:, 0].rearrange("p (h r b) -> p h r b", h=2, r=4) for o in (oT_h, oT_l)]
        vTf = spare[:, 640:704].rearrange("p (t n) -> p t n", t=2)
        q127 = early[0:B, 0:1024].rearrange("p (h e) -> p h e", e=DH)
        tmpq = spare[0:B, 1024:2048].rearrange("p (h e) -> p h e", e=DH)
        kprow = early[0:B, 1024:1536].rearrange("p (k n) -> p k n", k=NP)
        dots = stage[0][0:B, 0:1024].rearrange("p (h e) -> p h e", e=DH)
        vrow = stage[1][0:B, 0:768].rearrange("p (r n) -> p r n", r=3)
        s127 = stage[1][0:B, 768:768 + NP * H].rearrange("p (k h) -> p k h", k=NP)
        sm127 = stage[1][0:B, 832:832 + 6 * H].rearrange("p (k h) -> p k h", k=6)
        rT = prod[:].rearrange("p a n -> p (a n)")[:, 0:8 * 48].rearrange("p (j r b) -> p j r b", j=8, r=3)
        vws = spare[0:NP * B, 0:2048].rearrange("p (h n) -> p h n", n=D)
        rows_sb = updf[0:48, :]

        names = """tab_ld mask_ld c_ld mod_ld small_ld stage_ld0 stage_ld1 x_ld0 x_ld1 x_ld2 x_ld3
        silu_t silu_a silu_row cT_ps cT_copied mod_ps modrow_done gate_fix modT_ps modT_done gates_st
        lsc_exp lsc_done amp_d mix_done mask_done const_done q_scaled piece_hi piece_lo
        bn1 aggr1 stats_done rs_var rs_done
        a_xh a_ps a_hf a_hi a_lo a_kps a_ksem a_km a_krot a_kp_ps a_kp a_hp
        hp_hi hp_lo z_v_ps z_v_copied z_q_ps z_kp_ps z_chain z_exp z_row_ps z_rT z_rT_hi
        z_rT_lo z_vT_ps z_vT z_vT_hi z_vT_lo z_rows_ps z_rows z_rows_st z_vw_ps z_vw z_vw_st z_zero
        gate_a_ld gate_f_ld vw_ld row_ld
        mod_a_ready xh_ready hT_ps hf_ready h_hi h_lo k_ps q_ps v_ps k_sem v_hi q_sem v_lo k_m q_m k_rot q_rot
        kT_ps qT_ps kpz kT_hi kT_lo qT_hi qT_lo s_ps nmax_ready exp_done rinv_ready p_ready
        pT_ps pT_hi pT_lo o_ps oT_hi_r oT_lo_r pp_ps ppT_ready row_ps y_ps upd_ready x_mid
        f_bn f_var f_veps f_rs f_xh f_mod f_hT_ps f_hf f_hi f_lo l_ps lg_ready top_ready nm_ready take_ready
        rest_ready ex_ready coef_ready den_ready rcp_ready rn_ready cT2_ps cT2_ready w_ps w8_ready
        gu_ps th_ready ag_ready chunk_done mix_sum mixed_ready m_ps mT_hi_r mT_lo_r d_ps updf_ready x_done
        out_st""".split()
        S = {n: sem(n) for n in names}

        block = ctx.enter_context(nc.Block())

        def d_rows(ap):
            return ap.rearrange("(h p) n -> p h n", p=P)

        def halves(stg):
            return stg[:].rearrange("p (h n) -> p h n", h=2)

        wo_rows = wo.rearrange("(t s j e) n -> s t e j n", t=2, s=2, j=JH_)

        PIECES = ["m0", "m1", "m2", "kv", "qs", "qg", "o0", "o1", "rd", "g0", "u0", "g1", "u1", "sh"]
        SPLIT = PIECES[3:]
        LOADS = {"kv": 3, "o0": 2, "o1": 2, "rd": 3, "sh": 2}

        def loads_to(i):
            return 16 * sum(LOADS.get(p, 1) for p in PIECES[i % 2:i + 1:2])

        def split_views(name, stg):
            s3 = halves(stg)
            if name == "kv":
                r = []
                for lo, e0 in ((0, 0), (128, 32)):
                    src = s3[:, :, lo:lo + 128].rearrange("p h (g e) -> p h g e", e=32)
                    dst = [w[:, :, QC:QC + KC].rearrange("p h (g e) -> p h g e", e=DH)[:, :, :, e0:e0 + 32]
                           for w in (wqkv_h, wqkv_l)]
                    r.append((src, dst[0], dst[1]))
                r.append((s3[:, :, 256:512], wqkv_h[:, :, QC + KC:QKV], wqkv_l[:, :, QC + KC:QKV]))
                return r
            if name in ("qs", "qg"):
                e0 = 0 if name == "qs" else 32
                r = []
                for h in range(2):
                    for t in range(2):
                        src = s3[:, h, 256 * t:256 * t + 256].rearrange("p (s j e) -> p j s e", s=2, j=4)
                        dst = [w[:, h, 512 * t:512 * t + 512].rearrange("p (j s e) -> p j s e", j=4, s=2)
                               [:, :, :, e0:e0 + 32] for w in (wqkv_h, wqkv_l)]
                        r.append((src, dst[0], dst[1]))
                return r
            if name in ("o0", "o1"):
                t = int(name[1])
                return [(stg[:].rearrange("p (j n) -> p j n", j=4), wo_h[:, 4 * t:4 * t + 4, :],
                         wo_l[:, 4 * t:4 * t + 4, :])]
            if name == "rd":
                return [(stg[:, 0:256].rearrange("p (h n) -> p h n", h=2), wr_h[:], wr_l[:]),
                        (stg[:, 256:1024].rearrange("p (k n) -> p k n", k=3), wd_h[:], wd_l[:])]
            if name == "sh":
                s4_ = stg[:].rearrange("p (a h n) -> p a h n", a=2, h=2)
                return [(s4_[:, a], wgu_h[:, :, 0, 256 * a:256 * a + 256], wgu_l[:, :, 0, 256 * a:256 * a + 256])
                        for a in range(2)]
            a, c0 = (0 if name[0] == "g" else 256), 1 + 2 * int(name[1])
            return [(s3.rearrange("p h (c n) -> p h c n", c=2), wgu_h[:, :, c0:c0 + 2, a:a + 256],
                     wgu_l[:, :, c0:c0 + 2, a:a + 256])]

        def beside(v):
            return v[:].rearrange("p t s (g e) -> p t (s g) e", e=DH)[:, :, 0:4:3, :]

        def real(n):
            return not isinstance(n, int) or 0 <= n < NT

        @block.sync
        def _(sp):
            sp.dma_start(c_row[:, 0, :], c_in).then_inc(S["c_ld"], 16)
            sp.dma_start(tab[:], table).then_inc(S["tab_ld"], 16)
            sp.dma_start(mask_f, mask_in).then_inc(S["mask_ld"], 16)
            sp.dma_start(lsc[:, 0, :], logit_scale.rearrange("(a h) -> a h", a=1).to_broadcast([P, H])
                         ).then_inc(S["small_ld"], 16)
            sp.dma_start(amp[:], amplitudes).then_inc(S["small_ld"], 16)
            sp.dma_start(amps[:, 2:3], expert_scale.rearrange("(e a) -> e a", a=1)).then_inc(S["small_ld"], 16)

            def load_piece(i):
                name, stg, s = PIECES[i], stage[i % 2], S[f"stage_ld{i % 2}"]
                s3 = halves(stg)
                if 2 <= i < 5:
                    sp.wait_ge(S["mod_ps"], i - 1)
                if i >= 5:
                    sp.wait_ge(S["piece_lo"], i - 4)
                if name[0] == "m":
                    n = int(name[1])
                    sp.dma_start(s3, d_rows(wmod)[:, :, 512 * n:512 * n + 512]).then_inc(s, 16)
                elif name == "kv":
                    sp.dma_start(s3[:, :, 0:128], d_rows(wk_sem)).then_inc(s, 16)
                    sp.dma_start(s3[:, :, 128:256], d_rows(wk_geo)).then_inc(s, 16)
                    sp.dma_start(s3[:, :, 256:512], d_rows(wv)).then_inc(s, 16)
                elif name in ("qs", "qg"):
                    sp.dma_start(s3, d_rows(wq_sem if name == "qs" else wq_geo)).then_inc(s, 16)
                elif name in ("o0", "o1"):
                    o4 = stg[:].rearrange("p (j n) -> p j n", j=4)
                    for k in range(2):
                        sp.dma_start(o4[64 * k:64 * k + 64], wo_rows[k, int(name[1])]).then_inc(s, 16)
                elif name == "rd":
                    sp.dma_start(stg[:, 0:256].rearrange("p (h n) -> p h n", h=2), d_rows(w_router)).then_inc(s, 16)
                    sp.dma_start(stg[:, 256:512], w_down).then_inc(s, 16)
                    sp.dma_start(stg[:, 512:1024].rearrange("p (h n) -> p h n", h=2), d_rows(sw_down)).then_inc(s, 16)
                elif name == "sh":
                    s4_ = stg[:].rearrange("p (a h n) -> p a h n", a=2, h=2)
                    sp.dma_start(s4_[:, 0], d_rows(sw_gate)).then_inc(s, 16)
                    sp.dma_start(s4_[:, 1], d_rows(sw_up)).then_inc(s, 16)
                else:
                    w, n = (w_gate if name[0] == "g" else w_up), int(name[1])
                    sp.dma_start(s3, d_rows(w)[:, :, 512 * n:512 * n + 512]).then_inc(s, 16)

            load_piece(0)
            load_piece(1)
            x_tiles = x_in.rearrange("b (u p) d -> p (b u) d", p=P)
            for q in range(2):
                sp.dma_start(x[:, 8 * q:8 * q + 8, :], x_tiles[:, 8 * q:8 * q + 8, :]).then_inc(S[f"x_ld{q}"], 16)
            load_piece(2)
            load_piece(3)
            for q in range(2, 4):
                sp.dma_start(x[:, 8 * q:8 * q + 8, :], x_tiles[:, 8 * q:8 * q + 8, :]).then_inc(S[f"x_ld{q}"], 16)
            sp.wait_ge(S["gate_fix"], 5)
            for a, col in ((0, 2 * D), (1, 5 * D)):
                sp.dma_start(gates_dram[:, a, :], modrow[:, col:col + D]).then_inc(S["gates_st"], 16)
            for i in range(4, len(PIECES)):
                load_piece(i)
            sp.wait_ge(S["z_rows"], 1)
            sp.dma_start(rows_dram.rearrange("r b n -> (r b) n"), rows_sb).then_inc(S["z_rows_st"], 16)
            for t in range(2):
                sp.wait_ge(S["z_vw"], 4 * t + 4)
                for k in range(NP):
                    sp.dma_start(vw_dram[:, k, 8 * t:8 * t + 8, :], vws[B * k:B * k + B]).then_inc(S["z_vw_st"], 16)
            sp.wait_ge(S["gates_st"], 32)
            sp.wait_ge(S["z_rows_st"], 16)
            sp.wait_ge(S["z_vw_st"], 64)

            def load_entry(b):
                sp.dma_start(gate_a[:], gates_dram[b, 0:1, :].to_broadcast([P, D])).then_inc(S["gate_a_ld"], 16)
                sp.dma_start(vwb, vw_dram[b].rearrange("k h n -> (k h) n")).then_inc(S["vw_ld"], 16)
                sp.dma_start(rowb, rows_dram[:, b, :]).then_inc(S["row_ld"], 16)

            def load_gate_f(f):
                sp.dma_start(gate_f[:], gates_dram[f, 1:2, :].to_broadcast([P, D])).then_inc(S["gate_f_ld"], 16)

            def store(f):
                for u in range(2):
                    sp.wait_ge(S["x_done"], 2 * f + u + 2)
                    sp.dma_start(out[f, P * u:P * u + P, :], x[:, 2 * f + u, :]).then_inc(S["out_st"], 16)

            load_entry(0)
            sp.wait_ge(S["x_mid"], 1)
            load_entry(1)
            load_gate_f(0)
            with sp.Fori(2, B) as b:
                sp.wait_ge(S["x_mid"], b)
                load_entry(b)
                store(b - 2)
                load_gate_f(b - 1)
            store(B - 2)
            load_gate_f(B - 1)
            store(B - 1)
            sp.wait_ge(S["out_st"], 16 * NT)

        @block.gpsimd
        def _(gp):
            gp.memset(leps[:], LN_EPS)
            gp.memset(mhalf[:], -0.5).then_inc(S["const_done"], 1)
            for i, name in enumerate(SPLIT):
                gp.wait_ge(S["piece_hi"], i + 1)
                views = split_views(name, stage[(i + 3) % 2])
                for k, (src, hi, lo) in enumerate(views):
                    ins = gp.tensor_tensor(lo, src, hi.bitcast(F32), ALU.subtract)
                    if k == len(views) - 1:
                        ins.then_inc(S["piece_lo"], 1)
                if name == "kv":
                    gp.wait_ge(S["stats_done"], NT // 4)
                    gp.wait_ge(S["const_done"], 1)
                    gp.tensor_scalar(rs1[:], st[:, :, 1], LN_EPS, None, ALU.add).then_inc(S["rs_var"], 1)
                    gp.wait_ge(S["rs_var"], 1)
                    gp.tensor_tensor(rs1[:], rs1[:], mhalf[:], ALU.pow).then_inc(S["rs_done"], 1)

            def keys_and_queries(b):
                gp.wait_ge(S["k_m"], b + 1)
                gp.tensor_tensor(rot1[:, H:], rot1[:, H:], rot2[:, H:], ALU.add).then_inc(S["k_rot"], 1)
                gp.wait_ge(S["q_m"], b + 1)
                gp.tensor_tensor(rot1[:, 0:H], rot1[:, 0:H], rot2[:, 0:H], ALU.add).then_inc(S["q_rot"], 1)

            def normalise(b, t):
                gp.wait_ge(S["rinv_ready"], 2 * b + t + 1)
                scale = rinv[:, 8 * t:8 * t + 8].unsqueeze(2)
                gp.tensor_tensor(pp[:, :, 8 * t:8 * t + 8].rearrange("p k h -> p h k"),
                                 probs[:, 8 * t:8 * t + 8, P:NK], scale.to_broadcast([P, 8, NP]), ALU.mult)
                gp.tensor_tensor(probs[:, 8 * t:8 * t + 8, 0:P], probs[:, 8 * t:8 * t + 8, 0:P],
                                 scale.to_broadcast([P, 8, P]), ALU.mult).then_inc(S["p_ready"], 1)

            def ln2(n):
                gp.wait_ge(S["f_var"], n + 1)
                gp.tensor_tensor(veps[:], mv[:, 1:2], leps[:], ALU.add).then_inc(S["f_veps"], 1)
                gp.wait_ge(S["f_veps"], n + 1)
                gp.tensor_tensor(rs2[:], veps[:], mhalf[:, 0:1], ALU.pow).then_inc(S["f_rs"], 1)

            def mix_sum(n, u, k):
                gp.wait_ge(S["chunk_done"], NCH * n + k + 1 + 2)
                if k == 2:
                    if not (isinstance(n, int) and n == 0):
                        gp.wait_ge(S["mixed_ready"], n)
                    gp.tensor_tensor(acc, prod[:, 0, :], prod[:, 1, :], ALU.add).then_inc(S["mix_sum"], 1)
                else:
                    gp.wait_ge(S["mix_sum"], 3 * n + k - 2)
                    gp.tensor_tensor(acc, acc, prod[:, k - 1, :], ALU.add).then_inc(S["mix_sum"], 1)
                if k == 4:
                    gp.wait_ge(S["mix_sum"], 3 * n + 3)
                    gp.tensor_tensor(mixed[u], acc[:, 0:128], acc[:, 128:256], ALU.add
                                     ).then_inc(S["mixed_ready"], 1)

            def body(b, back, front):
                m0, m1, m2 = 2 * b - 3, 2 * b - 2, 2 * b - 1
                if real(m1):
                    ln2(m1)
                if back:
                    normalise(b, 0)
                    normalise(b, 1)
                if real(m0):
                    mix_sum(m0, 1, 2)
                    mix_sum(m0, 1, 3)
                if front:
                    keys_and_queries(b + 1)
                if real(m2):
                    ln2(m2)
                if real(m0):
                    mix_sum(m0, 1, 4)
                if real(m1):
                    mix_sum(m1, 0, 2)
                    mix_sum(m1, 0, 3)
                    mix_sum(m1, 0, 4)

            keys_and_queries(0)
            body(0, True, True)
            body(1, True, True)
            with gp.Fori(2, B - 1) as b:
                body(b, True, True)
            body(B - 1, True, False)
            body(B, False, False)
            body(B + 1, False, False)

        @block.tensor
        def _(pe):
            def mm3(out_, lh, ll, rh, rl, start, stop, **kw):
                pe.matmul(out_, lh, rh, start=start, stop=False, **kw)
                pe.matmul(out_, lh, rl, start=False, stop=False, **kw)
                return pe.matmul(out_, ll, rh, start=False, stop=stop, **kw)

            pe.wait_ge(S["tab_ld"], 16)
            pe.wait_ge(S["silu_row"], 1)
            for h in range(2):
                ins = pe.transpose(ps[:, AO, 16 * h:16 * h + 16], c_row[:, 2, P * h:P * h + P], ident[0:B, 0:B])
            ins.then_inc(S["cT_ps"], 1)
            pe.wait_ge(S["cT_copied"], 1)
            for n in range(3):
                pe.wait_ge(S[f"stage_ld{n % 2}"], loads_to(n))
                for h in range(2):
                    ins = pe.matmul(ps[0:B, n, :], cT[:, h, :], halves(stage[n % 2])[:, h, :],
                                    start=(h == 0), stop=(h == 1))
                ins.then_inc(S["mod_ps"], 1)
            pe.wait_ge(S["modrow_done"], 4)
            for k, col in enumerate((D, 0, 4 * D, 3 * D)):
                for h in range(2):
                    ins = pe.transpose(ps[:, AO, 32 + 16 * (2 * k + h):48 + 16 * (2 * k + h)],
                                       modrow[:, col + P * h:col + P * h + P], ident[0:B, 0:B])
            ins.then_inc(S["modT_ps"], 1)

            pe.wait_ge(S["piece_lo"], 1)
            with pe.Fori(0, B // 2) as i:
                for p in range(2):
                    pe.wait_ge(S["a_xh"], 2 * i + p + 1)
                    for h in range(2):
                        pe.transpose(ps[:, p, P * h:P * h + P], xh0[p][:, P * h:P * h + P], ident)
                    for h in range(2):
                        pe.matmul(ps[:, p, 256 + 4 * h:260 + 4 * h], xh0[p][:, P * h:P * h + P], pool0,
                                  start=True, stop=False)
                        ins = pe.matmul(ps[:, p, 256 + 4 * h:260 + 4 * h], xh1[p][:, P * h:P * h + P], pool1,
                                        start=False, stop=True)
                    ins.then_inc(S["a_ps"], 1)
                for p in range(2):
                    pe.wait_ge(S["a_lo"], 2 * i + p + 1)
                    for h in range(2):
                        ins = mm3(ps[:, 2 + p, 0:KC], h0h[p][:, h, :], h0l[p][:, h, :],
                                  wqkv_h[:, h, QC:QC + KC], wqkv_l[:, h, QC:QC + KC], h == 0, h == 1)
                    ins.then_inc(S["a_kps"], 1)
                for p in range(2):
                    pe.wait_ge(S["a_krot"], 2 * i + p + 1)
                    for t in range(2):
                        ins = pe.matmul(ps[:, 4 + p, 2 * t:2 * t + 2], kr0[p][:, P * t:P * t + P],
                                        pool0[:, 0:2], start=True, stop=True)
                    ins.then_inc(S["a_kp_ps"], 1)

            pe.wait_ge(S["hp_lo"], 1)
            pe.wait_ge(S["piece_lo"], 5)
            for k, r in enumerate((3, 0, 1)):
                for h in range(2):
                    ins = mm3(ps[0:B, k // 2, 256 * (k % 2):256 * (k % 2) + 256], hp_h[:, h, r, :], hp_l[:, h, r, :],
                              wqkv_h[:, h, QC + KC:QKV], wqkv_l[:, h, QC + KC:QKV], h == 0, h == 1)
            ins.then_inc(S["z_v_ps"], 1)
            for t in range(2):
                for h in range(2):
                    ins = mm3(ps[0:B, 2 + t, :], hp_h[:, h, 2, :], hp_l[:, h, 2, :],
                              wqkv_h[:, h, 512 * t:512 * t + 512], wqkv_l[:, h, 512 * t:512 * t + 512],
                              h == 0, h == 1)
            ins.then_inc(S["z_q_ps"], 1)
            pe.wait_ge(S["a_kp"], B)
            for k in range(NP):
                for t in range(2):
                    ins = pe.transpose(ps[0:B, 4, 256 * k + P * t:256 * k + P * t + P], kpool[:, :, t, k], ident)
            ins.then_inc(S["z_kp_ps"], 1)
            for t in range(2):
                for h in range(2):
                    ins = mm3(ps[:, 5, 32 * t:32 * t + 32], wqkv_h[:, h, QC + KC + P * t:QC + KC + P * t + P],
                              wqkv_l[:, h, QC + KC + P * t:QC + KC + P * t + P],
                              hp_h[:, h, 0:2, :], hp_l[:, h, 0:2, :], h == 0, h == 1)
            ins.then_inc(S["z_vT_ps"], 1)
            pe.wait_ge(S["z_v_copied"], 1)
            for r in range(2):
                for t in range(2):
                    ins = pe.transpose(ps[:, 6, 16 * (2 * r + t):16 * (2 * r + t) + 16],
                                       vrow[:, r, P * t:P * t + P], ident[0:B, 0:B])
            pe.wait_ge(S["z_chain"], Z_ROW_C)
            for j in range(8):
                ins = pe.transpose(ps[:, 6, 64 + 16 * j:80 + 16 * j],
                                   tmpq[:, 2 * j:2 * j + 2, :], ident[0:B, 0:B])
            ins.then_inc(S["z_row_ps"], 1)
            pe.wait_ge(S["z_rT_lo"], 1)
            for j in range(8):
                ins = mm3(ps[0:48, 7, 0:D], qT_h[:, j, 0:48], qT_l[:, j, 0:48], wo_h[:, j, :], wo_l[:, j, :],
                          j == 0, j == 7)
            ins.then_inc(S["z_rows_ps"], 1)
            pe.wait_ge(S["z_vT_lo"], 1)
            for j in range(8):
                if j >= 2:
                    pe.wait_ge(S["z_vw"], j - 1)
                for s in range(2):
                    r = slice(64 * s, 64 * s + 64)
                    ins = mm3(ps[0:NP * B, 2 * (j % 2) + s, 0:D], pT_h[r, j // 4, 0:32], pT_l[r, j // 4, 0:32],
                              wo_h[r, j, :], wo_l[r, j, :], True, True)
                ins.then_inc(S["z_vw_ps"], 1)

            def to_features(b):
                pe.wait_ge(S["xh_ready"], b + 1)
                for h in range(2):
                    ins = pe.transpose(ps[:, A3, P * h:P * h + P], xh[:, P * h:P * h + P], ident)
                ins.then_inc(S["hT_ps"], 1)

            def project(b):
                pe.wait_ge(S["h_lo"], b + 1)
                if not (isinstance(b, int) and b == 0):
                    pe.wait_ge(S["exp_done"], 8 * b)
                for bank, lo, n in ((A2, QC, KC), (A0, 0, 512), (A1, 512, 512)):
                    for h in range(2):
                        ins = mm3(ps[:, bank, 0:n], hh[:, h, :], hl[:, h, :], wqkv_h[:, h, lo:lo + n],
                                  wqkv_l[:, h, lo:lo + n], h == 0, h == 1)
                    if bank == A2:
                        ins.then_inc(S["k_ps"], 1)
                ins.then_inc(S["q_ps"], 1)

            def project_v(b):
                if not (isinstance(b, int) and b == 0):
                    pe.wait_ge(S["pT_lo"], 4 * b)
                for h in range(2):
                    ins = mm3(ps[:, A3, 256:512], hh[:, h, :], hl[:, h, :], wqkv_h[:, h, QC + KC:QKV],
                              wqkv_l[:, h, QC + KC:QKV], h == 0, h == 1)
                ins.then_inc(S["v_ps"], 1)

            def keys_T(b):
                pe.wait_ge(S["k_rot"], b + 1)
                for t in range(2):
                    ins = pe.transpose(ps[:, A2, P * t:P * t + P], qk[:, H + 2 * t:H + 2 * t + 2, :], ident)
                ins.then_inc(S["kT_ps"], 1)

            def queries_T(b):
                pe.wait_ge(S["q_rot"], b + 1)
                for t in range(2):
                    for j in range(4):
                        p = 8 * t + 2 * j
                        ins = pe.transpose(ps[:, A0 + t, P * j:P * j + P], qk[:, p:p + 2, :], ident)
                    ins.then_inc(S["qT_ps"], 1)

            def scores(b, g):
                if g == 0:
                    pe.wait_ge(S["kT_lo"], b + 1)
                    pe.wait_ge(S["qT_lo"], 2 * b + 2)
                if g >= 3:
                    pe.wait_ge(S["exp_done"], 8 * b + g - 2)
                o = ps[:, A0 + g % 3, 0:2 * NK].rearrange("p (s k) -> p s k", k=NK)
                pe.matmul(o, id16[:], mask16[:], start=True, stop=False)
                mm3(o, qT_h[:, g, :], qT_l[:, g, :], kT_h[:, g // 4], kT_l[:, g // 4], False, True
                    ).then_inc(S["s_ps"], 1)

            def probs_T(b, t, s, more=True):
                n = 4 * b + 2 * t + s
                if s == 0:
                    pe.wait_ge(S["p_ready"], 2 * b + t + 1)
                if t == 0 and s == 0:
                    pe.wait_ge(S["v_lo"], b + 1)
                    if more:
                        pe.wait_ge(S["hf_ready"], b + 2)
                if t or s:
                    pe.wait_ge(S["pT_lo"], n)
                for j in range(4):
                    ins = pe.transpose(ps[:, A3, P * j:P * j + P], probs[:, 8 * t + 2 * j + s, 0:P], ident)
                ins.then_inc(S["pT_ps"], 1)

            def values(b, t):
                if t:
                    pe.wait_ge(S["oT_lo_r"], 2 * b + 1)
                for s in range(2):
                    pe.wait_ge(S["pT_lo"], 4 * b + 2 * t + s + 1)
                    ins = mm3(ps[:, AO, :], v_h[:, t, s, :], v_l[:, t, s, :], pT_h[:, s, :], pT_l[:, s, :],
                              s == 0, s == 1)
                ins.then_inc(S["o_ps"], 1)

            def pooled_T(b):
                pe.wait_ge(S["p_ready"], 2 * b + 2)
                pe.wait_ge(S["oT_lo_r"], 2 * b + 2)
                pe.transpose(ps[0:NP * H, AO, 256:384], pp[:].rearrange("p k h -> p (k h)"), ident
                             ).then_inc(S["pp_ps"], 1)

            def first_tile(b, more):
                pe.wait_ge(S["row_ld"], 16 * b + 16)
                if more:
                    pe.wait_ge(S["v_lo"], b + 2)
                else:
                    pe.wait_ge(S["pT_lo"], 4 * b + 4)
                pe.matmul(ps[:, A3, 0:D], tab[NP * H:NP * H + 3, C_SEL:C_SEL + P], rowb, start=True, stop=True
                          ).then_inc(S["row_ps"], 1)

            def project_out(b):
                pe.wait_ge(S["oT_lo_r"], 2 * b + 2)
                pe.wait_ge(S["ppT_ready"], b + 1)
                pe.wait_ge(S["vw_ld"], 16 * b + 16)
                pe.matmul(ps[:, AO, 0:D], ppT[:], vwb, start=True, stop=False)
                for j in range(8):
                    ins = mm3(ps[:, AO, 0:D], oT_h[:, j, :], oT_l[:, j, :], wo_h[:, j, :], wo_l[:, j, :],
                              False, j == 7)
                ins.then_inc(S["y_ps"], 1)

            def f_features(n, u):
                pe.wait_ge(S["f_xh"], n + 1)
                if not (isinstance(n, int) and n == 0):
                    pe.wait_ge(S["w8_ready"], n)
                for h in range(2):
                    ins = pe.transpose(ps[:, FM, P * h:P * h + P], xh2[:, P * h:P * h + P], ident)
                ins.then_inc(S["f_hT_ps"], 1)

            def f_inner_T(n, u):
                pe.wait_ge(S["mixed_ready"], n + 1)
                if real(n + 2):
                    pe.wait_ge(S["f_hf"], n + 3)
                elif n == NT - 2:
                    pe.wait_ge(S["w8_ready"], NT)
                else:
                    pe.wait_ge(S["x_done"], NT)
                pe.transpose(ps[:, FM, 0:P], mixed[u], ident)
                for h in range(2):
                    ins = pe.transpose(ps[:, FM, P * (h + 1):P * (h + 2)], shared[u][:, P * h:P * h + P], ident)
                ins.then_inc(S["m_ps"], 1)

            def f_logits(n, u):
                pe.wait_ge(S["f_lo"], n + 1)
                if real(n - 2):
                    pe.wait_ge(S["mT_lo_r"], n - 1)
                for h in range(2):
                    ins = mm3(ps[:, FM, 256:384], fh[u][:, h, :], fl[u][:, h, :], wr_h[:, h, :], wr_l[:, h, :],
                              h == 0, h == 1)
                ins.then_inc(S["l_ps"], 1)

            def f_down(n):
                pe.wait_ge(S["mT_lo_r"], n + 1)
                if real(n + 2):
                    pe.wait_ge(S["top_ready"], n + 3)
                for k in range(3):
                    ins = mm3(ps[:, FM, 0:D], mT_h[:, k, :], mT_l[:, k, :], wd_h[:, k, :], wd_l[:, k, :],
                              k == 0, k == 2)
                ins.then_inc(S["d_ps"], 1)

            def f_coefT(n):
                pe.wait_ge(S["coef_ready"], n + 1)
                if real(n - 2):
                    pe.wait_ge(S["x_done"], n)
                pe.transpose(ps[:, FM, 384:512], coef[:], ident).then_inc(S["cT2_ps"], 1)

            def f_weights(n):
                pe.wait_ge(S["cT2_ready"], n + 1)
                pe.matmul(ps[:, FM, 0:NB], coefT[:], mix[:], start=True, stop=True).then_inc(S["w_ps"], 1)

            def f_chunk(n, u, k):
                bank = FR + (k + u) % 2
                pe.wait_ge(S["chunk_done"], NCH * n + k + 1)
                if k == 0:
                    pe.wait_ge(S["f_lo"], n + 1)
                for h in range(2):
                    ins = mm3(ps[:, bank, :], fh[u][:, h, :], fl[u][:, h, :], wgu_h[:, h, k, :],
                              wgu_l[:, h, k, :], h == 0, h == 1)
                ins.then_inc(S["gu_ps"], 1)

            def body(b, back, front):
                m0, m1, m2 = 2 * b - 3, 2 * b - 2, 2 * b - 1
                if back:
                    scores(b, 0)
                if real(m0):
                    f_chunk(m0, 1, 0)
                if back:
                    scores(b, 1)
                    scores(b, 2)
                    scores(b, 3)
                if front:
                    to_features(b + 1)
                if real(m0):
                    f_chunk(m0, 1, 1)
                    f_chunk(m0, 1, 2)
                if real(m1):
                    f_features(m1, 0)
                if back:
                    scores(b, 4)
                    scores(b, 5)
                if real(m1 - 2):
                    f_inner_T(m1 - 2, 0)
                if back:
                    scores(b, 6)
                if real(m0):
                    f_chunk(m0, 1, 3)
                if back:
                    scores(b, 7)
                if real(m1):
                    f_logits(m1, 0)
                if back:
                    probs_T(b, 0, 0, front)
                if real(m1 - 2):
                    f_down(m1 - 2)
                if real(m0):
                    f_chunk(m0, 1, 4)
                if back:
                    probs_T(b, 0, 1)
                if real(m1):
                    f_coefT(m1)
                if front:
                    project(b + 1)
                if real(m1):
                    f_weights(m1)
                if back:
                    values(b, 0)
                    probs_T(b, 1, 0)
                if real(m1):
                    f_chunk(m1, 0, 0)
                if front:
                    keys_T(b + 1)
                if real(m1):
                    f_chunk(m1, 0, 1)
                if back:
                    probs_T(b, 1, 1)
                if front:
                    queries_T(b + 1)
                if real(m2):
                    f_features(m2, 1)
                if back:
                    values(b, 1)
                if real(m0):
                    f_inner_T(m0, 1)
                if real(m1):
                    f_chunk(m1, 0, 2)
                if front:
                    project_v(b + 1)
                if real(m2):
                    f_logits(m2, 1)
                if real(m1):
                    f_chunk(m1, 0, 3)
                if back:
                    pooled_T(b)
                    first_tile(b, front)
                if real(m0):
                    f_down(m0)
                if back:
                    project_out(b)
                if real(m2):
                    f_coefT(m2)
                if real(m1):
                    f_chunk(m1, 0, 4)
                if real(m2):
                    f_weights(m2)

            to_features(0)
            project(0)
            keys_T(0)
            queries_T(0)
            project_v(0)
            body(0, True, True)
            body(1, True, True)
            with pe.Fori(2, B - 1) as b:
                body(b, True, True)
            body(B - 1, True, False)
            body(B, False, False)
            body(B + 1, False, False)

        @block.scalar
        def _(act):
            act.wait_ge(S["small_ld"], 48)
            act.activation(lsc[:, 1, :], lsc[:, 0, :], ACT.Exp).then_inc(S["lsc_exp"], 1)
            act.wait_ge(S["c_ld"], 16)
            act.activation(c_row[:, 1, :], c_row[:, 0, :], ACT.Tanh, scale=0.5).then_inc(S["silu_t"], 1)
            for n in range(3):
                act.wait_ge(S["mod_ps"], n + 1)
                act.copy(modrow[:, 512 * n:512 * n + 512], ps[0:B, n, :]).then_inc(S["mod_ld"], 1)

            def split(i):
                name = SPLIT[i]
                if name in ("qs", "qg"):
                    act.wait_ge(S["q_scaled"], 1 + ("qs", "qg").index(name))
                else:
                    act.wait_ge(S[f"stage_ld{(i + 3) % 2}"], loads_to(i + 3))
                views = split_views(name, stage[(i + 3) % 2])
                for k, (src, hi, lo) in enumerate(views):
                    ins = act.copy(hi, src)
                    if k == len(views) - 1:
                        ins.then_inc(S["piece_hi"], 1)

            for i in range(5):
                split(i)

            def first_half_keys(i):
                for p in range(2):
                    act.wait_ge(S["a_ps"], 2 * i + p + 1)
                    for h in range(2):
                        ins = act.activation(hf0[p][:, h, :], ps[:, p, P * h:P * h + P], ACT.Identity,
                                             bias=mod_p[p][:, 2 + h:3 + h], scale=mod_p[p][:, h:h + 1])
                    ins.then_inc(S["a_hf"], 1)
                for p in range(2):
                    act.wait_ge(S["a_kps"], 2 * i + p + 1)
                    act.copy(kr0[p].rearrange("p (g e) -> p g e", e=DH)[:, :, 0:32],
                             ps[:, 2 + p, 0:KC].rearrange("p (g e) -> p g e", e=DH)[:, :, 0:32]
                             ).then_inc(S["a_ksem"], 1)

            with act.Fori(0, B // 2) as i:
                first_half_keys(i)
            for i in range(5, len(SPLIT)):
                split(i)

            act.wait_ge(S["z_chain"], Z_MAX)
            act.activation(sm127[:, 2:4, :], sm127[:, 0:2, :], ACT.Exp).then_inc(S["z_exp"], 1)

            def hidden(b):
                act.wait_ge(S["hT_ps"], b + 1)
                for h in range(2):
                    ins = act.activation(hf[:, h, :], ps[:, A3, P * h:P * h + P], ACT.Identity,
                                         bias=mod_a[:, 2 + h:3 + h], scale=mod_a[:, h:h + 1])
                ins.then_inc(S["hf_ready"], 1)
                act.wait_ge(S["hf_ready"], b + 1)
                act.copy(hh[:], hf[:]).then_inc(S["h_hi"], 1)

            def semantic_k(b):
                act.wait_ge(S["k_ps"], b + 1)
                act.copy(qk[:, H:, 0:32], ps[:, A2, 0:KC].rearrange("p (g e) -> p g e", e=DH)[:, :, 0:32]
                         ).then_inc(S["k_sem"], 1)

            def split_v(b):
                act.wait_ge(S["v_ps"], b + 1)
                act.copy(beside(v_h), ps[:, A3, 256:512].rearrange("p (t s e) -> p t s e", t=2, s=2)
                         ).then_inc(S["v_hi"], 1)

            def semantic_q(b):
                act.wait_ge(S["q_ps"], b + 1)
                act.copy(qk[:, 0:H, 0:32], ps[:, A0:A0 + 2, :].rearrange("p a (h e) -> p (a h) e", e=DH)[:, :, 0:32]
                         ).then_inc(S["q_sem"], 1)

            def split_k(b):
                act.wait_ge(S["kT_ps"], b + 1)
                for s in range(2):
                    r = slice(64 * s, 64 * s + 64)
                    ins = act.copy(kT_h[r, :, s, 0:P], ps[r, A2, 0:256].rearrange("p (t k) -> p t k", t=2))
                ins.then_inc(S["kT_hi"], 1)

            def split_q(b):
                for t in range(2):
                    act.wait_ge(S["qT_ps"], 2 * b + t + 1)
                    act.copy(qT_h[:, 4 * t:4 * t + 4, :], ps[:, A0 + t, :].rearrange("p (j k) -> p j k", j=4)
                             ).then_inc(S["qT_hi"], 1)

            def exps(b, g):
                act.wait_ge(S["nmax_ready"], 8 * b + g + 1)
                for s in range(2):
                    h = 2 * g + s
                    ins = act.activation(probs[:, h, :], ps[:, A0 + g % 3, NK * s:NK * s + NK], ACT.Exp,
                                         bias=nmax[:, h:h + 1], accum_out=psums[:, h:h + 1])
                ins.then_inc(S["exp_done"], 1)

            def split_probs(b, t, s):
                act.wait_ge(S["pT_ps"], 4 * b + 2 * t + s + 1)
                act.copy(pT_h[:, s, :], ps[:, A3, :]).then_inc(S["pT_hi"], 1)

            def split_out(b, t):
                act.wait_ge(S["o_ps"], 2 * b + t + 1)
                act.copy(oT_h[:, 4 * t:4 * t + 4, :], ps[:, AO, :].rearrange("p (j k) -> p j k", j=4)
                         ).then_inc(S["oT_hi_r"], 1)

            def pooled(b):
                act.wait_ge(S["pp_ps"], b + 1)
                act.copy(ppT[:], ps[0:NP * H, AO, 256:384]).then_inc(S["ppT_ready"], 1)

            def f_hidden(n, u):
                act.wait_ge(S["f_hT_ps"], n + 1)
                for h in range(2):
                    ins = act.activation(hf2[:, h, :], ps[:, FM, P * h:P * h + P], ACT.Identity,
                                         bias=mod_f[:, 2 + h:3 + h], scale=mod_f[:, h:h + 1])
                ins.then_inc(S["f_hf"], 1)
                act.wait_ge(S["f_hf"], n + 1)
                act.copy(fh[u][:], hf2).then_inc(S["f_hi"], 1)

            def f_route(n):
                act.wait_ge(S["nm_ready"], n + 1)
                act.activation(ex[:], lg[:], ACT.Exp, bias=nm[:, 0:1], accum_out=zsum[:]).then_inc(S["ex_ready"], 1)

            def f_coefT(n):
                act.wait_ge(S["cT2_ps"], n + 1)
                act.copy(coefT[:], ps[:, FM, 384:512]).then_inc(S["cT2_ready"], 1)

            def f_tanh(n, u, k):
                act.wait_ge(S["gu_ps"], NCH * n + k + 1)
                act.activation(th[(k + u) % 2], ps[:, FR + (k + u) % 2, 0:256], ACT.Tanh, scale=0.5
                               ).then_inc(S["th_ready"], 1)

            def f_inner(n):
                act.wait_ge(S["m_ps"], n + 1)
                act.copy(mT_h[:], ps[:, FM, 0:384].rearrange("p (k n) -> p k n", k=3)).then_inc(S["mT_hi_r"], 1)

            def body(b, back, front):
                m0, m1, m2 = 2 * b - 3, 2 * b - 2, 2 * b - 1
                if real(m0):
                    f_tanh(m0, 1, 0)
                if back:
                    exps(b, 0)
                    exps(b, 1)
                    exps(b, 2)
                    exps(b, 3)
                if real(m0):
                    f_tanh(m0, 1, 1)
                if front:
                    hidden(b + 1)
                if real(m1):
                    f_hidden(m1, 0)
                if real(m0):
                    f_tanh(m0, 1, 2)
                if real(m1 - 2):
                    f_inner(m1 - 2)
                if back:
                    exps(b, 4)
                    exps(b, 5)
                    exps(b, 6)
                    exps(b, 7)
                    split_probs(b, 0, 0)
                if real(m1):
                    f_route(m1)
                if real(m0):
                    f_tanh(m0, 1, 3)
                    f_tanh(m0, 1, 4)
                if back:
                    split_probs(b, 0, 1)
                if front:
                    semantic_k(b + 1)
                if real(m1):
                    f_coefT(m1)
                if front:
                    semantic_q(b + 1)
                if back:
                    split_out(b, 0)
                    split_probs(b, 1, 0)
                if front:
                    split_k(b + 1)
                if back:
                    split_probs(b, 1, 1)
                if real(m1):
                    f_tanh(m1, 0, 0)
                    f_tanh(m1, 0, 1)
                if real(m2):
                    f_hidden(m2, 1)
                if real(m0):
                    f_inner(m0)
                if front:
                    split_q(b + 1)
                if back:
                    split_out(b, 1)
                if front:
                    split_v(b + 1)
                if back:
                    pooled(b)
                if real(m1):
                    f_tanh(m1, 0, 2)
                if real(m2):
                    f_route(m2)
                if real(m1):
                    f_tanh(m1, 0, 3)
                if real(m2):
                    f_coefT(m2)
                if real(m1):
                    f_tanh(m1, 0, 4)

            hidden(0)
            semantic_k(0)
            semantic_q(0)
            split_k(0)
            split_q(0)
            split_v(0)
            body(0, True, True)
            body(1, True, True)
            with act.Fori(2, B - 1) as b:
                body(b, True, True)
            body(B - 1, True, False)
            body(B, False, False)
            body(B + 1, False, False)

        @block.vector
        def _(ve):
            cs1, sn1 = tab[:, C_COS1:C_COS1 + 32], tab[:, C_SIN1:C_SIN1 + 32]
            cs0, sn0 = tab[:, C_COS0:C_COS0 + 32], tab[:, C_SIN0:C_SIN0 + 32]

            def carrier(s, value):
                ve.wait_ge(s, value)
                ve.tensor_copy(beat[:, 1:2], beat[:, 0:1])

            def over_heads(ap, n):
                return ap.unsqueeze(1).to_broadcast([ap.shape[0], n, ap.shape[1]])

            def rotate_products(m1, m2, src, cs, sn, n):
                ve.tensor_tensor(m1, src[:, :, 32:64], over_heads(cs, n), ALU.mult)
                ve.tensor_tensor(m2[:, :, 0:16], src[:, :, 48:64], over_heads(sn[:, 0:16], n), ALU.mult)
                return ve.tensor_tensor(m2[:, :, 16:32], src[:, :, 32:48], over_heads(sn[:, 16:32], n), ALU.mult)

            ve.wait_ge(S["silu_t"], 1)
            ve.scalar_tensor_tensor(c_row[:, 1, :], c_row[:, 1, :], 1.0, c_row[:, 0, :], ALU.add, ALU.mult
                                    ).then_inc(S["silu_a"], 1)
            ve.wait_ge(S["silu_a"], 1)
            ve.tensor_scalar(c_row[:, 2, :], c_row[:, 1, :], 0.5, None, ALU.mult).then_inc(S["silu_row"], 1)
            ve.wait_ge(S["cT_ps"], 1)
            ve.tensor_copy(cT[:], ps[:, AO, 0:32].rearrange("p (h b) -> p h b", h=2)).then_inc(S["cT_copied"], 1)
            ve.wait_ge(S["mask_ld"], 16)
            ve.tensor_copy(mask16[:], mask_f.rearrange("p (a k) -> p a k", a=2))
            ve.wait_ge(S["tab_ld"], 16)
            ve.tensor_copy(id16[:], ident).then_inc(S["mask_done"], 1)
            ve.memset(take[:], TAKEN)
            ve.memset(beat[:], 0.0)
            ve.memset(den[:], 0.0).then_inc(S["chunk_done"], 2)
            ve.memset(rn[:], 0.0).then_inc(S["x_done"], 1)
            ve.wait_ge(S["lsc_exp"], 1)
            ve.tensor_scalar(lsc[:, 0, :], lsc[:, 1, :], 32.0 ** -0.5, None, ALU.mult).then_inc(S["lsc_done"], 1)
            ve.wait_ge(S["small_ld"], 48)
            ve.tensor_tensor(amp[:], amp[:], amp[:], ALU.mult).then_inc(S["amp_d"], 1)
            ve.wait_ge(S["amp_d"], 1)
            ve.tensor_tensor(ampp[:], amp[:, :, 0], amp[:, :, 1], ALU.add).then_inc(S["amp_d"], 1)
            ve.wait_ge(S["amp_d"], 2)
            ve.tensor_reduce(amps[:, 0:1], ampp[:], X, ALU.add).then_inc(S["amp_d"], 1)
            ve.wait_ge(S["amp_d"], 3)
            ve.tensor_scalar(amps[:, 1:2], amps[:, 0:1], EPS, None, ALU.add).then_inc(S["amp_d"], 1)
            ve.wait_ge(S["amp_d"], 4)
            ve.reciprocal(amps[:, 3:4], amps[:, 1:2]).then_inc(S["amp_d"], 1)
            ve.wait_ge(S["amp_d"], 5)
            ve.tensor_scalar(mix[:], ampp[:], amps[:, 3:4], amps[:, 2:3], ALU.mult, ALU.mult
                             ).then_inc(S["mix_done"], 1)
            ve.wait_ge(S["mod_ld"], 3)
            gates = modrow.rearrange("p (a k d) -> p a k d", a=2, k=3)[:, :, 2, :]
            ups = modrow.rearrange("p (a k d) -> p a k d", a=2, k=3)[:, :, 1, :]
            g_sign, g_neg = upd[0:B], prod[0:B, 0:2, :]
            ve.tensor_scalar(ups, ups, 1.0, None, ALU.add).then_inc(S["modrow_done"], 4)
            ve.wait_ge(S["mask_done"], 1)
            ve.tensor_scalar(g_sign, gates, 0.0, 2.0, ALU.is_ge, ALU.mult).then_inc(S["gate_fix"], 1)
            ve.wait_ge(S["gate_fix"], 1)
            ve.tensor_scalar(g_neg, gates, -1.0, None, ALU.mult).then_inc(S["gate_fix"], 1)
            ve.wait_ge(S["gate_fix"], 2)
            ve.tensor_tensor(gates, gates, g_neg, ALU.max).then_inc(S["gate_fix"], 1)
            ve.wait_ge(S["gate_fix"], 3)
            ve.tensor_scalar(gates, gates, 0.25, None, ALU.max).then_inc(S["gate_fix"], 1)
            ve.wait_ge(S["gate_fix"], 4)
            ve.scalar_tensor_tensor(gates, g_sign, -1.0, gates, ALU.add, ALU.mult).then_inc(S["gate_fix"], 1)
            ve.wait_ge(S["modT_ps"], 1)
            ve.tensor_copy(modT[:], ps[:, AO, 32:160].rearrange("p (k b) -> p b k", k=8)).then_inc(S["modT_done"], 1)
            for q in range(2):
                ve.wait_ge(S[f"x_ld{q}"], 16)
            for q in range(2, 4):
                ve.wait_ge(S[f"x_ld{q}"], 16)
            with ve.Fori(0, NT // 4) as i:
                for u in range(4):
                    ins = ve.bn_stats(bst4[:, u, :], x[:, 4 * i + u, :])
                ins.then_inc(S["bn1"], 1)
                carrier(S["bn1"], i + 1)
                for u in range(4):
                    ins = ve.bn_aggr(mv4[:, u, :], bst4[:, u, :])
                ins.then_inc(S["aggr1"], 1)
                ve.wait_ge(S["aggr1"], i + 1)
                ve.tensor_scalar(st[:, bass.ds(4 * i, 4), :], mv4[:], 1.0, None, ALU.mult).then_inc(S["stats_done"], 1)
            ve.wait_ge(S["lsc_done"], 1)
            for n, name in enumerate(("qs", "qg")):
                i = PIECES.index(name)
                ve.wait_ge(S[f"stage_ld{i % 2}"], loads_to(i))
                for h in range(2):
                    w = halves(stage[i % 2])[:, h, :].rearrange("p (h e) -> p h e", e=32)
                    ins = ve.tensor_tensor(w, w, lsc[:, 0, :].unsqueeze(2).to_broadcast([P, H, 32]), ALU.mult)
                ins.then_inc(S["q_scaled"], 1)
            zero = spare[:, 704:964]
            ve.memset(zero, 0.0).then_inc(S["z_zero"], 1)
            ve.wait_ge(S["z_zero"], 1)
            for k in (kT_h, kT_l):
                for s in range(2):
                    r = slice(64 - 64 * s, 128 - 64 * s)
                    ve.tensor_copy(k[r, :, s, :], zero[r].rearrange("p (t k) -> p t k", t=2))
            for v in (v_h, v_l):
                for s in range(2):
                    c = slice(64 - 64 * s, 128 - 64 * s)
                    ins = ve.tensor_copy(v[:, :, s, c], zero[:, 0:P].rearrange("p (t e) -> p t e", t=2))
            ins.then_inc(S["z_zero"], 1)

            ve.wait_ge(S["rs_done"], 1)
            ve.wait_ge(S["modT_done"], 1)
            ve.wait_ge(S["gates_st"], 32)
            with ve.Fori(0, B // 2) as i:
                for p in range(2):
                    b = 2 * i + p
                    ve.tensor_copy(mod_p[p][:], modT[:, b, 0:4])
                    for u, dst in ((0, xh0[p]), (1, xh1[p])):
                        ins = ve.tensor_scalar(dst, x[:, 2 * b + u, :], st[:, 2 * b + u, 0:1], rs1[:, bass.ds(2 * b + u, 1)],
                                               ALU.subtract, ALU.mult)
                    ins.then_inc(S["a_xh"], 1)
                for p in range(2):
                    b = 2 * i + p
                    ve.wait_ge(S["a_hf"], b + 1)
                    ve.tensor_copy(h0h[p][:], hf0[p]).then_inc(S["a_hi"], 1)
                    for h in range(2):
                        ins = ve.tensor_scalar(hpool[:, h, :, b], ps[:, p, 256 + 4 * h:260 + 4 * h],
                                               mod_p[p][:, h:h + 1], mod_p[p][:, 2 + h:3 + h], ALU.mult, ALU.add)
                    ins.then_inc(S["a_hp"], 1)
                    ve.wait_ge(S["a_hi"], b + 1)
                    ve.tensor_tensor(h0l[p][:], hf0[p], h0h[p][:].bitcast(F32), ALU.subtract
                                     ).then_inc(S["a_lo"], 1)
                for p in range(2):
                    b = 2 * i + p
                    ve.wait_ge(S["a_ksem"], b + 1)
                    src = ps[:, 2 + p, 0:KC].rearrange("p (g e) -> p g e", e=DH)
                    rotate_products(rk1[p], rk2[p], src, cs0, sn0, HKV).then_inc(S["a_km"], 1)
                for p in range(2):
                    b = 2 * i + p
                    ve.wait_ge(S["a_km"], b + 1)
                    ve.tensor_tensor(kr0[p].rearrange("p (g e) -> p g e", e=DH)[:, :, 32:64], rk1[p], rk2[p],
                                     ALU.add).then_inc(S["a_krot"], 1)
                for p in range(2):
                    b = 2 * i + p
                    ve.wait_ge(S["a_kp_ps"], b + 1)
                    ve.tensor_scalar(kpool[:, b], ps[:, 4 + p, 0:4].rearrange("p (t k) -> p t k", t=2), 1.0, None,
                                     ALU.mult).then_inc(S["a_kp"], 1)

            ve.wait_ge(S["a_hp"], B)
            ve.tensor_copy(hp_h, hpool).then_inc(S["hp_hi"], 1)
            ve.wait_ge(S["hp_hi"], 1)
            ve.tensor_tensor(hp_l, hpool, hp_h.bitcast(F32), ALU.subtract).then_inc(S["hp_lo"], 1)
            ve.memset(kpz_h[:].bitcast(F32), 0.0)
            ve.memset(kpz_l[:].bitcast(F32), 0.0).then_inc(S["kpz"], 1)
            ve.wait_ge(S["kpz"], 1)
            ve.wait_ge(S["a_kp"], B)
            for s in range(2):
                r = slice(64 * s, 64 * s + 64)
                ins = ve.tensor_copy(kpz_h[r, :, :, s, :], kpool[r])
            ins.then_inc(S["kpz"], 1)
            ve.wait_ge(S["kpz"], 2)
            for s in range(2):
                r = slice(64 * s, 64 * s + 64)
                ve.tensor_tensor(kpz_l[r, :, :, s, :], kpool[r], kpz_h[r, :, :, s, :].bitcast(F32), ALU.subtract)
            ve.wait_ge(S["z_v_ps"], 1)
            ve.wait_ge(S["piece_lo"], len(SPLIT))
            ve.tensor_copy(vrow, ps[0:B, 0:2, :].rearrange("p a n -> p (a n)")[:, 0:768]
                           .rearrange("p (r n) -> p r n", r=3)).then_inc(S["z_v_copied"], 1)
            csl = tab[0:B, C_COSL:C_COSL + 32]
            snl = tab[0:B, C_SINL:C_SINL + 32]
            z = [0]

            def link(ins):
                z[0] += 1
                ins.then_inc(S["z_chain"], 1)
                ve.wait_ge(S["z_chain"], z[0])

            ve.wait_ge(S["z_q_ps"], 1)
            q_ps = ps[0:B, 2:4, :].rearrange("p a (h e) -> p (a h) e", e=DH)
            ve.tensor_copy(q127[:, :, 0:32], q_ps[:, :, 0:32])
            link(rotate_products(dots[:, :, 0:32], dots[:, :, 32:64], q_ps, csl, snl, H))
            ve.tensor_tensor(q127[:, :, 32:64], dots[:, :, 0:32], dots[:, :, 32:64], ALU.add)
            ve.wait_ge(S["z_kp_ps"], 1)
            ins = ve.tensor_copy(kprow, ps[0:B, 4, :].rearrange("p (k n) -> p k n", k=NP))
            link(ins)
            for k in range(NP):
                for t in range(2):
                    kk = kprow[:, k, P * t:P * t + P].unsqueeze(1).to_broadcast([B, 4, P])
                    q4 = q127[:, 8 * t:8 * t + 8, :].rearrange("p (j s) e -> p j (s e)", j=4)
                    d4 = dots[:, 8 * t:8 * t + 8, :].rearrange("p (j s) e -> p j (s e)", j=4)
                    ins = ve.tensor_tensor(d4, q4, kk, ALU.mult)
                link(ins)
                link(ve.tensor_reduce(s127[:, k, :], dots, X, ALU.add))
            link(ve.tensor_tensor(sm127[:, 4, :], s127[:, 0, :], s127[:, 1, :], ALU.max))
            for k in range(NP):
                ins = ve.tensor_tensor(sm127[:, k, :], s127[:, k, :], sm127[:, 4, :], ALU.subtract)
            link(ins)
            assert z[0] == Z_MAX
            ve.wait_ge(S["z_exp"], 1)
            link(ve.tensor_tensor(sm127[:, 4, :], sm127[:, 2, :], sm127[:, 3, :], ALU.add))
            link(ve.reciprocal(sm127[:, 5, :], sm127[:, 4, :]))
            for k in range(NP):
                ins = ve.tensor_tensor(s127[:, k, :], sm127[:, 2 + k, :], sm127[:, 5, :], ALU.mult)
            link(ins)
            for k in range(NP):
                for t in range(2):
                    dst = (dots, tmpq)[k][:, 8 * t:8 * t + 8, :]
                    vv = vrow[:, 1 + k, P * t:P * t + P].unsqueeze(1).to_broadcast([B, 4, P])
                    pp = s127[:, k, 8 * t:8 * t + 8].unsqueeze(2).to_broadcast([B, 8, DH])
                    link(ve.tensor_copy(dst.rearrange("p (j s) e -> p j (s e)", j=4), vv))
                    ins = ve.tensor_tensor(dst, dst, pp, ALU.mult)
            link(ins)
            link(ve.tensor_tensor(tmpq, tmpq, dots, ALU.add))
            assert z[0] == Z_ROW_C
            ve.wait_ge(S["z_vT_ps"], 1)
            ve.tensor_copy(vTf, ps[:, 5, 0:64].rearrange("p (t n) -> p t n", t=2)).then_inc(S["z_vT"], 1)
            ve.wait_ge(S["z_vT"], 1)
            ve.tensor_copy(pT_h[:, :, 0:32], vTf).then_inc(S["z_vT_hi"], 1)
            ve.wait_ge(S["z_vT_hi"], 1)
            ve.tensor_tensor(pT_l[:, :, 0:32], vTf, pT_h[:, :, 0:32].bitcast(F32), ALU.subtract
                             ).then_inc(S["z_vT_lo"], 1)
            ve.wait_ge(S["z_row_ps"], 1)
            for r in range(2):
                for t in range(2):
                    ve.tensor_copy(rT[:, 4 * t:4 * t + 4, r, :], ps[:, 6, 16 * (2 * r + t):16 * (2 * r + t) + 16]
                                   .unsqueeze(1).to_broadcast([P, 4, B]))
            ve.tensor_copy(rT[:, :, 2, :], ps[:, 6, 64:192].rearrange("p (j b) -> p j b", j=8)
                           ).then_inc(S["z_rT"], 1)
            ve.wait_ge(S["z_rT"], 1)
            rT2 = rT.rearrange("p j r b -> p j (r b)")
            ve.tensor_copy(qT_h[:, :, 0:48], rT2).then_inc(S["z_rT_hi"], 1)
            ve.wait_ge(S["z_rT_hi"], 1)
            ve.tensor_tensor(qT_l[:, :, 0:48], rT2, qT_h[:, :, 0:48].bitcast(F32), ALU.subtract
                             ).then_inc(S["z_rT_lo"], 1)
            ve.wait_ge(S["z_rows_ps"], 1)
            ve.tensor_copy(rows_sb, ps[0:48, 7, 0:D]).then_inc(S["z_rows"], 1)
            for j in range(8):
                ve.wait_ge(S["z_vw_ps"], j + 1)
                if j == 4:
                    ve.wait_ge(S["z_vw_st"], 32)
                for s in range(2):
                    ins = ve.tensor_copy(vws[:, (2 * j + s) % 8, :], ps[0:NP * B, 2 * (j % 2) + s, 0:D])
                ins.then_inc(S["z_vw"], 1)
            ve.wait_ge(S["z_vw_st"], 64)
            ve.wait_ge(S["z_rows_st"], 16)

            def normed(b):
                ve.tensor_scalar(mod_a[:], modT[:, b, 0:4], 1.0, None, ALU.mult)
                ve.tensor_scalar(xh[:], x[:, 2 * b + 1, :], st[:, 2 * b + 1, 0:1], rs1[:, bass.ds(2 * b + 1, 1)],
                                 ALU.subtract, ALU.mult).then_inc(S["xh_ready"], 1)

            def split_h(b):
                ve.wait_ge(S["h_hi"], b + 1)
                ve.tensor_tensor(hl[:], hf[:], hh[:].bitcast(F32), ALU.subtract).then_inc(S["h_lo"], 1)

            def rotate_k(b):
                ve.wait_ge(S["k_sem"], b + 1)
                rotate_products(rot1[:, H:], rot2[:, H:], ps[:, A2, 0:KC].rearrange("p (g e) -> p g e", e=DH),
                                cs1, sn1, HKV).then_inc(S["k_m"], 1)

            def split_v(b):
                ve.wait_ge(S["v_hi"], b + 1)
                ve.tensor_tensor(beside(v_l), ps[:, A3, 256:512].rearrange("p (t s e) -> p t s e", t=2, s=2),
                                 beside(v_h).bitcast(F32), ALU.subtract).then_inc(S["v_lo"], 1)

            def rotate_q(b):
                ve.wait_ge(S["q_sem"], b + 1)
                rotate_products(rot1[:, 0:H], rot2[:, 0:H],
                                ps[:, A0:A0 + 2, :].rearrange("p a (h e) -> p (a h) e", e=DH),
                                cs1, sn1, H).then_inc(S["q_m"], 1)

            def split_k(b):
                ve.wait_ge(S["kT_hi"], b + 1)
                for s in range(2):
                    r = slice(64 * s, 64 * s + 64)
                    ins = ve.tensor_tensor(kT_l[r, :, s, 0:P], ps[r, A2, 0:256].rearrange("p (t k) -> p t k", t=2),
                                           kT_h[r, :, s, 0:P].bitcast(F32), ALU.subtract)
                ve.tensor_scalar(kT_h[:, :, :, P:NK], kpz_h[:, b], 1.0, None, ALU.mult)
                ve.tensor_scalar(kT_l[:, :, :, P:NK], kpz_l[:, b], 1.0, None, ALU.mult).then_inc(S["kT_lo"], 1)

            def split_q(b):
                for t in range(2):
                    ve.wait_ge(S["qT_hi"], 2 * b + t + 1)
                    ve.tensor_tensor(qT_l[:, 4 * t:4 * t + 4, :], ps[:, A0 + t, :].rearrange("p (j k) -> p j k", j=4),
                                     qT_h[:, 4 * t:4 * t + 4, :].bitcast(F32), ALU.subtract
                                     ).then_inc(S["qT_lo"], 1)

            def maxima(b, g):
                ve.wait_ge(S["s_ps"], 8 * b + g + 1)
                ve.tensor_reduce(nmax[:, 2 * g:2 * g + 2],
                                 ps[:, A0 + g % 3, 0:2 * NK].rearrange("p (s k) -> p s k", k=NK), X, ALU.max,
                                 negate=True).then_inc(S["nmax_ready"], 1)

            def inverse_sums(b, t):
                ve.wait_ge(S["exp_done"], 8 * b + 4 * t + 4)
                ve.reciprocal(rinv[:, 8 * t:8 * t + 8], psums[:, 8 * t:8 * t + 8]).then_inc(S["rinv_ready"], 1)

            def split_probs(b, t, s):
                ve.wait_ge(S["pT_hi"], 4 * b + 2 * t + s + 1)
                ve.tensor_tensor(pT_l[:, s, :], ps[:, A3, :], pT_h[:, s, :].bitcast(F32), ALU.subtract
                                 ).then_inc(S["pT_lo"], 1)

            def split_out(b, t):
                ve.wait_ge(S["oT_hi_r"], 2 * b + t + 1)
                ve.tensor_tensor(oT_l[:, 4 * t:4 * t + 4, :], ps[:, AO, :].rearrange("p (j k) -> p j k", j=4),
                                 oT_h[:, 4 * t:4 * t + 4, :].bitcast(F32), ALU.subtract
                                 ).then_inc(S["oT_lo_r"], 1)

            def add_attention(b):
                ve.wait_ge(S["gate_a_ld"], 16 * b + 16)
                ve.wait_ge(S["row_ps"], b + 1)
                ve.tensor_tensor(upd[:, 0, :], ps[:, A3, 0:D], gate_a[:], ALU.mult).then_inc(S["upd_ready"], 1)
                ve.wait_ge(S["upd_ready"], 2 * b + 1)
                ve.tensor_tensor(x[:, 2 * b, :], x[:, 2 * b, :], upd[:, 0, :], ALU.add)
                ve.wait_ge(S["y_ps"], b + 1)
                ve.tensor_tensor(upd[:, 1, :], ps[:, AO, 0:D], gate_a[:], ALU.mult).then_inc(S["upd_ready"], 1)
                ve.wait_ge(S["upd_ready"], 2 * b + 2)
                ve.tensor_tensor(x[:, 2 * b + 1, :], x[:, 2 * b + 1, :], upd[:, 1, :], ALU.add
                                 ).then_inc(S["x_mid"], 1)

            def f_norm(n, f, u):
                if u == 0:
                    ve.wait_ge(S["x_mid"], f + 1)
                    ve.tensor_scalar(mod_f[:], modT[:, f, 4:8], 1.0, None, ALU.mult)
                ve.bn_stats(bst[:], x[:, n, :]).then_inc(S["f_bn"], 1)
                carrier(S["f_bn"], n + 1)
                ve.bn_aggr(mv[:], bst[:]).then_inc(S["f_var"], 1)
                ve.wait_ge(S["f_rs"], n + 1)
                ve.wait_ge(S["f_var"], n + 1)
                ve.tensor_scalar(xh2, x[:, n, :], mv[:, 0:1], rs2[:, 0:1], ALU.subtract, ALU.mult
                                 ).then_inc(S["f_xh"], 1)

            def f_split(n, u):
                ve.wait_ge(S["f_hi"], n + 1)
                ve.tensor_tensor(fl[u][:], hf2, fh[u][:].bitcast(F32), ALU.subtract).then_inc(S["f_lo"], 1)

            def f_top4(n):
                ve.wait_ge(S["l_ps"], n + 1)
                ve.tensor_copy(lg[:], ps[:, FM, 256:384]).then_inc(S["lg_ready"], 1)
                ve.max(top8[:], ps[:, FM, 256:384]).then_inc(S["top_ready"], 1)
                ve.wait_ge(S["top_ready"], n + 1)
                ve.tensor_copy(take[:, 0:4], top8[:, 0:4]).then_inc(S["take_ready"], 1)
                ve.wait_ge(S["take_ready"], n + 1)
                ve.tensor_scalar(nm[:], top8[:, 0:1], -1.0, None, ALU.mult).then_inc(S["nm_ready"], 1)
                ve.match_replace(rest[:], take[:], lg[:], TAKEN).then_inc(S["rest_ready"], 1)

            def f_coefficients(n):
                ve.wait_ge(S["rest_ready"], n + 1)
                ve.wait_ge(S["ex_ready"], n + 1)
                ve.scalar_tensor_tensor(coef[:], rest[:], 0.999 * TAKEN, ex[:], ALU.is_le, ALU.mult,
                                        accum_out=s4[:]).then_inc(S["coef_ready"], 1)
                ve.wait_ge(S["coef_ready"], n + 1)
                ve.scalar_tensor_tensor(den[:, 0:1], zsum[:], EPS, s4[:], ALU.mult, ALU.add
                                        ).then_inc(S["den_ready"], 1)
                ve.wait_ge(S["den_ready"], n + 1)
                ve.reciprocal(den[:, 1:2], den[:, 0:1]).then_inc(S["rcp_ready"], 1)
                ve.wait_ge(S["rcp_ready"], n + 1)

            def f_weights(n, u):
                ve.wait_ge(S["w_ps"], n + 1)
                ve.tensor_scalar(w8[u][:], ps[:, FM, 0:NB], den[:, 1:2], 0.5, ALU.mult, ALU.mult
                                 ).then_inc(S["w8_ready"], 1)

            def f_chunk(n, u, k):
                r = (k + u) % 2
                ve.wait_ge(S["th_ready"], NCH * n + k + 1)
                bank = ps[:, FR + r, :]
                ve.scalar_tensor_tensor(act_g[r], th[r], 1.0, bank[:, 0:256], ALU.add, ALU.mult
                                        ).then_inc(S["ag_ready"], 1)
                ve.wait_ge(S["ag_ready"], NCH * n + k + 1)
                if k == 0:
                    ve.scalar_tensor_tensor(shared[u][:], act_g[r], 0.5, bank[:, 256:512], ALU.mult, ALU.mult
                                            ).then_inc(S["chunk_done"], 1)
                    return
                if k == 1:
                    ve.wait_ge(S["w8_ready"], n + 1)
                if not (isinstance(n, int) and n == 0):
                    ve.wait_ge(S["mix_sum"], 3 * n - 3 + max(1, k - 1))
                for i in range(2):
                    ins = ve.scalar_tensor_tensor(prod[:, k - 1, P * i:P * i + P], act_g[r][:, P * i:P * i + P],
                                                  w8[u][:, 2 * (k - 1) + i:2 * (k - 1) + i + 1],
                                                  bank[:, 256 + P * i:256 + P * i + P], ALU.mult, ALU.mult)
                ins.then_inc(S["chunk_done"], 1)

            def f_inner(n):
                ve.wait_ge(S["mT_hi_r"], n + 1)
                ve.tensor_tensor(mT_l[:], ps[:, FM, 0:384].rearrange("p (k n) -> p k n", k=3),
                                 mT_h[:].bitcast(F32), ALU.subtract).then_inc(S["mT_lo_r"], 1)

            def f_add(n, f, u):
                ve.wait_ge(S["d_ps"], n + 1)
                if u == 0:
                    ve.wait_ge(S["gate_f_ld"], 16 * f + 16)
                ve.tensor_tensor(updf[:], ps[:, FM, 0:D], gate_f[:], ALU.mult).then_inc(S["updf_ready"], 1)
                ve.wait_ge(S["updf_ready"], n + 1)
                ve.tensor_tensor(x[:, n, :], x[:, n, :], updf[:], ALU.add).then_inc(S["x_done"], 1)

            def body(b, back, front):
                m0, m1, m2 = 2 * b - 3, 2 * b - 2, 2 * b - 1
                if front:
                    normed(b + 1)
                if back:
                    maxima(b, 0)
                    maxima(b, 1)
                if real(m0):
                    f_chunk(m0, 1, 0)
                if back:
                    maxima(b, 2)
                    maxima(b, 3)
                if real(m1):
                    f_norm(m1, b - 1, 0)
                if real(m0):
                    f_chunk(m0, 1, 1)
                if front:
                    split_h(b + 1)
                if back:
                    inverse_sums(b, 0)
                    maxima(b, 4)
                    maxima(b, 5)
                if real(m1):
                    f_split(m1, 0)
                if back:
                    maxima(b, 6)
                if real(m1 - 2):
                    f_inner(m1 - 2)
                if real(m0):
                    f_chunk(m0, 1, 2)
                if back:
                    maxima(b, 7)
                if real(m1):
                    f_top4(m1)
                if back:
                    split_probs(b, 0, 0)
                if real(m1):
                    f_coefficients(m1)
                if real(m1 - 2):
                    f_add(m1 - 2, b - 2, 0)
                if back:
                    inverse_sums(b, 1)
                if real(m0):
                    f_chunk(m0, 1, 3)
                if back:
                    split_probs(b, 0, 1)
                if front:
                    rotate_k(b + 1)
                if real(m0):
                    f_chunk(m0, 1, 4)
                if front:
                    rotate_q(b + 1)
                if real(m1):
                    f_weights(m1, 0)
                if back:
                    split_out(b, 0)
                    split_probs(b, 1, 0)
                if real(m2):
                    f_norm(m2, b - 1, 1)
                if front:
                    split_k(b + 1)
                if back:
                    split_probs(b, 1, 1)
                if real(m1):
                    f_chunk(m1, 0, 0)
                    f_chunk(m1, 0, 1)
                if real(m2):
                    f_split(m2, 1)
                if real(m0):
                    f_inner(m0)
                if front:
                    split_q(b + 1)
                if back:
                    split_out(b, 1)
                if front:
                    split_v(b + 1)
                if real(m2):
                    f_top4(m2)
                if real(m1):
                    f_chunk(m1, 0, 2)
                if real(m2):
                    f_coefficients(m2)
                if real(m0):
                    f_add(m0, b - 2, 1)
                if real(m1):
                    f_chunk(m1, 0, 3)
                if back:
                    add_attention(b)
                if real(m2):
                    f_weights(m2, 1)
                if real(m1):
                    f_chunk(m1, 0, 4)

            normed(0)
            split_h(0)
            rotate_k(0)
            rotate_q(0)
            split_k(0)
            split_q(0)
            split_v(0)
            body(0, True, True)
            body(1, True, True)
            with ve.Fori(2, B - 1) as b:
                body(b, True, True)
            body(B - 1, True, False)
            body(B, False, False)
            body(B + 1, False, False)


JH_ = H // HKV
Z_MAX = 8
Z_ROW_C = 17


_INS = ['L0_attn_x', 'L0_attn_Wq_sem', 'L0_attn_Wk_sem', 'L0_attn_Wq_geo', 'L0_attn_Wk_geo', 'L0_attn_Wv',
        'L0_attn_Wo', 'L0_attn_logit_scale', 'L0_ffn_w_router', 'L0_ffn_w_gate', 'L0_ffn_w_up', 'L0_ffn_w_down',
        'L0_ffn_amplitudes', 'L0_ffn_expert_scale', 'L0_ffn_shared_w_gate', 'L0_ffn_shared_w_up',
        'L0_ffn_shared_w_down', 'L0_c', 'L0_wmod']


def constants():
    import numpy as np

    tab = np.zeros((P, NTAB), np.float32)
    tab[:, C_ID:C_ID + P] = np.eye(P)
    freq = (1.0 / np.float32(10000.0) ** (np.arange(0, 32, 2, dtype=np.float32) / np.float32(32))).astype(np.float32)

    def rotary(pos, c, s):
        ang = (pos.astype(np.float32)[:, None] * freq).astype(np.float32)
        tab[:, c:c + 32] = np.concatenate([np.cos(ang), np.cos(ang)], 1)
        tab[:, s:s + 32] = np.concatenate([-np.sin(ang), np.sin(ang)], 1)

    rotary(np.arange(P, 2 * P), C_COS1, C_SIN1)
    rotary(np.arange(P), C_COS0, C_SIN0)
    rotary(np.full(P, P - 1), C_COSL, C_SINL)
    tab[0:64, C_POOL0] = 1.0 / 64
    tab[64:P, C_POOL0 + 1] = 1.0 / 64
    tab[P - 1, C_POOL0 + 2] = 1.0
    tab[:, C_POOL0 + 3] = 1.0 / (64 * NK)
    tab[:, C_POOL1 + 3] = 1.0 / NK
    tab[NP * H, C_SEL:C_SEL + 63] = 1.0
    tab[NP * H + 1, C_SEL + 63:C_SEL + P - 1] = 1.0
    tab[NP * H + 2, C_SEL + P - 1] = 1.0
    mask = np.zeros((P, 2, NK), np.float32)
    mask[:, :, 0:P] = np.where(np.arange(P)[None, :] <= np.arange(P)[:, None], 0.0, HIDE)[:, None, :]
    return tab, mask.reshape(P, 2 * NK)


def kernel(**inputs):
    import numpy as np
    import concourse.bacc as bacc
    from concourse.bass_utils import run_bass_kernel_spmd

    nc = bacc.Bacc("TRN2", target_bir_lowering=False, num_devices=1)
    tab, mask = constants()
    arrays, args = {}, []
    named = [(n, np.ascontiguousarray(inputs[n])) for n in _INS] + [("table", tab), ("mask", mask)]
    for name, a in named:
        arrays[f"in_{name}_dram"] = a
        args.append(nc.dram_tensor(f"in_{name}_dram", a.shape, mybir.dt.from_np(a.dtype), kind="ExternalInput").ap())
    args.append(nc.dram_tensor("out_0_dram", (B, T, D), F32, kind="ExternalOutput").ap())
    build(nc, *args)
    r = run_bass_kernel_spmd(nc, [arrays], core_ids=[0])
    return r.results[0]["out_0_dram"]
```

```python
from contextlib import ExitStack

import concourse.bass as bass
from concourse import mybir

ALU = mybir.AluOpType
ACT = mybir.ActivationFunctionType
F32 = mybir.dt.float32
F32R = mybir.dt.float32r
BF16 = mybir.dt.bfloat16
X = mybir.AxisListType.X

P = 128
B, T, D = 16, 256, 256
NT = B * T // P
H, HKV, DH = 16, 4, 64
NP = 2
NK = P + NP
QC, KC, VC = H * DH, HKV * DH, HKV * DH
QKV = QC + KC + VC
NE, NB = 128, 8
NCH = 5
LN_EPS, EPS = 1e-5, 1e-8
HIDE = -float(2 ** 30)
TAKEN = -3.0e38

C_ID = 0
C_COS1 = C_ID + P
C_SIN1 = C_COS1 + 32
C_COSL = C_SIN1 + 32
C_SINL = C_COSL + 32
C_ROT = C_SINL + 32
C_POOL0 = C_ROT + 64
C_POOL1 = C_POOL0 + 4
C_WS = C_POOL1 + 4
C_DI = C_WS + 64
C_DB = C_DI + 16
C_SEL = C_DB + 8
NTAB = C_SEL + P

A0, A1, A2, A3, AO, FM, FR = 0, 1, 2, 3, 4, 5, 6


def build(nc, x_in, wq_sem, wk_sem, wq_geo, wk_geo, wv, wo, logit_scale, w_router, w_gate, w_up,
          w_down, amplitudes, expert_scale, sw_gate, sw_up, sw_down, c_in, wmod, table, mask_in, out):
    gates_dram = nc.dram_tensor("gates", [B, 2, D], F32, kind="Internal").ap()
    rows_dram = nc.dram_tensor("rows", [3, B, D], F32, kind="Internal").ap()
    vw_dram = nc.dram_tensor("vw", [B, NP, H, D], F32, kind="Internal").ap()

    with ExitStack() as ctx:
        def sb(name, shape, dt=F32):
            return ctx.enter_context(nc.sbuf_tensor(name, shape, dt))

        def sem(name):
            return ctx.enter_context(nc.semaphore(name))

        ps = ctx.enter_context(nc.psum_tensor("ps", [P, 8, 512], F32))

        tab = sb("tab", [P, NTAB])
        ident = tab[:, C_ID:C_ID + P]
        rot_pool, pool1 = tab[:, C_ROT:C_ROT + 68], tab[:, C_POOL1:C_POOL1 + 4]
        x = sb("x", [P, NT, D])
        st = sb("st", [P, NT, 2])
        rs1 = sb("rs1", [P, NT])
        modT = sb("modT", [P, B, 8])
        wqkv_h = sb("wqkv_h", [P, 2, QKV], F32R)
        wqkv_l = sb("wqkv_l", [P, 2, QKV], F32R)
        wo_h = sb("wo_h", [P, 8, D], F32R)
        wo_l = sb("wo_l", [P, 8, D], F32R)
        wgu_h = sb("wgu_h", [P, 2, NCH, 512], F32R)
        wgu_l = sb("wgu_l", [P, 2, NCH, 512], F32R)
        wr_h = sb("wr_h", [P, 2, NE], F32R)
        wr_l = sb("wr_l", [P, 2, NE], F32R)
        wd_h = sb("wd_h", [P, 3, D], F32R)
        wd_l = sb("wd_l", [P, 3, D], F32R)
        mix = sb("mix", [P, NB])
        kpool = sb("kpool", [P, B, 2, NP])
        kpz_h = sb("kpz_h", [P, B, 2, 2, NP], F32R)
        kpz_l = sb("kpz_l", [P, B, 2, 2, NP], F32R)
        id16 = sb("id16", [P, P], BF16)
        mask16 = sb("mask16", [P, 2, NK], BF16)
        mhalf = sb("mhalf", [P, NT])

        probs = sb("probs", [P, H, NK])
        early = sb("early", [P, 1920])
        qk = early[:, 0:QC + KC].rearrange("p (h e) -> p h e", e=DH)
        rot1 = qk[:, :, 32:64]
        rot2 = early[:, 1280:1920].rearrange("p (h e) -> p h e", e=32)
        gate_a = sb("gate_a", [P, D])
        gate_f = sb("gate_f", [P, D])
        entry = sb("entry", [NP * H + 3, D])
        vwb = entry[0:NP * H]
        rowb = entry[NP * H:]
        mod_a = sb("mod_a", [P, 4])
        mod_f = sb("mod_f", [P, 4])
        xh = sb("xh", [P, D])
        hf = sb("hf", [P, 2, P])
        hh = sb("hh", [P, 2, P], F32R)
        hl = sb("hl", [P, 2, P], F32R)
        qT_h = sb("qT_h", [P, 8, P], F32R)
        qT_l = sb("qT_l", [P, 8, P], F32R)
        kT_h = sb("kT_h", [P, 2, 2, NK], F32R)
        kT_l = sb("kT_l", [P, 2, 2, NK], F32R)
        v_h = sb("v_h", [P, 2, 2, P], F32R)
        v_l = sb("v_l", [P, 2, 2, P], F32R)
        nmax = sb("nmax", [P, H])
        psums = sb("psums", [P, H])
        rinv = sb("rinv", [P, H])
        pT_h = sb("pT_h", [P, 2, 512], F32R)
        pT_l = sb("pT_l", [P, 2, 512], F32R)
        pp = sb("pp", [P, NP, H])
        ppT = sb("ppT", [NP * H, P])
        oT_h = sb("oT_h", [P, 8, P], F32R)
        oT_l = sb("oT_l", [P, 8, P], F32R)
        upd = sb("upd", [P, 2, D])

        both = sb("both", [P, 2048])
        stage = [both[:, 1024 * i:1024 * i + 1024] for i in range(2)]
        th = [stage[0][:, 256 * i:256 * i + 256] for i in range(2)]
        act_g = [stage[0][:, 512 + 256 * i:768 + 256 * i] for i in range(2)]
        acc = stage[1][:, 0:256]
        mixed = [stage[1][:, 256 + 128 * i:384 + 128 * i] for i in range(2)]
        xh2 = stage[1][:, 512:768]
        hf2 = stage[1][:, 768:1024].rearrange("p (h n) -> p h n", h=2)
        prod = sb("prod", [P, 4, 256])
        shared2 = sb("shared", [P, 2, 256])
        shared = [shared2[:, u] for u in range(2)]
        bst = sb("bst", [P, 6])
        beat = sb("beat", [P, 2])
        leps = sb("leps", [P, 1])
        mv = sb("mv", [P, 2])
        veps = sb("veps", [P, 1])
        rs2 = sb("rs2", [P, 1])
        fh2, fl2 = sb("fh", [P, 2, 2, P], F32R), sb("fl", [P, 2, 2, P], F32R)
        fh, fl = [fh2[:, u] for u in range(2)], [fl2[:, u] for u in range(2)]
        lg = sb("lg", [P, NE])
        top8 = sb("top8", [P, 8])
        take = sb("take", [P, 8])
        nm = sb("nm", [P, 1])
        rest = sb("rest", [P, NE])
        ex = sb("ex", [P, NE])
        zsum = sb("zsum", [P, 1])
        s4 = sb("s4", [P, 1])
        den = sb("den", [P, 2])
        rn = sb("rn", [P, 1])
        coef = sb("coef", [P, NE])
        coefT = lg
        w8 = [sb(f"w8_{u}", [P, NB]) for u in range(2)]
        mT_h = sb("mT_h", [P, 3, P], F32R)
        mT_l = sb("mT_l", [P, 3, P], F32R)
        updf = sb("updf", [P, D])

        spare = probs[:].rearrange("p h k -> p (h k)")
        c_row = spare[0:B, 0:768].rearrange("p (a d) -> p a d", a=3)
        modrow = early[0:B, 0:6 * D]
        cT = sb("cT", [P, 2, B])
        bst4 = sb("bst4", [P, 4, 6])
        mv4 = sb("mv4", [P, 4, 2])
        lsc = sb("lsc", [P, 2, H])
        amp = sb("amp", [P, NB, 2])
        ampp = sb("ampp", [P, NB])
        amps = sb("amps", [P, 4])
        mask_f = upd[:].rearrange("p a d -> p (a d)")[:, 0:2 * NK]
        xh0 = [early[:, 512 * i:512 * i + 256] for i in range(2)]
        xh1 = [early[:, 512 * i + 256:512 * i + 512] for i in range(2)]
        mt = [early[:, 1024 + 136 * i:1160 + 136 * i].rearrange("p (h c) -> p h c", h=2) for i in range(2)]
        hpool = early[:, 1296:1424].rearrange("p (h r b) -> p h r b", h=2, r=4)
        hp_h, hp_l = [q[:, :, 64:64 + B].rearrange("p (h r) b -> p h r b", h=2) for q in (qT_h, qT_l)]
        ht = spare[:, 0:2048].rearrange("p (h c b i) -> p h c b i", h=2, c=4, b=B)
        ht_h = [oT_h[:].rearrange("p j n -> p (j n)"), oT_l[:].rearrange("p j n -> p (j n)")]
        ht_l = [pT_h[:].rearrange("p j n -> p (j n)"), pT_l[:].rearrange("p j n -> p (j n)")]
        diag = spare[:, 0:1024]
        spread = spare[:, 1024:2048].rearrange("p (x e) -> p x e", e=DH)
        vTf = ex[:, 0:64].rearrange("p (t n) -> p t n", t=2)
        prod_row = prod[:].rearrange("p a n -> p (a n)")
        q127 = prod_row[0:B].rearrange("p (h e) -> p h e", e=DH)
        dots, tmpq = [stage[i][0:B].rearrange("p (h e) -> p h e", e=DH) for i in range(2)]
        kprow = shared2[0:B]
        vrow = [a[0:B] for a in (updf[:], gate_f[:], upd[:, 0, :])]
        s127 = coef[0:B, 0:32].rearrange("p (k h) -> p k h", k=NP)
        sm127 = coef[0:B, 32:128].rearrange("p (k h) -> p k h", k=6)
        rT = prod_row[:, 0:8 * 48].rearrange("p (j r b) -> p j r b", j=8, r=3)
        rT_h, rT_l = [f[:].rearrange("p u h n -> p (u h n)")[:, 0:8 * 48].rearrange("p (j r) -> p j r", j=8)
                      for f in (fh2, fl2)]
        vT_h, vT_l = mT_h[:, 0:2, 0:32], mT_l[:, 0:2, 0:32]
        vws = both[0:NP * B].rearrange("p (h n) -> p h n", n=D)
        rows_sb = updf[0:48, :]

        names = """tab_ld mask_ld c_ld mod_ld small_ld stage_ld0 stage_ld1 x_ld0 x_ld1 x_ld2 x_ld3
        silu_t silu_a silu_row cT_ps cT_copied mod_ps modrow_done gate_fix modT_ps modT_done gates_st
        lsc_exp lsc_done amp_d mix_done mask_done const_done q_scaled piece_hi piece_lo
        bn1 aggr1 stats_done rs_var rs_done
        a_xh a_ps a_mt a_post ht_hi ht_lo a_kps a_diag a_spread a_kp_ps a_kp
        hp_hi hp_lo z_v_ps z_v_copied z_q_ps z_kp_ps z_chain z_exp z_row_ps z_rT z_rT_hi
        z_rT_lo z_vT_ps z_vT z_vT_hi z_vT_lo z_rows_ps z_rows z_rows_st z_vw_ps z_vw z_vw_st z_zero
        gate_a_ld gate_f_ld vw_ld row_ld
        mod_a_ready xh_ready hT_ps hf_ready h_hi h_lo k_ps q_ps v_ps k_sem v_hi q_sem v_lo k_m q_m k_rot q_rot
        kT_ps qT_ps kpz kT_hi kT_lo qT_hi qT_lo s_ps nmax_ready exp_done rinv_ready p_ready
        pT_ps pT_hi pT_lo o_ps oT_hi_r oT_lo_r pp_ps ppT_ready row_ps y_ps upd_ready x_mid
        f_bn f_var f_veps f_rs f_xh f_mod f_hT_ps f_hf f_hi f_lo l_ps lg_ready top_ready nm_ready take_ready
        rest_ready ex_ready coef_ready den_ready rcp_ready rn_ready cT2_ps cT2_ready w_ps w8_ready
        gu_ps th_ready ag_ready chunk_done mix_sum mixed_ready m_ps mT_hi_r mT_lo_r d_ps updf_ready x_done
        out_st""".split()
        S = {n: sem(n) for n in names}

        block = ctx.enter_context(nc.Block())

        def d_rows(ap):
            return ap.rearrange("(h p) n -> p h n", p=P)

        def halves(stg):
            return stg[:].rearrange("p (h n) -> p h n", h=2)

        wo_rows = wo.rearrange("(t s j e) n -> s t e j n", t=2, s=2, j=JH_)

        PIECES = ["m0", "m1", "m2", "kv", "qs", "qg", "o0", "o1", "rd", "g0", "u0", "g1", "u1", "sh"]
        SPLIT = PIECES[3:]
        LOADS = {"kv": 3, "o0": 2, "o1": 2, "rd": 3, "sh": 2}

        def loads_to(i):
            return 16 * sum(LOADS.get(p, 1) for p in PIECES[i % 2:i + 1:2])

        def split_views(name, stg):
            s3 = halves(stg)
            if name == "kv":
                r = []
                for lo, e0 in ((0, 0), (128, 32)):
                    src = s3[:, :, lo:lo + 128].rearrange("p h (g e) -> p h g e", e=32)
                    dst = [w[:, :, QC:QC + KC].rearrange("p h (g e) -> p h g e", e=DH)[:, :, :, e0:e0 + 32]
                           for w in (wqkv_h, wqkv_l)]
                    r.append((src, dst[0], dst[1]))
                r.append((s3[:, :, 256:512], wqkv_h[:, :, QC + KC:QKV], wqkv_l[:, :, QC + KC:QKV]))
                return r
            if name in ("qs", "qg"):
                e0 = 0 if name == "qs" else 32
                r = []
                for h in range(2):
                    for t in range(2):
                        src = s3[:, h, 256 * t:256 * t + 256].rearrange("p (s j e) -> p j s e", s=2, j=4)
                        dst = [w[:, h, 512 * t:512 * t + 512].rearrange("p (j s e) -> p j s e", j=4, s=2)
                               [:, :, :, e0:e0 + 32] for w in (wqkv_h, wqkv_l)]
                        r.append((src, dst[0], dst[1]))
                return r
            if name in ("o0", "o1"):
                t = int(name[1])
                return [(stg[:].rearrange("p (j n) -> p j n", j=4), wo_h[:, 4 * t:4 * t + 4, :],
                         wo_l[:, 4 * t:4 * t + 4, :])]
            if name == "rd":
                return [(stg[:, 0:256].rearrange("p (h n) -> p h n", h=2), wr_h[:], wr_l[:]),
                        (stg[:, 256:1024].rearrange("p (k n) -> p k n", k=3), wd_h[:], wd_l[:])]
            if name == "sh":
                s4_ = stg[:].rearrange("p (a h n) -> p a h n", a=2, h=2)
                return [(s4_[:, a], wgu_h[:, :, 0, 256 * a:256 * a + 256], wgu_l[:, :, 0, 256 * a:256 * a + 256])
                        for a in range(2)]
            a, c0 = (0 if name[0] == "g" else 256), 1 + 2 * int(name[1])
            return [(s3.rearrange("p h (c n) -> p h c n", c=2), wgu_h[:, :, c0:c0 + 2, a:a + 256],
                     wgu_l[:, :, c0:c0 + 2, a:a + 256])]

        def beside(v):
            return v[:].rearrange("p t s (g e) -> p t (s g) e", e=DH)[:, :, 0:4:3, :]

        def real(n):
            return not isinstance(n, int) or 0 <= n < NT

        @block.sync
        def _(sp):
            sp.dma_start(c_row[:, 0, :], c_in).then_inc(S["c_ld"], 16)
            sp.dma_start(tab[:], table).then_inc(S["tab_ld"], 16)
            sp.dma_start(mask_f, mask_in).then_inc(S["mask_ld"], 16)
            sp.dma_start(lsc[:, 0, :], logit_scale.rearrange("(a h) -> a h", a=1).to_broadcast([P, H])
                         ).then_inc(S["small_ld"], 16)
            sp.dma_start(amp[:], amplitudes).then_inc(S["small_ld"], 16)
            sp.dma_start(amps[:, 2:3], expert_scale.rearrange("(e a) -> e a", a=1)).then_inc(S["small_ld"], 16)

            def load_piece(i):
                name, stg, s = PIECES[i], stage[i % 2], S[f"stage_ld{i % 2}"]
                s3 = halves(stg)
                if 2 <= i < 5:
                    sp.wait_ge(S["mod_ps"], i - 1)
                if i >= 5:
                    sp.wait_ge(S["piece_lo"], i - 4)
                if name[0] == "m":
                    n = int(name[1])
                    sp.dma_start(s3, d_rows(wmod)[:, :, 512 * n:512 * n + 512]).then_inc(s, 16)
                elif name == "kv":
                    sp.dma_start(s3[:, :, 0:128], d_rows(wk_sem)).then_inc(s, 16)
                    sp.dma_start(s3[:, :, 128:256], d_rows(wk_geo)).then_inc(s, 16)
                    sp.dma_start(s3[:, :, 256:512], d_rows(wv)).then_inc(s, 16)
                elif name in ("qs", "qg"):
                    sp.dma_start(s3, d_rows(wq_sem if name == "qs" else wq_geo)).then_inc(s, 16)
                elif name in ("o0", "o1"):
                    o4 = stg[:].rearrange("p (j n) -> p j n", j=4)
                    for k in range(2):
                        sp.dma_start(o4[64 * k:64 * k + 64], wo_rows[k, int(name[1])]).then_inc(s, 16)
                elif name == "rd":
                    sp.dma_start(stg[:, 0:256].rearrange("p (h n) -> p h n", h=2), d_rows(w_router)).then_inc(s, 16)
                    sp.dma_start(stg[:, 256:512], w_down).then_inc(s, 16)
                    sp.dma_start(stg[:, 512:1024].rearrange("p (h n) -> p h n", h=2), d_rows(sw_down)).then_inc(s, 16)
                elif name == "sh":
                    s4_ = stg[:].rearrange("p (a h n) -> p a h n", a=2, h=2)
                    sp.dma_start(s4_[:, 0], d_rows(sw_gate)).then_inc(s, 16)
                    sp.dma_start(s4_[:, 1], d_rows(sw_up)).then_inc(s, 16)
                else:
                    w, n = (w_gate if name[0] == "g" else w_up), int(name[1])
                    sp.dma_start(s3, d_rows(w)[:, :, 512 * n:512 * n + 512]).then_inc(s, 16)

            x_tiles = x_in.rearrange("b (u p) d -> p (b u) d", p=P)

            def load_x(q):
                sp.dma_start(x[:, 8 * q:8 * q + 8, :], x_tiles[:, 8 * q:8 * q + 8, :]).then_inc(S[f"x_ld{q}"], 16)

            load_x(0)
            load_piece(0)
            load_piece(1)
            load_x(1)
            load_piece(2)
            load_x(2)
            load_piece(3)
            load_x(3)
            sp.wait_ge(S["gate_fix"], 5)
            for a, col in ((0, 2 * D), (1, 5 * D)):
                sp.dma_start(gates_dram[:, a, :], modrow[:, col:col + D]).then_inc(S["gates_st"], 16)
            for i in range(4, len(PIECES)):
                load_piece(i)
            sp.wait_ge(S["z_rows"], 1)
            sp.dma_start(rows_dram.rearrange("r b n -> (r b) n"), rows_sb).then_inc(S["z_rows_st"], 16)
            for t in range(2):
                sp.wait_ge(S["z_vw"], 8 * t + 8)
                for k in range(NP):
                    sp.dma_start(vw_dram[:, k, 8 * t:8 * t + 8, :], vws[B * k:B * k + B]).then_inc(S["z_vw_st"], 16)
            sp.wait_ge(S["gates_st"], 32)
            sp.wait_ge(S["z_rows_st"], 16)
            sp.wait_ge(S["z_vw_st"], 64)

            def load_entry(b):
                sp.dma_start(gate_a[:], gates_dram[b, 0:1, :].to_broadcast([P, D])).then_inc(S["gate_a_ld"], 16)
                sp.dma_start(vwb, vw_dram[b].rearrange("k h n -> (k h) n")).then_inc(S["vw_ld"], 16)
                sp.dma_start(rowb, rows_dram[:, b, :]).then_inc(S["row_ld"], 16)

            def load_gate_f(f):
                sp.dma_start(gate_f[:], gates_dram[f, 1:2, :].to_broadcast([P, D])).then_inc(S["gate_f_ld"], 16)

            def store(f):
                for u in range(2):
                    sp.wait_ge(S["x_done"], 2 * f + u + 2)
                    sp.dma_start(out[f, P * u:P * u + P, :], x[:, 2 * f + u, :]).then_inc(S["out_st"], 16)

            load_entry(0)
            sp.wait_ge(S["x_mid"], 1)
            load_entry(1)
            load_gate_f(0)
            with sp.Fori(2, B) as b:
                sp.wait_ge(S["x_mid"], b)
                load_entry(b)
                store(b - 2)
                load_gate_f(b - 1)
            store(B - 2)
            load_gate_f(B - 1)
            store(B - 1)
            sp.wait_ge(S["out_st"], 16 * NT)

        @block.gpsimd
        def _(gp):
            gp.memset(leps[:], LN_EPS)
            gp.memset(mhalf[:], -0.5).then_inc(S["const_done"], 1)

            def inverse_std(q):
                c = slice(8 * q, 8 * q + 8)
                gp.wait_ge(S["stats_done"], 2 * q + 2)
                gp.tensor_scalar(rs1[:, c], st[:, c, 1], LN_EPS, None, ALU.add).then_inc(S["rs_var"], 1)
                gp.wait_ge(S["rs_var"], q + 1)
                gp.tensor_tensor(rs1[:, c], rs1[:, c], mhalf[:, c], ALU.pow).then_inc(S["rs_done"], 1)

            gp.wait_ge(S["const_done"], 1)
            for i, name in enumerate(SPLIT):
                if name in ("qs", "qg"):
                    gp.wait_ge(S["lsc_done"], 1)
                    gp.wait_ge(S[f"stage_ld{(i + 3) % 2}"], loads_to(i + 3))
                    for h in range(2):
                        w = halves(stage[(i + 3) % 2])[:, h, :].rearrange("p (h e) -> p h e", e=32)
                        ins = gp.tensor_tensor(w, w, lsc[:, 0, :].unsqueeze(2).to_broadcast([P, H, 32]), ALU.mult)
                    ins.then_inc(S["q_scaled"], 1)
                gp.wait_ge(S["piece_hi"], i + 1)
                views = split_views(name, stage[(i + 3) % 2])
                for k, (src, hi, lo) in enumerate(views):
                    ins = gp.tensor_tensor(lo, src, hi.bitcast(F32), ALU.subtract)
                    if k == len(views) - 1:
                        ins.then_inc(S["piece_lo"], 1)
                if name == "kv":
                    for q in range(2):
                        inverse_std(q)
                if name == "qs":
                    for q in range(2, 4):
                        inverse_std(q)

            def keys_and_queries(b):
                gp.wait_ge(S["k_m"], b + 1)
                gp.tensor_tensor(rot1[:, H:], rot1[:, H:], rot2[:, H:], ALU.add).then_inc(S["k_rot"], 1)
                gp.wait_ge(S["q_m"], b + 1)
                gp.tensor_tensor(rot1[:, 0:H], rot1[:, 0:H], rot2[:, 0:H], ALU.add).then_inc(S["q_rot"], 1)

            def normalise(b, t):
                gp.wait_ge(S["rinv_ready"], 2 * b + t + 1)
                scale = rinv[:, 8 * t:8 * t + 8].unsqueeze(2)
                gp.tensor_tensor(pp[:, :, 8 * t:8 * t + 8].rearrange("p k h -> p h k"),
                                 probs[:, 8 * t:8 * t + 8, P:NK], scale.to_broadcast([P, 8, NP]), ALU.mult)
                gp.tensor_tensor(probs[:, 8 * t:8 * t + 8, 0:P], probs[:, 8 * t:8 * t + 8, 0:P],
                                 scale.to_broadcast([P, 8, P]), ALU.mult).then_inc(S["p_ready"], 1)

            def ln2(n):
                gp.wait_ge(S["f_var"], n + 1)
                gp.tensor_tensor(veps[:], mv[:, 1:2], leps[:], ALU.add).then_inc(S["f_veps"], 1)
                gp.wait_ge(S["f_veps"], n + 1)
                gp.tensor_tensor(rs2[:], veps[:], mhalf[:, 0:1], ALU.pow).then_inc(S["f_rs"], 1)

            def mix_sum(n, u, k):
                gp.wait_ge(S["chunk_done"], NCH * n + k + 1 + 2)
                if k == 2:
                    if not (isinstance(n, int) and n == 0):
                        gp.wait_ge(S["mixed_ready"], n)
                    gp.tensor_tensor(acc, prod[:, 0, :], prod[:, 1, :], ALU.add).then_inc(S["mix_sum"], 1)
                else:
                    gp.wait_ge(S["mix_sum"], 3 * n + k - 2)
                    gp.tensor_tensor(acc, acc, prod[:, k - 1, :], ALU.add).then_inc(S["mix_sum"], 1)
                if k == 4:
                    gp.wait_ge(S["mix_sum"], 3 * n + 3)
                    gp.tensor_tensor(mixed[u], acc[:, 0:128], acc[:, 128:256], ALU.add
                                     ).then_inc(S["mixed_ready"], 1)

            def body(b, back, front):
                m0, m1, m2 = 2 * b - 3, 2 * b - 2, 2 * b - 1
                if real(m1):
                    ln2(m1)
                if back:
                    normalise(b, 0)
                    normalise(b, 1)
                if real(m0):
                    mix_sum(m0, 1, 2)
                    mix_sum(m0, 1, 3)
                if front:
                    keys_and_queries(b + 1)
                if real(m2):
                    ln2(m2)
                if real(m0):
                    mix_sum(m0, 1, 4)
                if real(m1):
                    mix_sum(m1, 0, 2)
                    mix_sum(m1, 0, 3)
                    mix_sum(m1, 0, 4)

            keys_and_queries(0)
            body(0, True, True)
            body(1, True, True)
            with gp.Fori(2, B - 1) as b:
                body(b, True, True)
            body(B - 1, True, False)
            body(B, False, False)
            body(B + 1, False, False)

        @block.tensor
        def _(pe):
            def mm3(out_, lh, ll, rh, rl, start, stop, **kw):
                pe.matmul(out_, lh, rh, start=start, stop=False, **kw)
                pe.matmul(out_, lh, rl, start=False, stop=False, **kw)
                return pe.matmul(out_, ll, rh, start=False, stop=stop, **kw)

            pe.wait_ge(S["tab_ld"], 16)
            pe.wait_ge(S["silu_row"], 1)
            for h in range(2):
                ins = pe.transpose(ps[:, AO, 16 * h:16 * h + 16], c_row[:, 2, P * h:P * h + P], ident[0:B, 0:B])
            ins.then_inc(S["cT_ps"], 1)
            pe.wait_ge(S["cT_copied"], 1)
            for n in range(3):
                pe.wait_ge(S[f"stage_ld{n % 2}"], loads_to(n))
                for h in range(2):
                    ins = pe.matmul(ps[0:B, n, :], cT[:, h, :], halves(stage[n % 2])[:, h, :],
                                    start=(h == 0), stop=(h == 1))
                ins.then_inc(S["mod_ps"], 1)
            pe.wait_ge(S["modrow_done"], 4)
            for k, col in enumerate((D, 0, 4 * D, 3 * D)):
                for h in range(2):
                    ins = pe.transpose(ps[:, AO, 32 + 16 * (2 * k + h):48 + 16 * (2 * k + h)],
                                       modrow[:, col + P * h:col + P * h + P], ident[0:B, 0:B])
            ins.then_inc(S["modT_ps"], 1)

            with pe.Fori(0, B // 2) as i:
                for p in range(2):
                    pe.wait_ge(S["a_xh"], 2 * i + p + 1)
                    for h in range(2):
                        o = ps[:, p, P * h:P * h + 68]
                        pe.matmul(o, xh0[p][:, P * h:P * h + P], rot_pool, start=True, stop=False,
                                  skip_group_check=True)
                        ins = pe.matmul(o[:, 64:68], xh1[p][:, P * h:P * h + P], pool1, start=False, stop=True,
                                        skip_group_check=True)
                    ins.then_inc(S["a_ps"], 1)

            pe.wait_ge(S["hp_lo"], 1)
            pe.wait_ge(S["piece_lo"], 3)
            for t in range(2):
                for h in range(2):
                    c = QC + P * t
                    mm3(ps[:, 4, 64 + 32 * t:96 + 32 * t], wqkv_h[:, h, c:c + P], wqkv_l[:, h, c:c + P],
                        hp_h[:, h, 0:2, :], hp_l[:, h, 0:2, :], h == 0, h == 1)
            for k, r in enumerate((3, 0, 1)):
                for h in range(2):
                    ins = mm3(ps[0:B, k // 2, 256 * (k % 2):256 * (k % 2) + 256], hp_h[:, h, r, :], hp_l[:, h, r, :],
                              wqkv_h[:, h, QC + KC:QKV], wqkv_l[:, h, QC + KC:QKV], h == 0, h == 1)
            ins.then_inc(S["z_v_ps"], 1)
            for t in range(2):
                for h in range(2):
                    ins = mm3(ps[0:B, 2 + t, :], hp_h[:, h, 2, :], hp_l[:, h, 2, :],
                              wqkv_h[:, h, 512 * t:512 * t + 512], wqkv_l[:, h, 512 * t:512 * t + 512],
                              h == 0, h == 1)
            ins.then_inc(S["z_q_ps"], 1)
            pe.wait_ge(S["ht_lo"], 2)
            wk = [w[:, :, QC:QC + KC].rearrange("p h (g e) -> p h g e", e=DH)[:, :, :, 32:64]
                  for w in (wqkv_h, wqkv_l)]
            for a in range(2):
                for u in range(2):
                    for k in range(NP):
                        c = B * 16 * (NP * a + k) + P * u
                        for h in range(2):
                            ins = mm3(ps[:, 6 + a, P * (NP * u + k):P * (NP * u + k) + P], ht_h[h][:, c:c + P],
                                      ht_l[h][:, c:c + P], wk[0][:, h], wk[1][:, h], h == 0, h == 1)
            ins.then_inc(S["a_kps"], 1)
            def z_rows_T():
                pe.wait_ge(S["z_v_copied"], 1)
                for r in range(2):
                    for t in range(2):
                        ins = pe.transpose(ps[:, 6, 16 * (2 * r + t):16 * (2 * r + t) + 16],
                                           vrow[r][:, P * t:P * t + P], ident[0:B, 0:B])
                pe.wait_ge(S["z_chain"], Z_ROW_C)
                for j in range(8):
                    ins = pe.transpose(ps[:, 6, 64 + 16 * j:80 + 16 * j],
                                       tmpq[:, 2 * j:2 * j + 2, :], ident[0:B, 0:B])
                ins.then_inc(S["z_row_ps"], 1)

            def z_rows():
                pe.wait_ge(S["z_rT_lo"], 1)
                pe.wait_ge(S["piece_lo"], 5)
                for j in range(8):
                    ins = mm3(ps[0:48, 7, 0:D], rT_h[:, j, :], rT_l[:, j, :], wo_h[:, j, :], wo_l[:, j, :],
                              j == 0, j == 7)
                ins.then_inc(S["z_rows_ps"], 1)

            def z_vw(p):
                j, s = p // 2, p % 2
                if p == 0:
                    pe.wait_ge(S["z_vT_lo"], 1)
                if p == 2:
                    pe.wait_ge(S["z_rows"], 1)
                if p >= 3:
                    pe.wait_ge(S["z_vw"], p - 2)
                r = slice(64 * s, 64 * s + 64)
                mm3(ps[0:NP * B, 5 + p % 3, 0:D], vT_h[r, j // 4, :], vT_l[r, j // 4, :], wo_h[r, j, :], wo_l[r, j, :],
                    True, True).then_inc(S["z_vw_ps"], 1)

            def to_features(b):
                pe.wait_ge(S["xh_ready"], b + 1)
                for h in range(2):
                    ins = pe.transpose(ps[:, A3, P * h:P * h + P], xh[:, P * h:P * h + P], ident)
                ins.then_inc(S["hT_ps"], 1)

            def project(b):
                pe.wait_ge(S["h_lo"], b + 1)
                if not (isinstance(b, int) and b == 0):
                    pe.wait_ge(S["exp_done"], 8 * b)
                for bank, lo, n in ((A2, QC, KC), (A0, 0, 512), (A1, 512, 512)):
                    for h in range(2):
                        ins = mm3(ps[:, bank, 0:n], hh[:, h, :], hl[:, h, :], wqkv_h[:, h, lo:lo + n],
                                  wqkv_l[:, h, lo:lo + n], h == 0, h == 1)
                    if bank == A2:
                        ins.then_inc(S["k_ps"], 1)
                ins.then_inc(S["q_ps"], 1)

            def project_v(b):
                if not (isinstance(b, int) and b == 0):
                    pe.wait_ge(S["pT_lo"], 4 * b)
                for h in range(2):
                    ins = mm3(ps[:, A3, 256:512], hh[:, h, :], hl[:, h, :], wqkv_h[:, h, QC + KC:QKV],
                              wqkv_l[:, h, QC + KC:QKV], h == 0, h == 1)
                ins.then_inc(S["v_ps"], 1)

            def keys_T(b):
                pe.wait_ge(S["k_rot"], b + 1)
                for t in range(2):
                    ins = pe.transpose(ps[:, A2, P * t:P * t + P], qk[:, H + 2 * t:H + 2 * t + 2, :], ident)
                ins.then_inc(S["kT_ps"], 1)

            def queries_T(b):
                pe.wait_ge(S["q_rot"], b + 1)
                for t in range(2):
                    for j in range(4):
                        p = 8 * t + 2 * j
                        ins = pe.transpose(ps[:, A0 + t, P * j:P * j + P], qk[:, p:p + 2, :], ident)
                    ins.then_inc(S["qT_ps"], 1)

            def scores(b, g):
                if g == 0:
                    pe.wait_ge(S["kT_lo"], b + 1)
                    pe.wait_ge(S["qT_lo"], 2 * b + 2)
                if g >= 3:
                    pe.wait_ge(S["exp_done"], 8 * b + g - 2)
                o = ps[:, A0 + g % 3, 0:2 * NK].rearrange("p (s k) -> p s k", k=NK)
                pe.matmul(o, id16[:], mask16[:], start=True, stop=False)
                mm3(o, qT_h[:, g, :], qT_l[:, g, :], kT_h[:, g // 4], kT_l[:, g // 4], False, True
                    ).then_inc(S["s_ps"], 1)

            def probs_T(b, t, s, more=True):
                n = 4 * b + 2 * t + s
                if s == 0:
                    pe.wait_ge(S["p_ready"], 2 * b + t + 1)
                if t == 0 and s == 0:
                    pe.wait_ge(S["v_lo"], b + 1)
                    if more:
                        pe.wait_ge(S["hf_ready"], b + 2)
                if t or s:
                    pe.wait_ge(S["pT_lo"], n)
                for j in range(4):
                    ins = pe.transpose(ps[:, A3, P * j:P * j + P], probs[:, 8 * t + 2 * j + s, 0:P], ident)
                ins.then_inc(S["pT_ps"], 1)

            def values(b, t):
                if t:
                    pe.wait_ge(S["oT_lo_r"], 2 * b + 1)
                for s in range(2):
                    pe.wait_ge(S["pT_lo"], 4 * b + 2 * t + s + 1)
                    ins = mm3(ps[:, AO, :], v_h[:, t, s, :], v_l[:, t, s, :], pT_h[:, s, :], pT_l[:, s, :],
                              s == 0, s == 1)
                ins.then_inc(S["o_ps"], 1)

            def pooled_T(b):
                pe.wait_ge(S["p_ready"], 2 * b + 2)
                pe.wait_ge(S["oT_lo_r"], 2 * b + 2)
                pe.transpose(ps[0:NP * H, AO, 256:384], pp[:].rearrange("p k h -> p (k h)"), ident
                             ).then_inc(S["pp_ps"], 1)

            def first_tile(b, more):
                pe.wait_ge(S["row_ld"], 16 * b + 16)
                if more:
                    pe.wait_ge(S["v_lo"], b + 2)
                else:
                    pe.wait_ge(S["pT_lo"], 4 * b + 4)
                pe.matmul(ps[:, A3, 0:D], tab[NP * H:NP * H + 3, C_SEL:C_SEL + P], rowb, start=True, stop=True
                          ).then_inc(S["row_ps"], 1)

            def project_out(b):
                pe.wait_ge(S["oT_lo_r"], 2 * b + 2)
                pe.wait_ge(S["ppT_ready"], b + 1)
                pe.wait_ge(S["vw_ld"], 16 * b + 16)
                pe.matmul(ps[:, AO, 0:D], ppT[:], vwb, start=True, stop=False)
                for j in range(8):
                    ins = mm3(ps[:, AO, 0:D], oT_h[:, j, :], oT_l[:, j, :], wo_h[:, j, :], wo_l[:, j, :],
                              False, j == 7)
                ins.then_inc(S["y_ps"], 1)

            def f_features(n, u):
                pe.wait_ge(S["f_xh"], n + 1)
                if not (isinstance(n, int) and n == 0):
                    pe.wait_ge(S["w8_ready"], n)
                for h in range(2):
                    ins = pe.transpose(ps[:, FM, P * h:P * h + P], xh2[:, P * h:P * h + P], ident)
                ins.then_inc(S["f_hT_ps"], 1)

            def f_inner_T(n, u):
                pe.wait_ge(S["mixed_ready"], n + 1)
                if real(n + 2):
                    pe.wait_ge(S["f_hf"], n + 3)
                elif n == NT - 2:
                    pe.wait_ge(S["w8_ready"], NT)
                else:
                    pe.wait_ge(S["x_done"], NT)
                pe.transpose(ps[:, FM, 0:P], mixed[u], ident)
                for h in range(2):
                    ins = pe.transpose(ps[:, FM, P * (h + 1):P * (h + 2)], shared[u][:, P * h:P * h + P], ident)
                ins.then_inc(S["m_ps"], 1)

            def f_logits(n, u):
                pe.wait_ge(S["f_lo"], n + 1)
                if real(n - 2):
                    pe.wait_ge(S["mT_lo_r"], n - 1)
                for h in range(2):
                    ins = mm3(ps[:, FM, 256:384], fh[u][:, h, :], fl[u][:, h, :], wr_h[:, h, :], wr_l[:, h, :],
                              h == 0, h == 1)
                ins.then_inc(S["l_ps"], 1)

            def f_down(n):
                pe.wait_ge(S["mT_lo_r"], n + 1)
                if real(n + 2):
                    pe.wait_ge(S["top_ready"], n + 3)
                for k in range(3):
                    ins = mm3(ps[:, FM, 0:D], mT_h[:, k, :], mT_l[:, k, :], wd_h[:, k, :], wd_l[:, k, :],
                              k == 0, k == 2)
                ins.then_inc(S["d_ps"], 1)

            def f_coefT(n):
                pe.wait_ge(S["coef_ready"], n + 1)
                if real(n - 2):
                    pe.wait_ge(S["x_done"], n)
                pe.transpose(ps[:, FM, 384:512], coef[:], ident).then_inc(S["cT2_ps"], 1)

            def f_weights(n):
                pe.wait_ge(S["cT2_ready"], n + 1)
                pe.matmul(ps[:, FM, 0:NB], coefT[:], mix[:], start=True, stop=True).then_inc(S["w_ps"], 1)

            def f_chunk(n, u, k):
                bank = FR + (k + u) % 2
                pe.wait_ge(S["chunk_done"], NCH * n + k + 1)
                if k == 0:
                    pe.wait_ge(S["f_lo"], n + 1)
                for h in range(2):
                    ins = mm3(ps[:, bank, :], fh[u][:, h, :], fl[u][:, h, :], wgu_h[:, h, k, :],
                              wgu_l[:, h, k, :], h == 0, h == 1)
                ins.then_inc(S["gu_ps"], 1)

            def body(b, back, front):
                m0, m1, m2 = 2 * b - 3, 2 * b - 2, 2 * b - 1
                first = isinstance(b, int) and b == 0
                if back:
                    scores(b, 0)
                if real(m0):
                    f_chunk(m0, 1, 0)
                if back:
                    scores(b, 1)
                    scores(b, 2)
                    scores(b, 3)
                if front:
                    to_features(b + 1)
                if real(m0):
                    f_chunk(m0, 1, 1)
                    f_chunk(m0, 1, 2)
                if real(m1):
                    f_features(m1, 0)
                if back:
                    scores(b, 4)
                    scores(b, 5)
                if real(m1 - 2):
                    f_inner_T(m1 - 2, 0)
                if back:
                    scores(b, 6)
                if real(m0):
                    f_chunk(m0, 1, 3)
                if back:
                    scores(b, 7)
                if real(m1):
                    f_logits(m1, 0)
                if back:
                    probs_T(b, 0, 0, front)
                if real(m1 - 2):
                    f_down(m1 - 2)
                if real(m0):
                    f_chunk(m0, 1, 4)
                if back:
                    probs_T(b, 0, 1)
                if real(m1):
                    f_coefT(m1)
                if front:
                    project(b + 1)
                if real(m1):
                    f_weights(m1)
                if back:
                    values(b, 0)
                    probs_T(b, 1, 0)
                if real(m1):
                    f_chunk(m1, 0, 0)
                if front:
                    keys_T(b + 1)
                if real(m1):
                    f_chunk(m1, 0, 1)
                if back:
                    probs_T(b, 1, 1)
                if front:
                    queries_T(b + 1)
                if real(m2):
                    f_features(m2, 1)
                if back:
                    values(b, 1)
                if first:
                    z_rows_T()
                    z_rows()
                if real(m0):
                    f_inner_T(m0, 1)
                if real(m1):
                    f_chunk(m1, 0, 2)
                if front:
                    project_v(b + 1)
                if first:
                    z_vw(0)
                    z_vw(1)
                    z_vw(2)
                    z_vw(3)
                    z_vw(4)
                    z_vw(5)
                    z_vw(6)
                    z_vw(7)
                    z_vw(8)
                    z_vw(9)
                    z_vw(10)
                    z_vw(11)
                    z_vw(12)
                    z_vw(13)
                    z_vw(14)
                    z_vw(15)
                if real(m2):
                    f_logits(m2, 1)
                if real(m1):
                    f_chunk(m1, 0, 3)
                if back:
                    pooled_T(b)
                    first_tile(b, front)
                if real(m0):
                    f_down(m0)
                if back:
                    project_out(b)
                if real(m2):
                    f_coefT(m2)
                if real(m1):
                    f_chunk(m1, 0, 4)
                if real(m2):
                    f_weights(m2)

            pe.wait_ge(S["z_chain"], 1)
            to_features(0)
            pe.wait_ge(S["a_spread"], 2)
            for u in range(2):
                for k in range(NP):
                    for t in range(2):
                        n = (u * NP + k) * 2 + t
                        ins = pe.matmul(ps[:, 4, 8 * n:8 * n + 8], spread[:, 2 * n:2 * n + 2, :],
                                        tab[:, C_DB:C_DB + 8], start=True, stop=True)
            ins.then_inc(S["a_kp_ps"], 1)
            pe.wait_ge(S["z_v_copied"], 1)
            project(0)
            pe.wait_ge(S["a_kp"], 1)
            for k in range(NP):
                for t in range(2):
                    ins = pe.transpose(ps[0:B, 4, 256 * k + P * t:256 * k + P * t + P], kpool[:, :, t, k], ident)
            ins.then_inc(S["z_kp_ps"], 1)
            for t in range(2):
                for h in range(2):
                    ins = mm3(ps[:, 5, 32 * t:32 * t + 32], wqkv_h[:, h, QC + KC + P * t:QC + KC + P * t + P],
                              wqkv_l[:, h, QC + KC + P * t:QC + KC + P * t + P],
                              hp_h[:, h, 0:2, :], hp_l[:, h, 0:2, :], h == 0, h == 1)
            ins.then_inc(S["z_vT_ps"], 1)
            keys_T(0)
            queries_T(0)
            project_v(0)
            pe.wait_ge(S["mask_done"], 1)
            pe.wait_ge(S["z_zero"], 2)
            pe.wait_ge(S["mix_done"], 1)
            body(0, True, True)
            pe.wait_ge(S["piece_lo"], len(SPLIT))
            body(1, True, True)
            with pe.Fori(2, B - 1) as b:
                body(b, True, True)
            body(B - 1, True, False)
            body(B, False, False)
            body(B + 1, False, False)

        @block.scalar
        def _(act):
            act.wait_ge(S["small_ld"], 48)
            act.activation(lsc[:, 1, :], lsc[:, 0, :], ACT.Exp).then_inc(S["lsc_exp"], 1)
            act.wait_ge(S["c_ld"], 16)
            act.activation(c_row[:, 1, :], c_row[:, 0, :], ACT.Tanh, scale=0.5).then_inc(S["silu_t"], 1)
            for n in range(3):
                act.wait_ge(S["mod_ps"], n + 1)
                act.copy(modrow[:, 512 * n:512 * n + 512], ps[0:B, n, :]).then_inc(S["mod_ld"], 1)

            def split(i):
                name = SPLIT[i]
                if name in ("qs", "qg"):
                    act.wait_ge(S["q_scaled"], 1 + ("qs", "qg").index(name))
                else:
                    act.wait_ge(S[f"stage_ld{(i + 3) % 2}"], loads_to(i + 3))
                views = split_views(name, stage[(i + 3) % 2])
                for k, (src, hi, lo) in enumerate(views):
                    ins = act.copy(hi, src)
                    if k == len(views) - 1:
                        ins.then_inc(S["piece_hi"], 1)

            for i in range(len(SPLIT)):
                split(i)

            act.wait_ge(S["a_post"], B)
            for h in range(2):
                act.copy(ht_h[h], ht[:, h].rearrange("p c b i -> p (c b i)")).then_inc(S["ht_hi"], 1)

            def z_exp():
                act.wait_ge(S["z_chain"], Z_MAX)
                act.activation(sm127[:, 2:4, :], sm127[:, 0:2, :], ACT.Exp).then_inc(S["z_exp"], 1)

            def z_vw(p):
                act.wait_ge(S["z_vw_ps"], p + 1)
                if p == 8:
                    act.wait_ge(S["z_vw_st"], 32)
                act.copy(vws[:, p % 8, :], ps[0:NP * B, 5 + p % 3, 0:D]).then_inc(S["z_vw"], 1)

            def hidden(b):
                act.wait_ge(S["hT_ps"], b + 1)
                for h in range(2):
                    ins = act.activation(hf[:, h, :], ps[:, A3, P * h:P * h + P], ACT.Identity,
                                         bias=mod_a[:, 2 + h:3 + h], scale=mod_a[:, h:h + 1])
                ins.then_inc(S["hf_ready"], 1)
                act.wait_ge(S["hf_ready"], b + 1)
                act.copy(hh[:], hf[:]).then_inc(S["h_hi"], 1)

            def semantic_k(b):
                act.wait_ge(S["k_ps"], b + 1)
                act.copy(qk[:, H:, 0:32], ps[:, A2, 0:KC].rearrange("p (g e) -> p g e", e=DH)[:, :, 0:32]
                         ).then_inc(S["k_sem"], 1)

            def split_v(b):
                act.wait_ge(S["v_ps"], b + 1)
                act.copy(beside(v_h), ps[:, A3, 256:512].rearrange("p (t s e) -> p t s e", t=2, s=2)
                         ).then_inc(S["v_hi"], 1)

            def semantic_q(b):
                act.wait_ge(S["q_ps"], b + 1)
                act.copy(qk[:, 0:H, 0:32], ps[:, A0:A0 + 2, :].rearrange("p a (h e) -> p (a h) e", e=DH)[:, :, 0:32]
                         ).then_inc(S["q_sem"], 1)

            def split_k(b):
                act.wait_ge(S["kT_ps"], b + 1)
                for s in range(2):
                    r = slice(64 * s, 64 * s + 64)
                    ins = act.copy(kT_h[r, :, s, 0:P], ps[r, A2, 0:256].rearrange("p (t k) -> p t k", t=2))
                ins.then_inc(S["kT_hi"], 1)

            def split_q(b):
                for t in range(2):
                    act.wait_ge(S["qT_ps"], 2 * b + t + 1)
                    act.copy(qT_h[:, 4 * t:4 * t + 4, :], ps[:, A0 + t, :].rearrange("p (j k) -> p j k", j=4)
                             ).then_inc(S["qT_hi"], 1)

            def exps(b, g):
                act.wait_ge(S["nmax_ready"], 8 * b + g + 1)
                for s in range(2):
                    h = 2 * g + s
                    ins = act.activation(probs[:, h, :], ps[:, A0 + g % 3, NK * s:NK * s + NK], ACT.Exp,
                                         bias=nmax[:, h:h + 1], accum_out=psums[:, h:h + 1])
                ins.then_inc(S["exp_done"], 1)

            def split_probs(b, t, s):
                act.wait_ge(S["pT_ps"], 4 * b + 2 * t + s + 1)
                act.copy(pT_h[:, s, :], ps[:, A3, :]).then_inc(S["pT_hi"], 1)

            def split_out(b, t):
                act.wait_ge(S["o_ps"], 2 * b + t + 1)
                act.copy(oT_h[:, 4 * t:4 * t + 4, :], ps[:, AO, :].rearrange("p (j k) -> p j k", j=4)
                         ).then_inc(S["oT_hi_r"], 1)

            def pooled(b):
                act.wait_ge(S["pp_ps"], b + 1)
                act.copy(ppT[:], ps[0:NP * H, AO, 256:384]).then_inc(S["ppT_ready"], 1)

            def f_hidden(n, u):
                act.wait_ge(S["f_hT_ps"], n + 1)
                for h in range(2):
                    ins = act.activation(hf2[:, h, :], ps[:, FM, P * h:P * h + P], ACT.Identity,
                                         bias=mod_f[:, 2 + h:3 + h], scale=mod_f[:, h:h + 1])
                ins.then_inc(S["f_hf"], 1)
                act.wait_ge(S["f_hf"], n + 1)
                act.copy(fh[u][:], hf2).then_inc(S["f_hi"], 1)

            def f_route(n):
                act.wait_ge(S["nm_ready"], n + 1)
                act.activation(ex[:], lg[:], ACT.Exp, bias=nm[:, 0:1], accum_out=zsum[:]).then_inc(S["ex_ready"], 1)

            def f_coefT(n):
                act.wait_ge(S["cT2_ps"], n + 1)
                act.copy(coefT[:], ps[:, FM, 384:512]).then_inc(S["cT2_ready"], 1)

            def f_tanh(n, u, k):
                act.wait_ge(S["gu_ps"], NCH * n + k + 1)
                act.activation(th[(k + u) % 2], ps[:, FR + (k + u) % 2, 0:256], ACT.Tanh, scale=0.5
                               ).then_inc(S["th_ready"], 1)

            def f_inner(n):
                act.wait_ge(S["m_ps"], n + 1)
                act.copy(mT_h[:], ps[:, FM, 0:384].rearrange("p (k n) -> p k n", k=3)).then_inc(S["mT_hi_r"], 1)

            def body(b, back, front):
                m0, m1, m2 = 2 * b - 3, 2 * b - 2, 2 * b - 1
                first = isinstance(b, int) and b == 0
                if real(m0):
                    f_tanh(m0, 1, 0)
                if back:
                    exps(b, 0)
                    exps(b, 1)
                    exps(b, 2)
                    exps(b, 3)
                if real(m0):
                    f_tanh(m0, 1, 1)
                if front:
                    hidden(b + 1)
                if real(m1):
                    f_hidden(m1, 0)
                if real(m0):
                    f_tanh(m0, 1, 2)
                if real(m1 - 2):
                    f_inner(m1 - 2)
                if back:
                    exps(b, 4)
                    exps(b, 5)
                    exps(b, 6)
                    exps(b, 7)
                if first:
                    z_exp()
                if back:
                    split_probs(b, 0, 0)
                if real(m1):
                    f_route(m1)
                if real(m0):
                    f_tanh(m0, 1, 3)
                    f_tanh(m0, 1, 4)
                if back:
                    split_probs(b, 0, 1)
                if front:
                    semantic_k(b + 1)
                if real(m1):
                    f_coefT(m1)
                if front:
                    semantic_q(b + 1)
                if back:
                    split_out(b, 0)
                    split_probs(b, 1, 0)
                if front:
                    split_k(b + 1)
                if back:
                    split_probs(b, 1, 1)
                if real(m1):
                    f_tanh(m1, 0, 0)
                    f_tanh(m1, 0, 1)
                if real(m2):
                    f_hidden(m2, 1)
                if real(m0):
                    f_inner(m0)
                if front:
                    split_q(b + 1)
                if back:
                    split_out(b, 1)
                if front:
                    split_v(b + 1)
                if first:
                    z_vw(0)
                    z_vw(1)
                    z_vw(2)
                    z_vw(3)
                    z_vw(4)
                    z_vw(5)
                    z_vw(6)
                    z_vw(7)
                    z_vw(8)
                    z_vw(9)
                    z_vw(10)
                    z_vw(11)
                    z_vw(12)
                    z_vw(13)
                    z_vw(14)
                    z_vw(15)
                if back:
                    pooled(b)
                if real(m1):
                    f_tanh(m1, 0, 2)
                if real(m2):
                    f_route(m2)
                if real(m1):
                    f_tanh(m1, 0, 3)
                if real(m2):
                    f_coefT(m2)
                if real(m1):
                    f_tanh(m1, 0, 4)

            hidden(0)
            semantic_k(0)
            semantic_q(0)
            split_k(0)
            split_q(0)
            split_v(0)
            body(0, True, True)
            act.wait_ge(S["z_vw_st"], 64)
            body(1, True, True)
            with act.Fori(2, B - 1) as b:
                body(b, True, True)
            body(B - 1, True, False)
            body(B, False, False)
            body(B + 1, False, False)

        @block.vector
        def _(ve):
            cs1, sn1 = tab[:, C_COS1:C_COS1 + 32], tab[:, C_SIN1:C_SIN1 + 32]

            def carrier(s, value):
                ve.wait_ge(s, value)
                ve.tensor_copy(beat[:, 1:2], beat[:, 0:1])

            def over_heads(ap, n):
                return ap.unsqueeze(1).to_broadcast([ap.shape[0], n, ap.shape[1]])

            def rotate_products(m1, m2, src, cs, sn, n):
                ve.tensor_tensor(m1, src[:, :, 32:64], over_heads(cs, n), ALU.mult)
                ve.tensor_tensor(m2[:, :, 0:16], src[:, :, 48:64], over_heads(sn[:, 0:16], n), ALU.mult)
                return ve.tensor_tensor(m2[:, :, 16:32], src[:, :, 32:48], over_heads(sn[:, 16:32], n), ALU.mult)

            def statistics(q):
                ve.wait_ge(S[f"x_ld{q}"], 16)
                with ve.Fori(2 * q, 2 * q + 2) as i:
                    for u in range(4):
                        ins = ve.bn_stats(bst4[:, u, :], x[:, 4 * i + u, :])
                    ins.then_inc(S["bn1"], 1)
                    carrier(S["bn1"], i + 1)
                    for u in range(4):
                        ins = ve.bn_aggr(mv4[:, u, :], bst4[:, u, :])
                    ins.then_inc(S["aggr1"], 1)
                    ve.wait_ge(S["aggr1"], i + 1)
                    ve.tensor_scalar(st[:, bass.ds(4 * i, 4), :], mv4[:], 1.0, None, ALU.mult
                                     ).then_inc(S["stats_done"], 1)

            ve.wait_ge(S["silu_t"], 1)
            ve.scalar_tensor_tensor(c_row[:, 1, :], c_row[:, 1, :], 1.0, c_row[:, 0, :], ALU.add, ALU.mult
                                    ).then_inc(S["silu_a"], 1)
            ve.wait_ge(S["silu_a"], 1)
            ve.tensor_scalar(c_row[:, 2, :], c_row[:, 1, :], 0.5, None, ALU.mult).then_inc(S["silu_row"], 1)
            ve.wait_ge(S["cT_ps"], 1)
            ve.tensor_copy(cT[:], ps[:, AO, 0:32].rearrange("p (h b) -> p h b", h=2)).then_inc(S["cT_copied"], 1)
            ve.wait_ge(S["mask_ld"], 16)
            ve.tensor_copy(mask16[:], mask_f.rearrange("p (a k) -> p a k", a=2))
            ve.wait_ge(S["tab_ld"], 16)
            ve.tensor_copy(id16[:], ident).then_inc(S["mask_done"], 1)
            ve.memset(take[:], TAKEN)
            ve.memset(beat[:], 0.0)
            ve.memset(den[:], 0.0).then_inc(S["chunk_done"], 2)
            ve.memset(rn[:], 0.0).then_inc(S["x_done"], 1)
            ve.wait_ge(S["lsc_exp"], 1)
            ve.tensor_scalar(lsc[:, 0, :], lsc[:, 1, :], 32.0 ** -0.5, None, ALU.mult).then_inc(S["lsc_done"], 1)
            ve.wait_ge(S["small_ld"], 48)
            ve.tensor_tensor(amp[:], amp[:], amp[:], ALU.mult).then_inc(S["amp_d"], 1)
            ve.wait_ge(S["amp_d"], 1)
            ve.tensor_tensor(ampp[:], amp[:, :, 0], amp[:, :, 1], ALU.add).then_inc(S["amp_d"], 1)
            ve.wait_ge(S["amp_d"], 2)
            ve.tensor_reduce(amps[:, 0:1], ampp[:], X, ALU.add).then_inc(S["amp_d"], 1)
            ve.wait_ge(S["amp_d"], 3)
            ve.tensor_scalar(amps[:, 1:2], amps[:, 0:1], EPS, None, ALU.add).then_inc(S["amp_d"], 1)
            ve.wait_ge(S["amp_d"], 4)
            ve.reciprocal(amps[:, 3:4], amps[:, 1:2]).then_inc(S["amp_d"], 1)
            ve.wait_ge(S["amp_d"], 5)
            ve.tensor_scalar(mix[:], ampp[:], amps[:, 3:4], amps[:, 2:3], ALU.mult, ALU.mult
                             ).then_inc(S["mix_done"], 1)
            for q in range(2):
                statistics(q)
            ve.wait_ge(S["mod_ld"], 3)
            gates = modrow.rearrange("p (a k d) -> p a k d", a=2, k=3)[:, :, 2, :]
            ups = modrow.rearrange("p (a k d) -> p a k d", a=2, k=3)[:, :, 1, :]
            g_sign, g_neg = upd[0:B], prod[0:B, 0:2, :]
            ve.tensor_scalar(ups, ups, 1.0, None, ALU.add).then_inc(S["modrow_done"], 4)
            ve.wait_ge(S["mask_done"], 1)
            ve.tensor_scalar(g_sign, gates, 0.0, 2.0, ALU.is_ge, ALU.mult).then_inc(S["gate_fix"], 1)
            ve.wait_ge(S["gate_fix"], 1)
            ve.tensor_scalar(g_neg, gates, -1.0, None, ALU.mult).then_inc(S["gate_fix"], 1)
            ve.wait_ge(S["gate_fix"], 2)
            ve.tensor_tensor(gates, gates, g_neg, ALU.max).then_inc(S["gate_fix"], 1)
            ve.wait_ge(S["gate_fix"], 3)
            ve.tensor_scalar(gates, gates, 0.25, None, ALU.max).then_inc(S["gate_fix"], 1)
            ve.wait_ge(S["gate_fix"], 4)
            ve.scalar_tensor_tensor(gates, g_sign, -1.0, gates, ALU.add, ALU.mult).then_inc(S["gate_fix"], 1)
            ve.wait_ge(S["modT_ps"], 1)
            ve.tensor_copy(modT[:], ps[:, AO, 32:160].rearrange("p (k b) -> p b k", k=8)).then_inc(S["modT_done"], 1)
            for q in range(2, 4):
                statistics(q)
            zero = early[:, 1600:1860]
            ve.memset(zero, 0.0).then_inc(S["z_zero"], 1)
            ve.wait_ge(S["z_zero"], 1)
            for k in (kT_h, kT_l):
                for s in range(2):
                    r = slice(64 - 64 * s, 128 - 64 * s)
                    ve.tensor_copy(k[r, :, s, :], zero[r].rearrange("p (t k) -> p t k", t=2))
            for v in (v_h, v_l):
                for s in range(2):
                    c = slice(64 - 64 * s, 128 - 64 * s)
                    ins = ve.tensor_copy(v[:, :, s, c], zero[:, 0:P].rearrange("p (t e) -> p t e", t=2))
            ins.then_inc(S["z_zero"], 1)

            ve.wait_ge(S["rs_done"], 4)
            ve.wait_ge(S["modT_done"], 1)
            ve.wait_ge(S["gates_st"], 32)

            def first_norm(b, p):
                for u, dst in ((0, xh0[p]), (1, xh1[p])):
                    ins = ve.tensor_scalar(dst, x[:, 2 * b + u, :], st[:, 2 * b + u, 0:1],
                                           rs1[:, bass.ds(2 * b + u, 1)], ALU.subtract, ALU.mult)
                ins.then_inc(S["a_xh"], 1)

            def first_scaled(b, p):
                ve.wait_ge(S["a_ps"], b + 1)
                if not (isinstance(b, int) and b < 2):
                    ve.wait_ge(S["a_post"], b - 1)
                ve.tensor_tensor(mt[p], ps[:, p, 0:2 * P].rearrange("p (h c) -> p h c", h=2)[:, :, 0:68],
                                 modT[:, b, 0:2].unsqueeze(2).to_broadcast([P, 2, 68]), ALU.mult
                                 ).then_inc(S["a_mt"], 1)

            def first_shifted(b, p):
                ve.wait_ge(S["a_mt"], b + 1)
                for h in range(2):
                    shift = modT[:, b, 2 + h:3 + h]
                    ve.tensor_scalar(hpool[:, h, :, b], mt[p][:, h, 64:68], shift, None, ALU.add)
                    ins = ve.scalar_tensor_tensor(ht[:, h, :, b, :],
                                                  tab[:, C_WS:C_WS + 64].rearrange("p (c i) -> p c i", i=16), shift,
                                                  mt[p][:, h, 0:64].rearrange("p (c i) -> p c i", i=16),
                                                  ALU.mult, ALU.add)
                ins.then_inc(S["a_post"], 1)

            for p in range(2):
                first_norm(p, p)
            for p in range(2):
                first_scaled(p, p)
                first_norm(p + 2, p)
                first_shifted(p, p)
            with ve.Fori(1, B // 2 - 1) as i:
                for p in range(2):
                    first_scaled(2 * i + p, p)
                    first_norm(2 * i + p + 2, p)
                    first_shifted(2 * i + p, p)
            for p in range(2):
                first_scaled(B - 2 + p, p)
                first_shifted(B - 2 + p, p)

            ve.wait_ge(S["a_post"], B)
            ve.tensor_copy(hp_h, hpool).then_inc(S["hp_hi"], 1)
            ve.wait_ge(S["hp_hi"], 1)
            ve.tensor_tensor(hp_l, hpool, hp_h.bitcast(F32), ALU.subtract).then_inc(S["hp_lo"], 1)
            csl = tab[0:B, C_COSL:C_COSL + 32]
            snl = tab[0:B, C_SINL:C_SINL + 32]
            z = [0]

            def link(ins):
                z[0] += 1
                ins.then_inc(S["z_chain"], 1)
                ve.wait_ge(S["z_chain"], z[0])

            def z_scores(k):
                for t in range(2):
                    kk = kprow[:, k, P * t:P * t + P].unsqueeze(1).to_broadcast([B, 4, P])
                    q4 = q127[:, 8 * t:8 * t + 8, :].rearrange("p (j s) e -> p j (s e)", j=4)
                    d4 = dots[:, 8 * t:8 * t + 8, :].rearrange("p (j s) e -> p j (s e)", j=4)
                    ins = ve.tensor_tensor(d4, q4, kk, ALU.mult)
                link(ins)
                link(ve.tensor_reduce(s127[:, k, :], dots, X, ALU.add))

            def z_max():
                link(ve.tensor_tensor(sm127[:, 4, :], s127[:, 0, :], s127[:, 1, :], ALU.max))
                for k in range(NP):
                    ins = ve.tensor_tensor(sm127[:, k, :], s127[:, k, :], sm127[:, 4, :], ALU.subtract)
                link(ins)
                assert z[0] == Z_MAX

            def z_probs():
                ve.wait_ge(S["z_exp"], 1)
                link(ve.tensor_tensor(sm127[:, 4, :], sm127[:, 2, :], sm127[:, 3, :], ALU.add))
                link(ve.reciprocal(sm127[:, 5, :], sm127[:, 4, :]))
                for k in range(NP):
                    ins = ve.tensor_tensor(s127[:, k, :], sm127[:, 2 + k, :], sm127[:, 5, :], ALU.mult)
                link(ins)

            def z_weigh(k):
                for t in range(2):
                    dst = (dots, tmpq)[k][:, 8 * t:8 * t + 8, :].rearrange("p (j s) e -> p j s e", j=4)
                    vv = vrow[1 + k][:, P * t:P * t + P].rearrange("p (s e) -> p s e", s=2).unsqueeze(1)
                    pp = s127[:, k, 8 * t:8 * t + 8].rearrange("p (j s) -> p j s", j=4).unsqueeze(3)
                    ins = ve.tensor_tensor(dst, vv.to_broadcast([B, 4, 2, DH]), pp.to_broadcast([B, 4, 2, DH]),
                                           ALU.mult)
                link(ins)

            def z_row():
                link(ve.tensor_tensor(tmpq, tmpq, dots, ALU.add))
                assert z[0] == Z_ROW_C

            def z_split():
                ve.wait_ge(S["z_row_ps"], 1)
                for r in range(2):
                    for t in range(2):
                        ve.tensor_copy(rT[:, 4 * t:4 * t + 4, r, :], ps[:, 6, 16 * (2 * r + t):16 * (2 * r + t) + 16]
                                       .unsqueeze(1).to_broadcast([P, 4, B]))
                ve.tensor_copy(rT[:, :, 2, :], ps[:, 6, 64:192].rearrange("p (j b) -> p j b", j=8)
                               ).then_inc(S["z_rT"], 1)
                ve.wait_ge(S["z_rT"], 1)
                rT2 = rT.rearrange("p j r b -> p j (r b)")
                ve.tensor_copy(rT_h, rT2).then_inc(S["z_rT_hi"], 1)
                ve.wait_ge(S["z_rT_hi"], 1)
                ve.tensor_tensor(rT_l, rT2, rT_h.bitcast(F32), ALU.subtract
                                 ).then_inc(S["z_rT_lo"], 1)

            def z_rows():
                ve.wait_ge(S["z_rows_ps"], 1)
                ve.tensor_copy(rows_sb, ps[0:48, 7, 0:D]).then_inc(S["z_rows"], 1)

            def normed(b):
                ve.tensor_scalar(mod_a[:], modT[:, b, 0:4], 1.0, None, ALU.mult)
                ve.tensor_scalar(xh[:], x[:, 2 * b + 1, :], st[:, 2 * b + 1, 0:1], rs1[:, bass.ds(2 * b + 1, 1)],
                                 ALU.subtract, ALU.mult).then_inc(S["xh_ready"], 1)

            def split_h(b):
                ve.wait_ge(S["h_hi"], b + 1)
                ve.tensor_tensor(hl[:], hf[:], hh[:].bitcast(F32), ALU.subtract).then_inc(S["h_lo"], 1)

            def rotate_k(b):
                ve.wait_ge(S["k_sem"], b + 1)
                rotate_products(rot1[:, H:], rot2[:, H:], ps[:, A2, 0:KC].rearrange("p (g e) -> p g e", e=DH),
                                cs1, sn1, HKV).then_inc(S["k_m"], 1)

            def split_v(b):
                ve.wait_ge(S["v_hi"], b + 1)
                ve.tensor_tensor(beside(v_l), ps[:, A3, 256:512].rearrange("p (t s e) -> p t s e", t=2, s=2),
                                 beside(v_h).bitcast(F32), ALU.subtract).then_inc(S["v_lo"], 1)

            def rotate_q(b):
                ve.wait_ge(S["q_sem"], b + 1)
                rotate_products(rot1[:, 0:H], rot2[:, 0:H],
                                ps[:, A0:A0 + 2, :].rearrange("p a (h e) -> p (a h) e", e=DH),
                                cs1, sn1, H).then_inc(S["q_m"], 1)

            def split_k(b):
                ve.wait_ge(S["kT_hi"], b + 1)
                for s in range(2):
                    r = slice(64 * s, 64 * s + 64)
                    ins = ve.tensor_tensor(kT_l[r, :, s, 0:P], ps[r, A2, 0:256].rearrange("p (t k) -> p t k", t=2),
                                           kT_h[r, :, s, 0:P].bitcast(F32), ALU.subtract)
                ve.tensor_scalar(kT_h[:, :, :, P:NK], kpz_h[:, b], 1.0, None, ALU.mult)
                ve.tensor_scalar(kT_l[:, :, :, P:NK], kpz_l[:, b], 1.0, None, ALU.mult).then_inc(S["kT_lo"], 1)

            def split_q(b):
                for t in range(2):
                    ve.wait_ge(S["qT_hi"], 2 * b + t + 1)
                    ve.tensor_tensor(qT_l[:, 4 * t:4 * t + 4, :], ps[:, A0 + t, :].rearrange("p (j k) -> p j k", j=4),
                                     qT_h[:, 4 * t:4 * t + 4, :].bitcast(F32), ALU.subtract
                                     ).then_inc(S["qT_lo"], 1)

            def maxima(b, g):
                ve.wait_ge(S["s_ps"], 8 * b + g + 1)
                ve.tensor_reduce(nmax[:, 2 * g:2 * g + 2],
                                 ps[:, A0 + g % 3, 0:2 * NK].rearrange("p (s k) -> p s k", k=NK), X, ALU.max,
                                 negate=True).then_inc(S["nmax_ready"], 1)

            def inverse_sums(b, t):
                ve.wait_ge(S["exp_done"], 8 * b + 4 * t + 4)
                ve.reciprocal(rinv[:, 8 * t:8 * t + 8], psums[:, 8 * t:8 * t + 8]).then_inc(S["rinv_ready"], 1)

            def split_probs(b, t, s):
                ve.wait_ge(S["pT_hi"], 4 * b + 2 * t + s + 1)
                ve.tensor_tensor(pT_l[:, s, :], ps[:, A3, :], pT_h[:, s, :].bitcast(F32), ALU.subtract
                                 ).then_inc(S["pT_lo"], 1)

            def split_out(b, t):
                ve.wait_ge(S["oT_hi_r"], 2 * b + t + 1)
                ve.tensor_tensor(oT_l[:, 4 * t:4 * t + 4, :], ps[:, AO, :].rearrange("p (j k) -> p j k", j=4),
                                 oT_h[:, 4 * t:4 * t + 4, :].bitcast(F32), ALU.subtract
                                 ).then_inc(S["oT_lo_r"], 1)

            def add_attention(b):
                ve.wait_ge(S["gate_a_ld"], 16 * b + 16)
                ve.wait_ge(S["row_ps"], b + 1)
                ve.tensor_tensor(upd[:, 0, :], ps[:, A3, 0:D], gate_a[:], ALU.mult).then_inc(S["upd_ready"], 1)
                ve.wait_ge(S["upd_ready"], 2 * b + 1)
                ve.tensor_tensor(x[:, 2 * b, :], x[:, 2 * b, :], upd[:, 0, :], ALU.add)
                ve.wait_ge(S["y_ps"], b + 1)
                ve.tensor_tensor(upd[:, 1, :], ps[:, AO, 0:D], gate_a[:], ALU.mult).then_inc(S["upd_ready"], 1)
                ve.wait_ge(S["upd_ready"], 2 * b + 2)
                ve.tensor_tensor(x[:, 2 * b + 1, :], x[:, 2 * b + 1, :], upd[:, 1, :], ALU.add
                                 ).then_inc(S["x_mid"], 1)

            def f_norm(n, f, u):
                if u == 0:
                    ve.wait_ge(S["x_mid"], f + 1)
                    ve.tensor_scalar(mod_f[:], modT[:, f, 4:8], 1.0, None, ALU.mult)
                ve.bn_stats(bst[:], x[:, n, :]).then_inc(S["f_bn"], 1)
                carrier(S["f_bn"], n + 1)
                ve.bn_aggr(mv[:], bst[:]).then_inc(S["f_var"], 1)
                ve.wait_ge(S["f_rs"], n + 1)
                ve.wait_ge(S["f_var"], n + 1)
                ve.tensor_scalar(xh2, x[:, n, :], mv[:, 0:1], rs2[:, 0:1], ALU.subtract, ALU.mult
                                 ).then_inc(S["f_xh"], 1)

            def f_split(n, u):
                ve.wait_ge(S["f_hi"], n + 1)
                ve.tensor_tensor(fl[u][:], hf2, fh[u][:].bitcast(F32), ALU.subtract).then_inc(S["f_lo"], 1)

            def f_top4(n):
                ve.wait_ge(S["l_ps"], n + 1)
                ve.tensor_copy(lg[:], ps[:, FM, 256:384]).then_inc(S["lg_ready"], 1)
                ve.max(top8[:], ps[:, FM, 256:384]).then_inc(S["top_ready"], 1)
                ve.wait_ge(S["top_ready"], n + 1)
                ve.tensor_copy(take[:, 0:4], top8[:, 0:4]).then_inc(S["take_ready"], 1)
                ve.wait_ge(S["take_ready"], n + 1)
                ve.tensor_scalar(nm[:], top8[:, 0:1], -1.0, None, ALU.mult).then_inc(S["nm_ready"], 1)
                ve.match_replace(rest[:], take[:], lg[:], TAKEN).then_inc(S["rest_ready"], 1)

            def f_coefficients(n):
                ve.wait_ge(S["rest_ready"], n + 1)
                ve.wait_ge(S["ex_ready"], n + 1)
                ve.scalar_tensor_tensor(coef[:], rest[:], 0.999 * TAKEN, ex[:], ALU.is_le, ALU.mult,
                                        accum_out=s4[:]).then_inc(S["coef_ready"], 1)
                ve.wait_ge(S["coef_ready"], n + 1)
                ve.scalar_tensor_tensor(den[:, 0:1], zsum[:], EPS, s4[:], ALU.mult, ALU.add
                                        ).then_inc(S["den_ready"], 1)
                ve.wait_ge(S["den_ready"], n + 1)
                ve.reciprocal(den[:, 1:2], den[:, 0:1]).then_inc(S["rcp_ready"], 1)
                ve.wait_ge(S["rcp_ready"], n + 1)

            def f_weights(n, u):
                ve.wait_ge(S["w_ps"], n + 1)
                ve.tensor_scalar(w8[u][:], ps[:, FM, 0:NB], den[:, 1:2], 0.5, ALU.mult, ALU.mult
                                 ).then_inc(S["w8_ready"], 1)

            def f_chunk(n, u, k):
                r = (k + u) % 2
                ve.wait_ge(S["th_ready"], NCH * n + k + 1)
                bank = ps[:, FR + r, :]
                ve.scalar_tensor_tensor(act_g[r], th[r], 1.0, bank[:, 0:256], ALU.add, ALU.mult
                                        ).then_inc(S["ag_ready"], 1)
                ve.wait_ge(S["ag_ready"], NCH * n + k + 1)
                if k == 0:
                    ve.scalar_tensor_tensor(shared[u][:], act_g[r], 0.5, bank[:, 256:512], ALU.mult, ALU.mult
                                            ).then_inc(S["chunk_done"], 1)
                    return
                if k == 1:
                    ve.wait_ge(S["w8_ready"], n + 1)
                if not (isinstance(n, int) and n == 0):
                    ve.wait_ge(S["mix_sum"], 3 * n - 3 + max(1, k - 1))
                for i in range(2):
                    ins = ve.scalar_tensor_tensor(prod[:, k - 1, P * i:P * i + P], act_g[r][:, P * i:P * i + P],
                                                  w8[u][:, 2 * (k - 1) + i:2 * (k - 1) + i + 1],
                                                  bank[:, 256 + P * i:256 + P * i + P], ALU.mult, ALU.mult)
                ins.then_inc(S["chunk_done"], 1)

            def f_inner(n):
                ve.wait_ge(S["mT_hi_r"], n + 1)
                ve.tensor_tensor(mT_l[:], ps[:, FM, 0:384].rearrange("p (k n) -> p k n", k=3),
                                 mT_h[:].bitcast(F32), ALU.subtract).then_inc(S["mT_lo_r"], 1)

            def f_add(n, f, u):
                ve.wait_ge(S["d_ps"], n + 1)
                if u == 0:
                    ve.wait_ge(S["gate_f_ld"], 16 * f + 16)
                ve.tensor_tensor(updf[:], ps[:, FM, 0:D], gate_f[:], ALU.mult).then_inc(S["updf_ready"], 1)
                ve.wait_ge(S["updf_ready"], n + 1)
                ve.tensor_tensor(x[:, n, :], x[:, n, :], updf[:], ALU.add).then_inc(S["x_done"], 1)

            def body(b, back, front):
                m0, m1, m2 = 2 * b - 3, 2 * b - 2, 2 * b - 1
                first = isinstance(b, int) and b == 0
                if front:
                    normed(b + 1)
                if back:
                    maxima(b, 0)
                    maxima(b, 1)
                if real(m0):
                    f_chunk(m0, 1, 0)
                if back:
                    maxima(b, 2)
                    maxima(b, 3)
                if first:
                    z_scores(0)
                if real(m1):
                    f_norm(m1, b - 1, 0)
                if real(m0):
                    f_chunk(m0, 1, 1)
                if front:
                    split_h(b + 1)
                if back:
                    inverse_sums(b, 0)
                    maxima(b, 4)
                    maxima(b, 5)
                if real(m1):
                    f_split(m1, 0)
                if back:
                    maxima(b, 6)
                if real(m1 - 2):
                    f_inner(m1 - 2)
                if real(m0):
                    f_chunk(m0, 1, 2)
                if back:
                    maxima(b, 7)
                if first:
                    z_scores(1)
                    z_max()
                if real(m1):
                    f_top4(m1)
                if back:
                    split_probs(b, 0, 0)
                if first:
                    z_probs()
                    z_weigh(0)
                if real(m1):
                    f_coefficients(m1)
                if real(m1 - 2):
                    f_add(m1 - 2, b - 2, 0)
                if back:
                    inverse_sums(b, 1)
                if real(m0):
                    f_chunk(m0, 1, 3)
                if back:
                    split_probs(b, 0, 1)
                if first:
                    z_weigh(1)
                    z_row()
                if front:
                    rotate_k(b + 1)
                if real(m0):
                    f_chunk(m0, 1, 4)
                if front:
                    rotate_q(b + 1)
                if real(m1):
                    f_weights(m1, 0)
                if back:
                    split_out(b, 0)
                    split_probs(b, 1, 0)
                if real(m2):
                    f_norm(m2, b - 1, 1)
                if front:
                    split_k(b + 1)
                if back:
                    split_probs(b, 1, 1)
                if real(m1):
                    f_chunk(m1, 0, 0)
                    f_chunk(m1, 0, 1)
                if real(m2):
                    f_split(m2, 1)
                if real(m0):
                    f_inner(m0)
                if front:
                    split_q(b + 1)
                if back:
                    split_out(b, 1)
                if first:
                    z_split()
                if front:
                    split_v(b + 1)
                if first:
                    z_rows()
                if real(m2):
                    f_top4(m2)
                if real(m1):
                    f_chunk(m1, 0, 2)
                if real(m2):
                    f_coefficients(m2)
                if real(m0):
                    f_add(m0, b - 2, 1)
                if real(m1):
                    f_chunk(m1, 0, 3)
                if back:
                    add_attention(b)
                if real(m2):
                    f_weights(m2, 1)
                if real(m1):
                    f_chunk(m1, 0, 4)

            normed(0)
            for h in range(2):
                ve.wait_ge(S["ht_hi"], h + 1)
                ve.tensor_tensor(ht_l[h], ht[:, h].rearrange("p c b i -> p (c b i)"), ht_h[h].bitcast(F32),
                                 ALU.subtract).then_inc(S["ht_lo"], 1)
            ve.wait_ge(S["z_v_ps"], 1)
            ve.tensor_copy(vrow[0], ps[0:B, 0, 0:D])
            ve.tensor_copy(vrow[1], ps[0:B, 0, D:2 * D])
            ve.tensor_copy(vrow[2], ps[0:B, 1, 0:D]).then_inc(S["z_v_copied"], 1)
            ve.wait_ge(S["z_q_ps"], 1)
            ve.wait_ge(S["piece_lo"], len(SPLIT))
            q_ps = ps[0:B, 2:4, :].rearrange("p a (h e) -> p (a h) e", e=DH)
            ve.tensor_copy(q127[:, :, 0:32], q_ps[:, :, 0:32])
            link(rotate_products(dots[:, :, 0:32], dots[:, :, 32:64], q_ps, csl, snl, H))
            ve.wait_ge(S["a_kps"], 1)
            ve.tensor_tensor(diag.rearrange("p (c i) -> p c i", i=16),
                             ps[:, 6:8, :].rearrange("p a (c i) -> p (a c) i", i=16),
                             over_heads(tab[:, C_DI:C_DI + 16], 64), ALU.mult).then_inc(S["a_diag"], 1)
            ve.memset(spread[:, :, 0:32], 0.0)
            ve.wait_ge(S["a_diag"], 1)
            d_cos, d_sin = [diag[:, 512 * a:512 * a + 512].rearrange("p (x e) -> p x e", e=32) for a in range(2)]
            ve.tensor_tensor(spread[:, :, 32:48], d_cos[:, :, 0:16], d_sin[:, :, 16:32], ALU.subtract
                             ).then_inc(S["a_spread"], 1)
            ve.tensor_tensor(spread[:, :, 48:64], d_cos[:, :, 16:32], d_sin[:, :, 0:16], ALU.add
                             ).then_inc(S["a_spread"], 1)
            split_h(0)
            ve.wait_ge(S["a_kp_ps"], 1)
            for s in range(2):
                ins = ve.tensor_copy(kpool[64 * s:64 * s + 32],
                                     ps[64 * s:64 * s + 32, 4, 64:128].rearrange("p (t k b) -> p b t k", t=2, k=NP))
                for u in range(2):
                    r = slice(64 * s + 32, 64 * s + 64)
                    ins = ve.tensor_copy(kpool[r, 8 * u:8 * u + 8],
                                         ps[r, 4, 32 * u:32 * u + 32].rearrange("p (k t b) -> p b t k", k=NP, t=2))
            ins.then_inc(S["a_kp"], 1)
            ve.memset(kpz_h[:].bitcast(F32), 0.0)
            ve.memset(kpz_l[:].bitcast(F32), 0.0).then_inc(S["kpz"], 1)
            ve.wait_ge(S["kpz"], 1)
            ve.wait_ge(S["a_kp"], 1)
            for s in range(2):
                r = slice(64 * s, 64 * s + 64)
                ins = ve.tensor_copy(kpz_h[r, :, :, s, :], kpool[r])
            ins.then_inc(S["kpz"], 1)
            ve.wait_ge(S["kpz"], 2)
            for s in range(2):
                r = slice(64 * s, 64 * s + 64)
                ve.tensor_tensor(kpz_l[r, :, :, s, :], kpool[r], kpz_h[r, :, :, s, :].bitcast(F32), ALU.subtract)
            rotate_k(0)
            rotate_q(0)
            ve.tensor_tensor(q127[:, :, 32:64], dots[:, :, 0:32], dots[:, :, 32:64], ALU.add)
            ve.wait_ge(S["z_kp_ps"], 1)
            link(ve.tensor_copy(kprow, ps[0:B, 4, :].rearrange("p (k n) -> p k n", k=NP)))
            ve.wait_ge(S["z_vT_ps"], 1)
            ve.tensor_copy(vTf, ps[:, 5, 0:64].rearrange("p (t n) -> p t n", t=2)).then_inc(S["z_vT"], 1)
            ve.wait_ge(S["z_vT"], 1)
            ve.tensor_copy(vT_h, vTf).then_inc(S["z_vT_hi"], 1)
            ve.wait_ge(S["z_vT_hi"], 1)
            ve.tensor_tensor(vT_l, vTf, vT_h.bitcast(F32), ALU.subtract
                             ).then_inc(S["z_vT_lo"], 1)
            split_k(0)
            split_q(0)
            split_v(0)
            body(0, True, True)
            ve.wait_ge(S["z_vw_st"], 64)
            ve.wait_ge(S["z_rows_st"], 16)
            body(1, True, True)
            with ve.Fori(2, B - 1) as b:
                body(b, True, True)
            body(B - 1, True, False)
            body(B, False, False)
            body(B + 1, False, False)


JH_ = H // HKV
Z_MAX = 8
Z_ROW_C = 14


_INS = ['L0_attn_x', 'L0_attn_Wq_sem', 'L0_attn_Wk_sem', 'L0_attn_Wq_geo', 'L0_attn_Wk_geo', 'L0_attn_Wv',
        'L0_attn_Wo', 'L0_attn_logit_scale', 'L0_ffn_w_router', 'L0_ffn_w_gate', 'L0_ffn_w_up', 'L0_ffn_w_down',
        'L0_ffn_amplitudes', 'L0_ffn_expert_scale', 'L0_ffn_shared_w_gate', 'L0_ffn_shared_w_up',
        'L0_ffn_shared_w_down', 'L0_c', 'L0_wmod']


def constants():
    import numpy as np

    tab = np.zeros((P, NTAB), np.float32)
    tab[:, C_ID:C_ID + P] = np.eye(P)
    freq = (1.0 / np.float32(10000.0) ** (np.arange(0, 32, 2, dtype=np.float32) / np.float32(32))).astype(np.float32)

    def rotary(pos, c, s):
        ang = (pos.astype(np.float32)[:, None] * freq).astype(np.float32)
        tab[:, c:c + 32] = np.concatenate([np.cos(ang), np.cos(ang)], 1)
        tab[:, s:s + 32] = np.concatenate([-np.sin(ang), np.sin(ang)], 1)

    rotary(np.arange(P, 2 * P), C_COS1, C_SIN1)
    rotary(np.full(P, P - 1), C_COSL, C_SINL)
    ang = (np.arange(P, dtype=np.float32)[:, None] * freq).astype(np.float32)
    rot = np.zeros((P, 2, NP, 16), np.float32)
    for k in range(NP):
        for a, f in enumerate((np.cos, np.sin)):
            rot[64 * k:64 * k + 64, a, k] = f(ang[64 * k:64 * k + 64]) / 64
    tab[:, C_ROT:C_ROT + 64] = rot.reshape(P, 64)
    tab[:, C_WS:C_WS + 64] = rot.reshape(P, 64).astype(np.float64).sum(0)
    tab[np.arange(P), C_DI + np.arange(P) % 16] = 1.0
    tab[np.arange(P), C_DB + np.arange(P) // 16] = 1.0
    tab[0:64, C_POOL0] = 1.0 / 64
    tab[64:P, C_POOL0 + 1] = 1.0 / 64
    tab[P - 1, C_POOL0 + 2] = 1.0
    tab[:, C_POOL0 + 3] = 1.0 / (64 * NK)
    tab[:, C_POOL1 + 3] = 1.0 / NK
    tab[NP * H, C_SEL:C_SEL + 63] = 1.0
    tab[NP * H + 1, C_SEL + 63:C_SEL + P - 1] = 1.0
    tab[NP * H + 2, C_SEL + P - 1] = 1.0
    mask = np.zeros((P, 2, NK), np.float32)
    mask[:, :, 0:P] = np.where(np.arange(P)[None, :] <= np.arange(P)[:, None], 0.0, HIDE)[:, None, :]
    return tab, mask.reshape(P, 2 * NK)


def kernel(**inputs):
    import numpy as np
    import concourse.bacc as bacc
    from concourse.bass_utils import run_bass_kernel_spmd

    nc = bacc.Bacc("TRN2", target_bir_lowering=False, num_devices=1)
    tab, mask = constants()
    arrays, args = {}, []
    named = [(n, np.ascontiguousarray(inputs[n])) for n in _INS] + [("table", tab), ("mask", mask)]
    for name, a in named:
        arrays[f"in_{name}_dram"] = a
        args.append(nc.dram_tensor(f"in_{name}_dram", a.shape, mybir.dt.from_np(a.dtype), kind="ExternalInput").ap())
    args.append(nc.dram_tensor("out_0_dram", (B, T, D), F32, kind="ExternalOutput").ap())
    build(nc, *args)
    r = run_bass_kernel_spmd(nc, [arrays], core_ids=[0])
    return r.results[0]["out_0_dram"]
```
